# Optimizing a Trainium2 kernel written in Bass

```python
import numpy as np
import jax
import jax.numpy as jnp

def _softmax(x, axis=-1):
    return jax.nn.softmax(x, axis=axis)

def _gelu(x):
    return jax.nn.gelu(x, approximate=True)

def _silu(x):
    return jax.nn.silu(x)

def _sigmoid(x):
    return jax.nn.sigmoid(x)

def _layernorm(x, axis=-1, eps=1e-05):
    m = jnp.mean(x, axis=axis, keepdims=True)
    v = jnp.var(x, axis=axis, keepdims=True)
    return (x - m) / jnp.sqrt(v + eps)

def _scatter_add(tgt, idx, src, axis=0):
    return tgt.at[idx].add(src)

def _segment_sum(src, seg, n):
    return jax.ops.segment_sum(src, seg, n)
kernel_name = 'mk_gps_d2_gnn_r32_6b8904'

def setup_inputs(seed: int=0):
    np.random.seed(seed)
    _w = jnp.asarray

    def _rec_inputs():
        import jax
        import jax.numpy as jnp
        _gk = jax.random.key(seed)
        x = -0.0002117 + 1 * jax.random.normal(jax.random.fold_in(_gk, 1), (3125, 256), jnp.float32)
        _s = jax.random.randint(jax.random.fold_in(_gk, 2), (25000,), 0, 3125, jnp.int32)
        _d = jax.random.randint(jax.random.fold_in(_gk, 3), (25000,), 0, 3125, jnp.int32)
        _loop = jnp.arange(3125, dtype=jnp.int32)
        src = jnp.concatenate([_s, _d, _loop])
        dst = jnp.concatenate([_d, _s, _loop])
        _o = jnp.argsort(dst, stable=True)
        src = src[_o]
        dst = dst[_o]
        edge_weight = jax.random.uniform(jax.random.fold_in(_gk, 13), (53125,), jnp.float32, 0.0, 0.03125)
        return (x, src, dst, edge_weight)
    x, src, dst, edge_weight = _rec_inputs()

    def _L0_gnn_setup():
        import jax, jax.numpy as jnp
        import numpy as np
        N = 3125
        E = 100000
        D_IN = 256
        D_OUT = 256
        K = 3

        def _spmm(edge_weight, edge_row, edge_col, support):
            msgs = edge_weight[:, None] * support[edge_col]
            return jax.ops.segment_sum(msgs, edge_row, num_segments=N)
        key = jax.random.key(seed)
        k1, k2, k3, k4, k5 = jax.random.split(key, 5)
        x = jax.random.normal(k1, (N, D_IN), dtype=jnp.float32)
        lim = float(np.sqrt(6.0 / (D_IN + D_OUT)))
        weight = jax.random.uniform(k2, (D_IN, D_OUT), dtype=jnp.float32, minval=-lim, maxval=lim)
        bias = jnp.zeros((D_OUT,), dtype=jnp.float32)
        edge_weight = jax.random.uniform(k3, (E,), dtype=jnp.float32) / 32.0
        edge_row = jax.random.randint(k4, (E,), 0, N, dtype=jnp.int32)
        edge_col = jax.random.randint(k5, (E,), 0, N, dtype=jnp.int32)
        return {'x': x, 'weight': weight, 'bias': bias, 'edge_weight': edge_weight, 'edge_row': edge_row, 'edge_col': edge_col}
    _L0_gnn_all = _L0_gnn_setup()
    _L0_gnn_in = {k: v for k, v in _L0_gnn_all.items() if k in ('weight', 'bias')}
    del _L0_gnn_all

    def _L0_mix_setup():
        import jax, jax.numpy as jnp
        import numpy as np
        D_MODEL = 256
        NHEAD = 8
        D_HEAD = D_MODEL // NHEAD
        DIM_FF = 1024
        B, L = (4, 512)
        LN_EPS = 1e-05

        def _layernorm(x, g, b):
            mu = jnp.mean(x, axis=-1, keepdims=True)
            var = jnp.mean((x - mu) ** 2, axis=-1, keepdims=True)
            return (x - mu) * jax.lax.rsqrt(var + LN_EPS) * g + b

        def _phi(x):
            return jnp.where(x > 0, x + 1.0, jnp.exp(x))
        key = jax.random.key(seed)
        ks = jax.random.split(key, 16)
        s_in = 1.0 / np.sqrt(D_MODEL)
        s_ff = 1.0 / np.sqrt(DIM_FF)
        inp = {'x': jax.random.normal(ks[0], (B, L, D_MODEL), dtype=jnp.float32), 'Wq': jax.random.normal(ks[1], (D_MODEL, D_MODEL), dtype=jnp.float32) * s_in, 'bq': jnp.zeros((D_MODEL,), jnp.float32), 'Wk': jax.random.normal(ks[2], (D_MODEL, D_MODEL), dtype=jnp.float32) * s_in, 'bk': jnp.zeros((D_MODEL,), jnp.float32), 'Wv': jax.random.normal(ks[3], (D_MODEL, D_MODEL), dtype=jnp.float32) * s_in, 'bv': jnp.zeros((D_MODEL,), jnp.float32), 'Wo': jax.random.normal(ks[4], (D_MODEL, D_MODEL), dtype=jnp.float32) * s_in, 'bo': jnp.zeros((D_MODEL,), jnp.float32), 'W1': jax.random.normal(ks[5], (D_MODEL, DIM_FF), dtype=jnp.float32) * s_in, 'b1': jnp.zeros((DIM_FF,), jnp.float32), 'W2': jax.random.normal(ks[6], (DIM_FF, D_MODEL), dtype=jnp.float32) * s_ff, 'b2': jnp.zeros((D_MODEL,), jnp.float32), 'ln1_g': jnp.ones((D_MODEL,), jnp.float32), 'ln1_b': jnp.zeros((D_MODEL,), jnp.float32), 'ln2_g': jnp.ones((D_MODEL,), jnp.float32), 'ln2_b': jnp.zeros((D_MODEL,), jnp.float32)}
        return inp
    _L0_mix_all = _L0_mix_setup()
    _L0_mix_in = {k: v for k, v in _L0_mix_all.items() if k in ('Wq', 'bq', 'Wk', 'bk', 'Wv', 'bv', 'Wo', 'bo', 'W1', 'b1', 'W2', 'b2', 'ln1_g', 'ln1_b', 'ln2_g', 'ln2_b')}
    del _L0_mix_all

    def _L0_ffn_setup():
        import jax, jax.numpy as jnp
        import numpy as np
        B, S, H, F, E, K = (8, 128, 256, 512, 16, 2)
        EPS = 1e-05
        key = jax.random.key(seed)
        ks = jax.random.split(key, 9)
        sc = 0.02
        return {'x': jax.random.normal(ks[0], (B, S, H), dtype=jnp.float32), 'gate_w': jax.random.normal(ks[1], (H, E), dtype=jnp.float32) * sc, 'gate_b': jnp.zeros((E,), dtype=jnp.float32), 'w1': jax.random.normal(ks[2], (E, H, F), dtype=jnp.float32) * sc, 'b1': jnp.zeros((E, F), dtype=jnp.float32), 'w2': jax.random.normal(ks[3], (E, F, H), dtype=jnp.float32) * sc, 'b2': jnp.zeros((E, H), dtype=jnp.float32), 'gamma': jnp.ones((H,), dtype=jnp.float32), 'beta': jnp.zeros((H,), dtype=jnp.float32)}
    _L0_ffn_all = _L0_ffn_setup()
    _L0_ffn_in = {k: v for k, v in _L0_ffn_all.items() if k in ('gate_w', 'gate_b', 'w1', 'b1', 'w2', 'b2', 'gamma', 'beta')}
    del _L0_ffn_all

    def _L1_gnn_setup():
        import jax, jax.numpy as jnp
        import numpy as np
        N = 50000
        E = 50000
        D = 256
        H = 256
        EPS = 1e-05

        def _gnn_layer(x, row, col, W, b, g, beta):
            n = x.shape[0]
            neigh = x[col]
            agg = jax.ops.segment_sum(neigh, row, num_segments=n)
            deg = jax.ops.segment_sum(jnp.ones((row.shape[0],), x.dtype), row, num_segments=n)
            deg = jnp.maximum(deg, 1.0)[:, None]
            h = (x + agg / deg) @ W.T + b
            mu = jnp.mean(h, axis=-1, keepdims=True)
            var = jnp.mean(jnp.square(h - mu), axis=-1, keepdims=True)
            hn = (h - mu) * jax.lax.rsqrt(var + EPS) * g + beta
            return jax.nn.silu(hn)
        key = jax.random.key(seed)
        ks = jax.random.split(key, 12)
        x = jax.random.normal(ks[0], (N, D), dtype=jnp.float32)
        edge_index = jax.random.randint(ks[1], (2, E), 0, N, dtype=jnp.int32)
        s0 = 1.0 / np.sqrt(D)
        s1 = 1.0 / np.sqrt(H)
        W0 = jax.random.uniform(ks[2], (H, D), jnp.float32, -s0, s0)
        b0 = jax.random.uniform(ks[3], (H,), jnp.float32, -s0, s0)
        g0 = jnp.ones((H,), jnp.float32)
        beta0 = jnp.zeros((H,), jnp.float32)
        W1 = jax.random.uniform(ks[4], (H, H), jnp.float32, -s1, s1)
        b1 = jax.random.uniform(ks[5], (H,), jnp.float32, -s1, s1)
        g1 = jnp.ones((H,), jnp.float32)
        beta1 = jnp.zeros((H,), jnp.float32)
        return {'x': x, 'edge_index': edge_index, 'W0': W0, 'b0': b0, 'g0': g0, 'beta0': beta0, 'W1': W1, 'b1': b1, 'g1': g1, 'beta1': beta1}
    _L1_gnn_all = _L1_gnn_setup()
    _L1_gnn_in = {k: v for k, v in _L1_gnn_all.items() if k in ('W0', 'b0', 'g0', 'beta0', 'W1', 'b1', 'g1', 'beta1')}
    del _L1_gnn_all

    def _L1_mix_setup():
        import jax, jax.numpy as jnp
        import numpy as np
        N, F, C, H = (32, 128, 256, 8)
        D = C // H
        EPS_ATTN = 1e-06
        EPS_LN = 1e-05

        def layer_norm(x, g, b):
            mu = jnp.mean(x, axis=-1, keepdims=True)
            var = jnp.var(x, axis=-1, keepdims=True)
            return (x - mu) * jax.lax.rsqrt(var + EPS_LN) * g + b
        key = jax.random.key(seed)
        ks = jax.random.split(key, 8)
        s = 1.0 / np.sqrt(C)
        return {'x': jax.random.normal(ks[0], (N, F, C), jnp.float32), 'Wqkv': jax.random.uniform(ks[1], (3 * C, C), jnp.float32, -s, s), 'ln1_g': jnp.ones((C,), jnp.float32), 'ln1_b': jnp.zeros((C,), jnp.float32), 'W1': jax.random.uniform(ks[2], (C, C), jnp.float32, -s, s), 'b1': jax.random.uniform(ks[3], (C,), jnp.float32, -s, s), 'W2': jax.random.uniform(ks[4], (C, C), jnp.float32, -s, s), 'b2': jax.random.uniform(ks[5], (C,), jnp.float32, -s, s), 'ln2_g': jnp.ones((C,), jnp.float32), 'ln2_b': jnp.zeros((C,), jnp.float32)}
    _L1_mix_all = _L1_mix_setup()
    _L1_mix_in = {k: v for k, v in _L1_mix_all.items() if k in ('Wqkv', 'ln1_g', 'ln1_b', 'W1', 'b1', 'W2', 'b2', 'ln2_g', 'ln2_b')}
    del _L1_mix_all

    def _L1_ffn_setup():
        import math
        import jax, jax.numpy as jnp
        import numpy as np
        CAPACITY_FACTOR = 1.25
        TOP_K = 2
        LN_EPS = 1e-05

        def _layer_norm(x, gamma, beta):
            mu = jnp.mean(x, axis=-1, keepdims=True)
            var = jnp.var(x, axis=-1, keepdims=True)
            return (x - mu) * jax.lax.rsqrt(var + LN_EPS) * gamma + beta
        key = jax.random.key(seed)
        ks = jax.random.split(key, 4)
        B, S, D, F, E = (8, 128, 256, 512, 8)
        x = jax.random.normal(ks[0], (B, S, D), dtype=jnp.float32)
        Wr = jax.random.normal(ks[1], (D, E), dtype=jnp.float32) / np.sqrt(D)
        br = jnp.zeros((E,), jnp.float32)
        W1 = jax.random.normal(ks[2], (E, D, F), dtype=jnp.float32) / np.sqrt(D)
        b1 = jnp.zeros((E, F), jnp.float32)
        W2 = jax.random.normal(ks[3], (E, F, D), dtype=jnp.float32) / np.sqrt(F)
        b2 = jnp.zeros((E, D), jnp.float32)
        gamma = jnp.ones((D,), jnp.float32)
        beta = jnp.zeros((D,), jnp.float32)
        return {'x': x, 'Wr': Wr, 'br': br, 'W1': W1, 'b1': b1, 'W2': W2, 'b2': b2, 'gamma': gamma, 'beta': beta}
    _L1_ffn_all = _L1_ffn_setup()
    _L1_ffn_in = {k: v for k, v in _L1_ffn_all.items() if k in ('Wr', 'br', 'W1', 'b1', 'W2', 'b2', 'gamma', 'beta')}
    del _L1_ffn_all
    return {'x': x, 'src': src, 'dst': dst, 'edge_weight': edge_weight, 'L0_gnn_weight': _L0_gnn_in['weight'], 'L0_gnn_bias': _L0_gnn_in['bias'], 'L0_mix_Wq': _L0_mix_in['Wq'], 'L0_mix_bq': _L0_mix_in['bq'], 'L0_mix_Wk': _L0_mix_in['Wk'], 'L0_mix_bk': _L0_mix_in['bk'], 'L0_mix_Wv': _L0_mix_in['Wv'], 'L0_mix_bv': _L0_mix_in['bv'], 'L0_mix_Wo': _L0_mix_in['Wo'], 'L0_mix_bo': _L0_mix_in['bo'], 'L0_mix_W1': _L0_mix_in['W1'], 'L0_mix_b1': _L0_mix_in['b1'], 'L0_mix_W2': _L0_mix_in['W2'], 'L0_mix_b2': _L0_mix_in['b2'], 'L0_mix_ln1_g': _L0_mix_in['ln1_g'], 'L0_mix_ln1_b': _L0_mix_in['ln1_b'], 'L0_mix_ln2_g': _L0_mix_in['ln2_g'], 'L0_mix_ln2_b': _L0_mix_in['ln2_b'], 'L0_ffn_gate_w': _L0_ffn_in['gate_w'], 'L0_ffn_gate_b': _L0_ffn_in['gate_b'], 'L0_ffn_w1': _L0_ffn_in['w1'], 'L0_ffn_b1': _L0_ffn_in['b1'], 'L0_ffn_w2': _L0_ffn_in['w2'], 'L0_ffn_b2': _L0_ffn_in['b2'], 'L0_ffn_gamma': _L0_ffn_in['gamma'], 'L0_ffn_beta': _L0_ffn_in['beta'], 'L1_gnn_W0': _L1_gnn_in['W0'], 'L1_gnn_b0': _L1_gnn_in['b0'], 'L1_gnn_g0': _L1_gnn_in['g0'], 'L1_gnn_beta0': _L1_gnn_in['beta0'], 'L1_gnn_W1': _L1_gnn_in['W1'], 'L1_gnn_b1': _L1_gnn_in['b1'], 'L1_gnn_g1': _L1_gnn_in['g1'], 'L1_gnn_beta1': _L1_gnn_in['beta1'], 'L1_mix_Wqkv': _L1_mix_in['Wqkv'], 'L1_mix_ln1_g': _L1_mix_in['ln1_g'], 'L1_mix_ln1_b': _L1_mix_in['ln1_b'], 'L1_mix_W1': _L1_mix_in['W1'], 'L1_mix_b1': _L1_mix_in['b1'], 'L1_mix_W2': _L1_mix_in['W2'], 'L1_mix_b2': _L1_mix_in['b2'], 'L1_mix_ln2_g': _L1_mix_in['ln2_g'], 'L1_mix_ln2_b': _L1_mix_in['ln2_b'], 'L1_ffn_Wr': _L1_ffn_in['Wr'], 'L1_ffn_br': _L1_ffn_in['br'], 'L1_ffn_W1': _L1_ffn_in['W1'], 'L1_ffn_b1': _L1_ffn_in['b1'], 'L1_ffn_W2': _L1_ffn_in['W2'], 'L1_ffn_b2': _L1_ffn_in['b2'], 'L1_ffn_gamma': _L1_ffn_in['gamma'], 'L1_ffn_beta': _L1_ffn_in['beta']}

def reference(x, src, dst, edge_weight, L0_gnn_weight, L0_gnn_bias, L0_mix_Wq, L0_mix_bq, L0_mix_Wk, L0_mix_bk, L0_mix_Wv, L0_mix_bv, L0_mix_Wo, L0_mix_bo, L0_mix_W1, L0_mix_b1, L0_mix_W2, L0_mix_b2, L0_mix_ln1_g, L0_mix_ln1_b, L0_mix_ln2_g, L0_mix_ln2_b, L0_ffn_gate_w, L0_ffn_gate_b, L0_ffn_w1, L0_ffn_b1, L0_ffn_w2, L0_ffn_b2, L0_ffn_gamma, L0_ffn_beta, L1_gnn_W0, L1_gnn_b0, L1_gnn_g0, L1_gnn_beta0, L1_gnn_W1, L1_gnn_b1, L1_gnn_g1, L1_gnn_beta1, L1_mix_Wqkv, L1_mix_ln1_g, L1_mix_ln1_b, L1_mix_W1, L1_mix_b1, L1_mix_W2, L1_mix_b2, L1_mix_ln2_g, L1_mix_ln2_b, L1_ffn_Wr, L1_ffn_br, L1_ffn_W1, L1_ffn_b1, L1_ffn_W2, L1_ffn_b2, L1_ffn_gamma, L1_ffn_beta):
    import jax
    import jax.numpy as jnp

    def _L0_gnn_ref(x, weight, bias, edge_weight, edge_row, edge_col):
        import jax, jax.numpy as jnp
        import numpy as np
        N = 3125
        E = 100000
        D_IN = 256
        D_OUT = 256
        K = 3

        def _spmm(edge_weight, edge_row, edge_col, support):
            msgs = edge_weight[:, None] * support[edge_col]
            return jax.ops.segment_sum(msgs, edge_row, num_segments=N)
        support = x @ weight
        output = support
        for _ in range(K):
            support = _spmm(edge_weight, edge_row, edge_col, support)
            output = output + support
        return output + bias

    def _L0_mix_ref(x, Wq, bq, Wk, bk, Wv, bv, Wo, bo, W1, b1, W2, b2, ln1_g, ln1_b, ln2_g, ln2_b):
        import jax, jax.numpy as jnp
        import numpy as np
        D_MODEL = 256
        NHEAD = 8
        D_HEAD = D_MODEL // NHEAD
        DIM_FF = 1024
        B, L = (4, 512)
        LN_EPS = 1e-05

        def _layernorm(x, g, b):
            mu = jnp.mean(x, axis=-1, keepdims=True)
            var = jnp.mean((x - mu) ** 2, axis=-1, keepdims=True)
            return (x - mu) * jax.lax.rsqrt(var + LN_EPS) * g + b

        def _phi(x):
            return jnp.where(x > 0, x + 1.0, jnp.exp(x))
        Bq, Lq, _ = x.shape
        q = (x @ Wq + bq).reshape(Bq, Lq, NHEAD, D_HEAD)
        k = (x @ Wk + bk).reshape(Bq, Lq, NHEAD, D_HEAD)
        v = (x @ Wv + bv).reshape(Bq, Lq, NHEAD, D_HEAD)
        q_phi = _phi(q)
        k_phi = _phi(k)
        kv = jnp.einsum('blhd,blhe->bhde', k_phi, v)
        k_sum = k_phi.sum(axis=1)
        z = 1.0 / (jnp.einsum('blhd,bhd->blh', q_phi, k_sum) + 1e-06)
        out = jnp.einsum('blhd,bhde,blh->blhe', q_phi, kv, z)
        out = out.reshape(Bq, Lq, D_MODEL) @ Wo + bo
        x = _layernorm(x + out, ln1_g, ln1_b)
        ff = jax.nn.relu(x @ W1 + b1) @ W2 + b2
        x = _layernorm(x + ff, ln2_g, ln2_b)
        return x

    def _L0_ffn_ref(x, gate_w, gate_b, w1, b1, w2, b2, gamma, beta):
        import jax, jax.numpy as jnp
        import numpy as np
        B, S, H, F, E, K = (8, 128, 256, 512, 16, 2)
        EPS = 1e-05
        gate_logits = x @ gate_w + gate_b
        topk_vals, topk_idx = jax.lax.top_k(gate_logits, K)
        topk_w = jax.nn.softmax(topk_vals, axis=-1)
        h = jax.nn.relu(jnp.einsum('bsh,ehf->bsef', x, w1) + b1)
        expert_out = jnp.einsum('bsef,efh->bseh', h, w2) + b2
        sel = jnp.take_along_axis(expert_out, topk_idx[:, :, :, None], axis=2)
        moe = jnp.sum(topk_w[..., None] * sel, axis=2)
        y = x + moe
        mu = jnp.mean(y, axis=-1, keepdims=True)
        var = jnp.var(y, axis=-1, keepdims=True)
        return (y - mu) / jnp.sqrt(var + EPS) * gamma + beta

    def _L1_gnn_ref(x, edge_index, W0, b0, g0, beta0, W1, b1, g1, beta1):
        import jax, jax.numpy as jnp
        import numpy as np
        N = 50000
        E = 50000
        D = 256
        H = 256
        EPS = 1e-05

        def _gnn_layer(x, row, col, W, b, g, beta):
            n = x.shape[0]
            neigh = x[col]
            agg = jax.ops.segment_sum(neigh, row, num_segments=n)
            deg = jax.ops.segment_sum(jnp.ones((row.shape[0],), x.dtype), row, num_segments=n)
            deg = jnp.maximum(deg, 1.0)[:, None]
            h = (x + agg / deg) @ W.T + b
            mu = jnp.mean(h, axis=-1, keepdims=True)
            var = jnp.mean(jnp.square(h - mu), axis=-1, keepdims=True)
            hn = (h - mu) * jax.lax.rsqrt(var + EPS) * g + beta
            return jax.nn.silu(hn)
        row, col = (edge_index[0], edge_index[1])
        x = _gnn_layer(x, row, col, W0, b0, g0, beta0)
        x = _gnn_layer(x, row, col, W1, b1, g1, beta1)
        return x

    def _L1_mix_ref(x, Wqkv, ln1_g, ln1_b, W1, b1, W2, b2, ln2_g, ln2_b):
        import jax, jax.numpy as jnp
        import numpy as np
        N, F, C, H = (32, 128, 256, 8)
        D = C // H
        EPS_ATTN = 1e-06
        EPS_LN = 1e-05

        def layer_norm(x, g, b):
            mu = jnp.mean(x, axis=-1, keepdims=True)
            var = jnp.var(x, axis=-1, keepdims=True)
            return (x - mu) * jax.lax.rsqrt(var + EPS_LN) * g + b
        n, f, c = x.shape
        qkv = jnp.einsum('nfc,oc->nfo', x, Wqkv)
        q, k, v = jnp.split(qkv, 3, axis=-1)
        q = q.reshape(n, f, H, D)
        k = k.reshape(n, f, H, D)
        v = v.reshape(n, f, H, D)
        q = jax.nn.elu(q) + 1.0
        k = jax.nn.elu(k) + 1.0
        kv = jnp.einsum('nshd,nshm->nhmd', k, v)
        ksum = jnp.sum(k, axis=1)
        z = 1.0 / (jnp.einsum('nlhd,nhd->nlh', q, ksum) + EPS_ATTN)
        t = jnp.einsum('nlhd,nhmd,nlh->nlhm', q, kv, z)
        t = t.reshape(n, f, c)
        x1 = layer_norm(t + x, ln1_g, ln1_b)
        h = jax.nn.gelu(jnp.einsum('nfc,oc->nfo', x1, W1) + b1, approximate=False)
        y = jnp.einsum('nfc,oc->nfo', h, W2) + b2
        return layer_norm(y + x1, ln2_g, ln2_b)

    def _L1_ffn_ref(x, Wr, br, W1, b1, W2, b2, gamma, beta):
        import math
        import jax, jax.numpy as jnp
        import numpy as np
        CAPACITY_FACTOR = 1.25
        TOP_K = 2
        LN_EPS = 1e-05

        def _layer_norm(x, gamma, beta):
            mu = jnp.mean(x, axis=-1, keepdims=True)
            var = jnp.var(x, axis=-1, keepdims=True)
            return (x - mu) * jax.lax.rsqrt(var + LN_EPS) * gamma + beta
        B, S, D = x.shape
        E = Wr.shape[1]
        N = B * S
        K = TOP_K
        logits = jnp.mean(x, axis=1) @ Wr + br
        routing_weights = jax.nn.softmax(logits, axis=-1)
        capacity = float(math.ceil(N * CAPACITY_FACTOR / E))
        expected_loads = routing_weights.sum(axis=0) * (N / B)
        scale = jnp.where(expected_loads > capacity, capacity / expected_loads, 1.0)
        routing_weights = jax.nn.softmax(routing_weights * scale, axis=-1)
        rw_tok = jnp.broadcast_to(routing_weights[:, None, :], (B, S, E)).reshape(N, E)
        top_w, top_i = jax.lax.top_k(rw_tok, K)
        top_w = jax.nn.softmax(top_w, axis=-1)
        xf = x.reshape(N, D)
        h = jax.nn.gelu(jnp.einsum('nd,edf->enf', xf, W1) + b1[:, None, :], approximate=False)
        y = jnp.einsum('enf,efd->end', h, W2) + b2[:, None, :]
        w_dense = jnp.zeros((N, E), x.dtype).at[jnp.arange(N)[:, None], top_i].add(top_w)
        out = jnp.einsum('ne,end->nd', w_dense, y).reshape(B, S, D)
        out = _layer_norm(out + x, gamma, beta)
        return out
    edge_index = jnp.stack([src, dst])
    xn = _layernorm(x, axis=-1)
    x = x + _L0_gnn_ref(xn, L0_gnn_weight, L0_gnn_bias, edge_weight, src, dst) + _L0_mix_ref(xn[None], L0_mix_Wq, L0_mix_bq, L0_mix_Wk, L0_mix_bk, L0_mix_Wv, L0_mix_bv, L0_mix_Wo, L0_mix_bo, L0_mix_W1, L0_mix_b1, L0_mix_W2, L0_mix_b2, L0_mix_ln1_g, L0_mix_ln1_b, L0_mix_ln2_g, L0_mix_ln2_b)[0]
    x = x + _L0_ffn_ref(_layernorm(x, axis=-1)[None], L0_ffn_gate_w, L0_ffn_gate_b, L0_ffn_w1, L0_ffn_b1, L0_ffn_w2, L0_ffn_b2, L0_ffn_gamma, L0_ffn_beta)[0]
    xn = _layernorm(x, axis=-1)
    x = x + _L1_gnn_ref(xn, edge_index, L1_gnn_W0, L1_gnn_b0, L1_gnn_g0, L1_gnn_beta0, L1_gnn_W1, L1_gnn_b1, L1_gnn_g1, L1_gnn_beta1) + _L1_mix_ref(xn[None], L1_mix_Wqkv, L1_mix_ln1_g, L1_mix_ln1_b, L1_mix_W1, L1_mix_b1, L1_mix_W2, L1_mix_b2, L1_mix_ln2_g, L1_mix_ln2_b)[0]
    x = x + _L1_ffn_ref(_layernorm(x, axis=-1)[None], L1_ffn_Wr, L1_ffn_br, L1_ffn_W1, L1_ffn_b1, L1_ffn_W2, L1_ffn_b2, L1_ffn_gamma, L1_ffn_beta)[0]
    return x

_drawn_inputs = setup_inputs


def setup_inputs(seed=0):
    import zlib

    import numpy as np

    out = dict(_drawn_inputs(seed))
    spreads = {'L0_gnn_bias': (0.0, 0.1),
     'L0_mix_bq': (0.0, 2.0),
     'L0_mix_bk': (0.0, 2.0),
     'L0_mix_bv': (0.0, 0.1),
     'L0_mix_bo': (0.0, 0.1),
     'L0_mix_b1': (0.0, 0.284),
     'L0_mix_b2': (0.0, 0.1),
     'L0_mix_ln1_g': (1.0, 0.2),
     'L0_mix_ln1_b': (0.0, 0.1),
     'L0_mix_ln2_g': (1.0, 0.2),
     'L0_mix_ln2_b': (0.0, 0.1),
     'L0_ffn_gate_b': (0.0, 0.36),
     'L0_ffn_b1': (0.0, 0.8),
     'L0_ffn_b2': (0.0, 0.344),
     'L0_ffn_gamma': (1.0, 0.2),
     'L0_ffn_beta': (0.0, 0.1),
     'L1_gnn_g0': (1.0, 0.2),
     'L1_gnn_beta0': (0.0, 0.444),
     'L1_gnn_g1': (1.0, 0.2),
     'L1_gnn_beta1': (0.0, 0.502),
     'L1_mix_ln1_g': (1.0, 0.2),
     'L1_mix_ln1_b': (0.0, 0.313),
     'L1_mix_ln2_g': (1.0, 0.2),
     'L1_mix_ln2_b': (0.0, 0.359),
     'L1_ffn_br': (0.0, 0.1),
     'L1_ffn_b1': (0.0, 0.8),
     'L1_ffn_b2': (0.0, 0.688),
     'L1_ffn_gamma': (1.0, 0.2),
     'L1_ffn_beta': (0.0, 0.433)}
    factors = {'edge_weight': 3.137,
     'L0_mix_Wq': 8.0,
     'L0_mix_Wk': 8.0,
     'L0_mix_Wv': 5.593,
     'L0_ffn_w1': 2.906,
     'L1_gnn_b0': 5.073,
     'L1_gnn_b1': 5.365,
     'L1_mix_b1': 22.16,
     'L1_mix_b2': 6.556}
    for name, (base, spread) in spreads.items():
        noise = np.random.default_rng([zlib.crc32(name.encode()), seed]).standard_normal(out[name].shape)
        drawn = base * np.exp(spread * noise) if base else spread * noise
        out[name] = jnp.asarray(drawn.astype(out[name].dtype))
    for name, factor in factors.items():
        out[name] = (out[name] * factor).astype(out[name].dtype)
    return out
```

```python
from contextlib import ExitStack

import concourse.bass as bass
from concourse import mybir

F32 = mybir.dt.float32
I32 = mybir.dt.int32
U32 = mybir.dt.uint32
ALU = mybir.AluOpType
ACT = mybir.ActivationFunctionType
AX = mybir.AxisListType

N = 3125
D = 256
TP = 125
NT = N // TP
BT = 5
NB = NT // BT
EDGES = 53125
P = 128
CH = 416
ITEMS = 440
GR, GC = 4, ITEMS // 4
HU = 8
HI = ITEMS // HU
E0, E1, F = 16, 8, 512
BS = 4
BS = 4
MB = 64
NOWHERE = 4000
EXP = 2 * F + 4 * D + 4
EPS = 1e-5


ROWS = ["L0_gnn_bias", "L0_mix_bkv", "L0_mix_bo", "L0_mix_b2", "L0_mix_ln1_g", "L0_mix_ln1_b", "L0_mix_ln2_g",
        "L0_mix_ln2_b", "L0_ffn_gate_b", "L0_ffn_gamma", "L0_ffn_beta", "L1_gnn_b0", "L1_gnn_g0", "L1_gnn_beta0",
        "L1_gnn_b1", "L1_gnn_g1", "L1_gnn_beta1", "L1_mix_ln1_g", "L1_mix_ln1_b", "L1_mix_b2", "L1_mix_ln2_g",
        "L1_mix_ln2_b", "L1_ffn_br", "L1_ffn_gamma", "L1_ffn_beta"]
ROW_LEN = {"L0_mix_bkv": 512, "L0_ffn_gate_b": E0, "L1_ffn_br": E1}
MATS = {"L0_gnn_w": D, "L0_wq": D, "L0_wkv": 2 * D, "L0_wo": D, "L0_w1": 1024, "L0_gate": E0,
        "L1_gnn_w0": D, "L1_gnn_w1": D, "L1_wq": D, "L1_wkv": 2 * D, "L1_w1": D, "L1_w2": D, "L1_wr": E1}


class Chain:

    def __init__(self, eng, sem, spare):
        self.eng, self.sem, self.spare, self.base, self.k, self.i, self.per = eng, sem, spare, 0, 0, None, 0

    def enter(self, i, per):
        self.i, self.per, self.k = i, per, 0

    def leave(self, times):
        assert self.k == self.per, (self.k, self.per)
        self.base, self.i, self.k = self.base + self.per * times, None, 0

    def link(self, ins):
        ins.then_inc(self.sem, 1)
        self.k += 1
        if self.i is None:
            self.base, self.k = self.base + 1, 0
            self.eng.wait_ge(self.sem, self.base)
        else:
            self.eng.wait_ge(self.sem, self.i * self.per + (self.base + self.k))
            self.eng.sem_inc(self.spare, 1)


def program(nc, a, out):
    with ExitStack() as ctx:
        def sb(name, shape, dt=F32):
            return ctx.enter_context(nc.sbuf_tensor(name, shape, dt))

        sems = {}

        def S(name):
            if name not in sems:
                sems[name] = ctx.enter_context(nc.semaphore(name))
            return sems[name]

        def dram(name, shape, dt=F32):
            return nc.dram_tensor(name, shape, dt, kind="Internal").ap()

        def after(eng, name, val):
            eng.wait_ge(S(name), val)
            if not isinstance(val, int):
                eng.sem_inc(S("spare"), 1)

        X = sb("X", [TP, NT, D])
        XN = sb("XN", [TP, NT, D])
        big = sb("big", [P, NT * D + NT * (D + 1)])
        H = big[0:TP, 0:NT * D].rearrange("p (t f) -> p t f", t=NT)
        ACC = big[0:TP, NT * D:].rearrange("p (t f) -> p t f", t=NT)
        wexp = big[:, 0:BS * EXP].rearrange("p (s f) -> p s f", s=BS)
        batch = {n: sb(n, [P, BT * D]) for n in ("a", "b", "r")}
        a5, b5, r5 = (batch[n][0:TP, :].rearrange("p (s f) -> p s f", s=BT) for n in ("a", "b", "r"))
        bT = batch["b"][:, 0:2 * BT * TP].rearrange("p (k s c) -> p k s c", k=2, s=BT)
        aT = sb("aT", [P, 2, BT, TP])
        pT = sb("pT", [P, 2, BT, TP])
        hid = sb("hid", [P, 8 * BT * TP])
        hT = hid[:, :].rearrange("p (f s c) -> p f s c", f=8, s=BT)
        k5 = hid[0:TP, 0:BT * D].rearrange("p (s f) -> p s f", s=BT)
        v5 = hid[0:TP, BT * D:BT * D + BT * 2 * (P + 1)].rearrange("p (s h f) -> p s h f", s=BT, h=2)
        xTb = hid[:, 0:BS * 2 * P].rearrange("p (s k c) -> p s k c", s=BS, k=2)
        hTb = hid[:, BS * 2 * P:BS * 6 * P].rearrange("p (s f c) -> p s f c", s=BS, f=4)
        stats = sb("stats", [TP, BT, 6])
        mv = sb("mv", [TP, BT, 2])
        std = sb("std", [TP, BT])
        rstd = sb("rstd", [TP, BT])
        zt = sb("zt", [TP, BT, 2, 4])
        kvacc = sb("kvacc", [P, 2 * (P + 1)])
        kvbd = sb("kvbd", [P, 2, P + 4])
        mats = {n: sb("w_" + n, [P, 2, c])[:, :, :] for n, c in MATS.items() if n.startswith("L0")}
        for mine, other, c0 in (("L1_gnn_w0", "L0_gnn_w", 0), ("L1_gnn_w1", "L0_wo", 0), ("L1_wq", "L0_wq", 0),
                                ("L1_wkv", "L0_wkv", 0), ("L1_wr", "L0_gate", 0), ("L1_w1", "L0_w1", 0),
                                ("L1_w2", "L0_w1", D)):
            mats[mine] = mats[other][:, :, c0:c0 + MATS[mine]]
        w2_0 = sb("w2_0", [P, 8, D])
        rows, at = {}, {"L0": 0, "L1": 0}
        total = {g: sum(ROW_LEN.get(r, D) for r in ROWS if r.startswith(g)) for g in at}
        row_store = sb("row_store", [P, total["L0"]])
        gnn1 = [r for r in ROWS if r.startswith("L1_gnn")]
        at["L1"] = -len(gnn1) * D
        for r in ROWS:
            g, n = r[:2], ROW_LEN.get(r, D)
            rows[r] = row_store[:, at[g]:at[g] + n] if at[g] >= 0 else \
                w2_0[:, :, :].rearrange("p a b -> p (a b)")[:, at[g] + len(gnn1) * D:][:, 0:n]
            at[g] += n
        cols = sb("cols", [P, 16])
        ident = sb("ident", [P, P])
        ones = sb("ones", [P, P])
        lower = sb("lower", [P, P])
        iota_j = sb("iota_j", [P, P])
        eps = sb("eps", [P, 1])
        ix = sb("ix", [P, 2, HU // 2], I32)
        g8 = sb("g8", [P, HU, D + 1])
        M8 = sb("M8", [P, HU, TP])
        SRCI = sb("SRCI", [P, ITEMS], I32)
        DLOC = sb("DLOC", [P, ITEMS])
        WI = sb("WI", [P, ITEMS])
        tile_i = sb("tile_i", [P, ITEMS], I32)
        rdeg = sb("rdeg", [TP, NT])
        lg5 = sb("lg5", [TP, BT, E0])
        mx5 = sb("mx5", [P, BT, 8])
        mi5 = sb("mi5", [P, BT, 8], U32)
        top_v = sb("top_v", [TP, 2, NT])
        top_e = sb("top_e", [TP, 2, NT])
        gate = sb("gate", [TP, 2, NT])
        pos = sb("pos", [TP, 2, NT], I32)
        block_e = sb("block_e", [P, MB], I32)
        route = sb("route", [P, 12, 8])
        b2x = M8[:, :, :].rearrange("p a b -> p (a b)")[:, 0:2 * D].rearrange("p (s f) -> p s f", s=2)
        b2b = batch["b"][:, 0:BS * D].rearrange("p (s f) -> p s f", s=BS)

        def scratch(k, n, width, rows_=P):
            return big[0:rows_, k:k + n * width]

        in_tile = scratch(0, NT, CH).rearrange("p (t c) -> p t c", t=NT)
        edge_in = batch["a"][:, 0:CH], batch["b"][:, 0:CH], batch["r"][:, 0:CH]
        tid, slot, slot_t = (batch[n][:, CH:2 * CH] for n in ("a", "b", "r"))
        masked = batch["a"][:, 2 * CH:3 * CH]
        record = hid[:, 0:4 * CH].rearrange("p (c r) -> p c r", r=4)
        slot_i = hid[:, 4 * CH:5 * CH].bitcast(I32)
        tiny = hid[:, 5 * CH:5 * CH + 12 * NT].rearrange("p (k t) -> p k t", k=12)
        tile_of, item_i = scratch(0, 1, ITEMS), scratch(512, 1, ITEMS)
        records_n = scratch(1024, GR, 4 * P, GC).rearrange("q (g e r) -> q g e r", g=GR, r=4)
        record8 = sb("record8", [P, 2, 4, 4])
        small_keep = sb("tile_blocks", [P, NT])
        one_row = pT[:, :, :, :].rearrange("p k s c -> p (k s c)")[:, 0:CH]
        unused = sb("unused", [P, 4 * 8])
        cs = [scratch(400 * k, 1, 400, TP) for k in range(10)]
        small = scratch(4096, 12, E0).rearrange("p (k e) -> p k e", k=12)

        PS = ctx.enter_context(nc.psum_tensor("PS", [P, 8 * 512], F32))
        ps = PS[:, :]

        def bank(b, n=1):
            return ps[:, b * 512:(b + n) * 512]

        strips = ps[:, 0:10 * P].rearrange("p (k s c) -> p k s c", k=2, s=BT)[:, :, :, 0:TP]

        def halves(b):
            return ps[0:TP, b * 512:b * 512 + BT * D].rearrange("p (s f) -> p s f", s=BT)

        def xblk(s):
            return g8[:, 2 * s, 0:D]

        def yblk(s):
            return g8[:, 2 * s + 1, 0:D]

        Sd = dram("gather_rows", [N, D])
        Rd = dram("edge_records", [ITEMS * P, 4])
        Xs = dram("slot_rows", [MB * P, D])
        Ys = dram("slot_results", [MB * P, D])

        def over(r, n):
            return r.unsqueeze(1).broadcast_to([TP, n, r.shape[1]])

        def rowbc(name, n=BT):
            return over(rows[name][0:TP, :], n)

        def tiles(t, i):
            return t[:, bass.ds(i * BT, BT), :]

        FN = {"L0": 8, "L1": 2}
        NCONST = 10
        block = ctx.enter_context(nc.Block())

        @block.sync
        def _(sp):
            for dst, src in zip(edge_in, ("src", "dst", "edge_weight")):
                sp.dma_start(dst if src == "edge_weight" else dst.bitcast(I32), a[src]).then_inc(S("edges_in"), 16)
            sp.dma_start(X[:, :, :], a["x"].rearrange("(t p) f -> p t f", p=TP)).then_inc(S("x_in"), 16)

            def load_layer(g):
                for m in MATS:
                    if m.startswith(g):
                        sp.dma_start(mats[m], a[m].rearrange("(k p) f -> p k f", p=P)).then_inc(S(g + "_weights"), 16)
                lo = len(gnn1) * D if g == "L1" else 0
                if lo:
                    sp.dma_start(w2_0[:, :, :].rearrange("p a b -> p (a b)")[:, 0:lo],
                                 a["L1_rows"][0:lo].partition_broadcast(P)).then_inc(S("L1_weights"), 16)
                else:
                    sp.dma_start(w2_0[:, :, :], a["L0_w2"].rearrange("(k p) f -> p k f", p=P)).then_inc(S("L0_weights"), 16)
                sp.dma_start(row_store[:, 0:total[g] - lo], a[g + "_rows"][lo:total[g]].partition_broadcast(P)).then_inc(S(g + "_weights"), 16)
                sp.dma_start(cols[:, :], a[g + "_cols"]).then_inc(S(g + "_weights"), 16)

            load_layer("L0")
            after(sp, "constants", NCONST)
            rd = Rd.rearrange("(p i) r -> p (i r)", p=P)
            for k in range(ITEMS * 4 // 32):
                sp.dma_start(rd[:, k * 32:(k + 1) * 32], unused[:, :]).then_inc(S("records_clear"), 16)
            zero_rows = Xs.rearrange("(p r) f -> p (r f)", p=P)
            for k in range(MB * D // 1024):
                sp.dma_start(zero_rows[:, k * 1024:(k + 1) * 1024],
                             g8[:, :, :].rearrange("p a b -> p (a b)")[:, 0:1024]).then_inc(S("slots_clear"), 16)

            def store_rows(rows_, wait, val):
                after(sp, wait, val)
                sp.dma_start(Sd.rearrange("(t p) f -> p t f", p=TP), rows_).then_inc(S("rows_out"), 16)

            store_rows(H, "L0_support", NB)
            for h in range(2):
                store_rows(ACC[:, :, 0:D], "added", ITEMS * (h + 1) + HU)

            after(sp, "slots_filled", 16 * 2 * NT)
            with sp.Fori(0, MB // BS) as i:
                for s in range(BS):
                    after(sp, f"block_y{s}", i + 1)
                    b = i * BS + s
                    e = sp.value_load(block_e[0:1, bass.ds(b, 1)], min_val=0, max_val=E0 - 1)
                    sp.dma_start(wexp[:, s, :], a["L0_experts"][bass.ds(e, 1), :, :].rearrange("a p f -> (a p) f")).then_inc(S(f"expert_in{s}"), 16)
                    sp.dma_start(b2b[:, s, :], a["L0_b2"][bass.ds(e, 1), :].rearrange("a f -> (a f)").partition_broadcast(P)).then_inc(S(f"expert_in{s}"), 16)
                    sp.dma_start(xblk(s), Xs[bass.ds(b * P, P), :]).then_inc(S(f"expert_in{s}"), 16)

            after(sp, "L0_ffn_out", NB)
            load_layer("L1")
            store_rows(XN[:, :, :], "normed", 3 * NB)
            store_rows(H, "L1_g0_out", NB)
            after(sp, "routed", 1)
            for j in range(2):
                e = sp.value_load(mi5[0:1, 0, j:j + 1].bitcast(I32), min_val=0, max_val=E1 - 1)
                sp.dma_start(wexp[:, j, :], a["L1_experts"][bass.ds(e, 1), :, :].rearrange("a p f -> (a p) f")).then_inc(S("L1_experts_in"), 16)
                sp.dma_start(b2x[:, j, :], a["L1_b2"][bass.ds(e, 1), :].rearrange("a f -> (a f)").partition_broadcast(P)).then_inc(S("L1_experts_in"), 16)
            after(sp, "L1_ffn_out", NB)
            sp.dma_start(out.rearrange("(t p) f -> p t f", p=TP), X[:, :, :]).then_inc(S("result_out"), 16)
            sp.wait_ge(S("result_out"), 16)

        @block.gpsimd
        def _(pool):
            g = nc.gpsimd
            g.memset(ident[:, :], 0.0).then_inc(S("constants"), 1)
            g.memset(ones[:, :], 1.0).then_inc(S("constants"), 1)
            g.memset(lower[:, :], 1.0).then_inc(S("constants"), 1)
            g.memset(eps[:, :], EPS).then_inc(S("constants"), 1)
            g.memset(g8[:, :, :], 0.0).then_inc(S("constants"), 1)
            g.iota(iota_j[:, :], [[1, P]], base=0, channel_multiplier=0, allow_small_or_imprecise_dtypes=True).then_inc(S("constants"), 1)
            g.memset(unused[:, :], 0.0).then_inc(S("constants"), 1)
            pool.wait_ge(S("constants"), 7)
            g.affine_select(out=ident[:, :], in_=ident[:, :], compare_op=ALU.not_equal, fill=1.0, base=0,
                            pattern=[[-1, P]], channel_multiplier=1).then_inc(S("constants"), 1)
            g.affine_select(out=lower[:, :], in_=lower[:, :], compare_op=ALU.is_gt, fill=0.0, base=0,
                            pattern=[[1, P]], channel_multiplier=-1).then_inc(S("constants"), 1)
            g.memset(unused[:, :].rearrange("p (i r) -> p i r", r=4)[:, :, 1], float(NOWHERE)).then_inc(S("constants"), 1)

            pool.wait_ge(S("records_clear"), 16 * (ITEMS * 4 // 32))
            with pool.Fori(0, CH // 8) as i:
                for half in range(2):
                    after(pool, "records_staged", i * 2 + (half + 1))
                    for j in range(4):
                        g.indirect_dma_start(Rd, bass.IndirectOffsetOnAxis(ap=ix[:, half, j:j + 1], axis=0), record8[:, half, j, :], None,
                                             bounds_check=ITEMS * P - 1, oob_is_err=False).then_inc(S(f"records_sent{half}"), 16)
            for half in range(2):
                pool.wait_ge(S(f"records_sent{half}"), 64 * (CH // 8))
            g.iota(item_i, [[1, ITEMS]], base=0, channel_multiplier=0, allow_small_or_imprecise_dtypes=True).then_inc(S("item_numbers"), 1)
            pool.dma_start(records_n.rearrange("q g e r -> q g (e r)"), Rd.rearrange("(g q e) r -> q g (e r)", g=GR, q=GC)).then_inc(S("records_in"), 16)

            def hop(h):
                pool.wait_ge(S("rows_out"), 16 * (h + 1))
                with pool.Fori(0, HI) as i:
                    for j in range(HU):
                        if j % (HU // 2) == 0:
                            after(pool, "indices", (i + h * HI) * 2 + (j // (HU // 2) + 1))
                        after(pool, "item_sums", (i + h * HI) * HU + (j + 1))
                        g.indirect_dma_start(g8[:, j, 0:D], None, Sd, bass.IndirectOffsetOnAxis(
                            ap=ix[:, j // 4, j % 4:j % 4 + 1], axis=0)).then_inc(S(f"gathered{j}"), 16)

            pool.wait_ge(S("slots_clear"), 16 * (MB * D // 1024))
            for h in range(3):
                hop(h)

            pool.wait_ge(S("slot_tables"), 1)
            for j in range(2):
                for t in range(NT):
                    g.indirect_dma_start(Xs, bass.IndirectOffsetOnAxis(ap=pos[:, j, t:t + 1], axis=0),
                                         XN[:, t, :], None).then_inc(S("slots_filled"), 16)
            for s in range(BS):
                pool.dma_start(Ys[s * P:(s + 1) * P, :], yblk(s)).then_inc(S(f"block_stored{s}"), 16)
            with pool.Fori(0, MB // BS) as i:
                for s in range(BS):
                    after(pool, f"block_y{s}", i + 2)
                    pool.dma_start(Ys[bass.ds((i * BS + s) * P, P), :], yblk(s)).then_inc(S(f"block_stored{s}"), 16)
            for s in range(BS):
                pool.wait_ge(S(f"block_stored{s}"), 16 * (MB // BS + 1))
            for j in range(2):
                for t in range(NT):
                    g.indirect_dma_start((H if j == 0 else ACC)[:, t, 0:D], None, Ys,
                                         bass.IndirectOffsetOnAxis(ap=pos[:, j, t:t + 1], axis=0)).then_inc(S("expert_rows"), 16)
            for h in range(3, 5):
                hop(h)

        @block.scalar
        def _(act):
            A = nc.scalar

            def ln_std(p, i):
                after(act, p + "_var", i + 1)
                A.activation(std[:, :], mv[:, :, 1], ACT.Sqrt, bias=eps[0:TP, :]).then_inc(S(p + "_std"), 1)

            def norm_pass(k):
                with act.Fori(0, NB) as i:
                    ln_std("norm", i + k * NB)

            def load_batch(i, name):
                A.activation(a5, tiles(XN, i), ACT.Copy).then_inc(S(name), 1)

            def transposed(p, i, frm, to):
                after(act, p + frm, i + 1)
                A.activation(aT[:, :, :, :], strips, ACT.Copy).then_inc(S(p + to), 1)

            def mix(L):
                p, o = "m1", (NB if L == "L1" else 0)
                with act.Fori(0, NB) as i:
                    load_batch(i, p + "_in")
                    transposed(p, i + o, "_tr", "_aT")
                    if L == "L0":
                        after(act, p + "_kv", i + (o + 1))
                        A.activation(tiles(H, i), halves(0), ACT.Copy).then_inc(S("L0_support"), 1)
                    after(act, p + "_min", i + (o + 1))
                    A.activation(r5, b5, ACT.Exp).then_inc(S(p + "_exp"), 1)
                p = "m2"
                with act.Fori(0, NB) as i:
                    after(act, p + "_out", i + (o + 1))
                    load_batch(i, p + "_in")
                    transposed(p, i + o, "_tr", "_aT")
                    after(act, p + "_q", i + (o + 1))
                    for k in range(2):
                        if L == "L0":
                            ins = A.activation(pT[:, k, :, :], strips[:, k, :, :], ACT.Relu, bias=cols[:, k:k + 1])
                        else:
                            ins = A.activation(pT[:, k, :, :], strips[:, k, :, :], ACT.Relu)
                    ins.then_inc(S(p + "_relu"), 1)
                    after(act, p + "_min", i + (o + 1))
                    A.activation(bT, bT, ACT.Exp).then_inc(S(p + "_exp"), 1)
                    if L == "L0":
                        transposed(p, i + o, "_ttr", "_tT")
                    ln_std(p + "a", i + o)
                    transposed(p, i + o, "_x1tr", "_x1T")
                    fn, h0 = FN[L], (0 if L == "L0" else FN["L0"] * NB)
                    for f in range(fn):
                        b = 2 * (f % 4)
                        after(act, p + "_hp", i * fn + (h0 + f + 1))
                        A.activation(hT[:, f, :, :], bank(b, 2)[:, 0:BT * P].rearrange("p (s c) -> p s c", s=BT)[:, :, 0:TP],
                                     ACT.Relu if L == "L0" else ACT.Gelu, bias=cols[:, 2 + f:3 + f]).then_inc(S(p + "_h"), 1)
                    ln_std(p + "b", i + o)

            def hop_indices(h):
                with act.Fori(0, HI) as i:
                    for half in range(2):
                        after(act, "item_sums", (i + h * HI) * HU + 4 * (half + 1))
                        A.activation(ix[:, half, :], SRCI[:, bass.ds(i * HU + 4 * half, 4)], ACT.Copy).then_inc(S("indices"), 1)

            act.wait_ge(S("constants"), NCONST)
            act.wait_ge(S("L0_weights"), 16 * 9)
            def stage(i, half):
                c = bass.ds(i * 8 + 4 * half, 4)
                A.activation(ix[:, half, :], slot_i[:, c], ACT.Copy)
                A.activation(record8[:, half, :, :], record[:, c, :], ACT.Copy).then_inc(S("records_staged"), 1)

            act.wait_ge(S("slots_of_edges"), 1)
            for half in range(2):
                stage(0, half)
            with act.Fori(0, CH // 8 - 1) as i:
                for half in range(2):
                    after(act, f"records_sent{half}", i * 64 + 64)
                    stage(i + 1, half)
            norm_pass(0)
            act.wait_ge(S("normed"), 1 * NB)
            mix("L0")
            act.wait_ge(S("items_ready"), 1)
            for h in range(3):
                hop_indices(h)

            norm_pass(1)
            act.wait_ge(S("normed"), 2 * NB)
            with act.Fori(0, NB) as i:
                load_batch(i, "gate_in")
                transposed("gate", i, "_tr", "_aT")
            act.wait_ge(S("gate_diff"), 1)
            A.activation(gate[:, 1, :], gate[:, 0, :], ACT.Exp).then_inc(S("gate_exp"), 1)
            with act.Fori(0, MB // BS) as i:
                for s in range(BS):
                    after(act, "slots_tr", i * BS + (s + 1))
                    A.activation(xTb[:, s, :, :], bank(2 * s)[:, 0:2 * P].rearrange("p (k c) -> p k c", k=2), ACT.Copy).then_inc(S("slots_T"), 1)
                for s in range(BS):
                    after(act, "slots_hp", i * BS + (s + 1))
                    for f in range(4):
                        ins = A.activation(hTb[:, s, f, :], bank(2 * s + 1)[:, f * P:(f + 1) * P], ACT.Relu,
                                           bias=wexp[:, s, EXP - 4 + f:EXP - 3 + f])
                    ins.then_inc(S("slots_h"), 1)
            norm_pass(2)

            norm_pass(3)
            act.wait_ge(S("normed"), 3 * NB)
            act.wait_ge(S("L1_weights"), 16 * 10)
            mix("L1")
            for h in range(3, 5):
                hop_indices(h)
                p, o = "gnn", (h - 3) * NB
                with act.Fori(0, NB) as i:
                    transposed(p, i + o, "_tr", "_aT")
                    ln_std(p, i + o)
                    after(act, p + "_pre", i + (o + 1))
                    if h == 3:
                        A.activation(tiles(H, i), b5, ACT.Silu).then_inc(S("L1_g0_out"), 1)
                    else:
                        A.activation(r5, b5, ACT.Silu).then_inc(S(p + "_silu"), 1)

            norm_pass(4)
            act.wait_ge(S("mean_tr"), 1)
            A.activation(aT[:, :, :, :].rearrange("p k s c -> p (k s c)")[:, 0:2 * P], bank(1)[:, 0:2 * P], ACT.Copy).then_inc(S("mean_T"), 1)
            for k in range(3):
                act.wait_ge(S("route_shift"), k + 1)
                if k < 2:
                    A.activation(route[:, 2, :], route[:, 0, :], ACT.Exp, bias=route[:, 1, 0:1], accum_out=route[:, 3, 0:1]).then_inc(S("route_exp"), 1)
                else:
                    A.activation(route[:, 2, 0:1], route[:, 1, 0:1], ACT.Exp).then_inc(S("route_exp"), 1)
            act.wait_ge(S("L1_experts_in"), 64)
            with act.Fori(0, NB) as i:
                load_batch(i, "ff_in")
                transposed("ff", i, "_tr", "_aT")
                for j in range(2):
                    for f in range(4):
                        after(act, "ff_hp", i * 8 + (4 * j + f + 1))
                        A.activation(hT[:, f, :, :], bank(2 * f, 2)[:, 0:BT * P].rearrange("p (s c) -> p s c", s=BT)[:, :, 0:TP],
                                     ACT.Gelu, bias=wexp[:, j, EXP - 4 + f:EXP - 3 + f]).then_inc(S("ff_h"), 1)
                ln_std("ff", i)

        @block.tensor
        def _(pe):
            T = nc.tensor

            def transposes(src, name):
                for k in range(2):
                    for s in range(BT):
                        ins = T.transpose(strips[:, k, s, :], src[:, s, k * P:(k + 1) * P], ident[0:TP, 0:TP])
                ins.then_inc(S(name), 1)

            def project(w, out_, n, name):
                for s in range(BT):
                    for k in range(2):
                        ins = T.matmul(out_(s), aT[:, k, s, :], w[:, k, 0:n], start=(k == 0), stop=(k == 1))
                if name:
                    ins.then_inc(S(name), 1)

            def project_T(w, f, src, strip0, name):
                s = 0
                while s < BT:
                    c = strip0 + s
                    n = min(BT - s, 4 - c % 4)
                    dst = ps[:, c * P:(c + n) * P].rearrange("p (s c) -> p s c", s=n)[:, :, 0:TP]
                    for k in range(2):
                        ins = T.matmul(dst, w[:, k, f * P:(f + 1) * P], src[:, k, s:s + n, :], start=(k == 0), stop=(k == 1))
                    s += n
                if name:
                    ins.then_inc(S(name), 1)

            def second(w, fn, name):
                for s in range(BT):
                    for f in range(fn):
                        ins = T.matmul(halves(0)[:, s, :], hT[:, f, s, :], w(f), start=(f == 0), stop=(f == fn - 1))
                ins.then_inc(S(name), 1)

            def mix(L):
                p, o = "m1", (NB if L == "L1" else 0)
                with pe.Fori(0, NB) as i:
                    after(pe, p + "_in", i + (o + 1))
                    after(pe, p + "_added", i + (o + 1))
                    transposes(a5, p + "_tr")
                    after(pe, p + "_aT", i + (o + 1))
                    if L == "L0":
                        project(mats["L0_gnn_w"], lambda s: halves(0)[:, s, :], D, None)
                    project(mats[L + "_wkv"], lambda s: bank(3 + s)[0:TP, :], 2 * D, p + "_kv")
                    after(pe, p + "_phi", i + (o + 1))
                    if L == "L0":
                        after(pe, "L0_support", i + 1)
                    for k in range(2):
                        for s in range(BT):
                            ins = T.matmul(bank(0)[:, k * (P + 1):(k + 1) * (P + 1)], b5[:, s, k * P:(k + 1) * P], v5[:, s, k, :],
                                           start=(s == 0), stop=(s == BT - 1))
                    ins.then_inc(S(p + "_kvp"), 1)
                p = "m2"
                pe.wait_ge(S(p + "_kvbd"), 1 + o // NB)
                with pe.Fori(0, NB) as i:
                    after(pe, p + "_in", i + (o + 1))
                    transposes(a5, p + "_tr")
                    after(pe, p + "_aT", i + (o + 1))
                    project_T(mats[L + "_wq"], 0, aT, 0, None)
                    project_T(mats[L + "_wq"], 1, aT, BT, p + "_q")
                    after(pe, p + "_phi", i + (o + 1))
                    for s in range(BT):
                        for k in range(2):
                            ins = T.matmul(bank(3 + s)[0:TP, k * (P + 4):(k + 1) * (P + 4)], pT[:, k, s, :], kvbd[:, k, :], start=True, stop=True)
                    ins.then_inc(S(p + "_num"), 1)
                    if L == "L0":
                        after(pe, p + "_t", i + (o + 1))
                        transposes(r5, p + "_ttr")
                        after(pe, p + "_tT", i + (o + 1))
                        project(mats["L0_wo"], lambda s: halves(3)[:, s, :], D, p + "_o")
                    after(pe, p + "_x1", i + (o + 1))
                    transposes(b5, p + "_x1tr")
                    after(pe, p + "_x1T", i + (o + 1))
                    fn, h0 = FN[L], (0 if L == "L0" else FN["L0"] * NB)
                    for f in range(fn):
                        if f >= 4:
                            after(pe, p + "_h", i * fn + (h0 + f - 3))
                        project_T(mats[L + "_w1"], f, aT, 8 * (f % 4), p + "_hp")
                    after(pe, p + "_h", i * fn + (h0 + fn))
                    second((lambda f: w2_0[:, f, :]) if L == "L0" else (lambda f: mats["L1_w2"][:, f, :]), fn, p + "_y")

            def hop(h):
                n = D + 1 if h == 3 else D
                with pe.Fori(0, HI) as i:
                    for j in range(HU):
                        after(pe, f"gathered{j}", (i + h * HI) * 16 + 16)
                        pe.wait_ge(S("added"), (i + h * HI) * HU + (j + 1))
                        pe.wait_ge(S("edge_maps"), (i + h * HI) * HU + (j + 1))
                        T.matmul(bank(j)[0:TP, 0:n], M8[:, j, :], g8[:, j, 0:n], start=True, stop=True).then_inc(S("item_sums"), 1)

            pe.wait_ge(S("constants"), NCONST)
            pe.wait_ge(S("tile_counts"), 1)
            T.matmul(bank(0)[:, 0:NT], lower[:, :], tiny[:, 0, :], start=True, stop=True)
            T.matmul(bank(1)[:, 0:NT], ones[:, :], tiny[:, 0, :], start=True, stop=True).then_inc(S("tile_ranks"), 1)
            pe.wait_ge(S("records_in"), 16)
            for r in range(3):
                for g in range(GR):
                    ins = T.transpose(bank(1 + r)[:, g * GC:(g + 1) * GC], records_n[:, g, :, r], ident[0:GC, 0:GC])
            ins.then_inc(S("item_edges"), 1)
            pe.wait_ge(S("L0_weights"), 16 * 9)
            mix("L0")
            pe.sem_inc(S("item_sums"), HU)
            for h in range(3):
                hop(h)

            with pe.Fori(0, NB) as i:
                after(pe, "gate_in", i + 1)
                transposes(a5, "gate_tr")
                after(pe, "gate_aT", i + 1)
                after(pe, "gate_out", i + 1)
                project(mats["L0_gate"], lambda s: bank(3)[0:TP, s * E0:(s + 1) * E0], E0, "gate_logits")
            pe.wait_ge(S("choices"), 1)
            T.matmul(bank(0)[0:TP, 0:400], lower[0:TP, 0:TP], cs[2], start=True, stop=True)
            T.matmul(bank(1)[:, 0:400], ones[0:TP, :], cs[2], start=True, stop=True).then_inc(S("ranks"), 1)
            with pe.Fori(0, MB // BS) as i:
                for s in range(BS):
                    after(pe, f"expert_in{s}", i * 48 + 48)
                    for k in range(2):
                        ins = T.transpose(bank(2 * s)[:, k * P:(k + 1) * P], xblk(s)[:, k * P:(k + 1) * P], ident[:, :])
                    ins.then_inc(S("slots_tr"), 1)
                for s in range(BS):
                    after(pe, "slots_T", i * BS + (s + 1))
                    for f in range(4):
                        for k in range(2):
                            ins = T.matmul(bank(2 * s + 1)[:, f * P:(f + 1) * P], wexp[:, s, k * F + f * P:k * F + (f + 1) * P],
                                           xTb[:, s, k, :], start=(k == 0), stop=(k == 1))
                    ins.then_inc(S("slots_hp"), 1)
                for s in range(BS):
                    after(pe, "slots_h", i * BS + (s + 1))
                    for f in range(4):
                        ins = T.matmul(bank(2 * s)[:, 2 * P:4 * P], hTb[:, s, f, :], wexp[:, s, 2 * F + f * D:2 * F + (f + 1) * D],
                                       start=(f == 0), stop=(f == 3))
                    ins.then_inc(S("slots_yp"), 1)

            pe.wait_ge(S("L1_weights"), 16 * 10)
            pe.wait_ge(S("normed"), 3 * NB)
            mix("L1")
            for h in range(3, 5):
                hop(h)
                p, o = "gnn", (h - 3) * NB
                with pe.Fori(0, NB) as i:
                    after(pe, p + "_in", i + (o + 1))
                    transposes(a5, p + "_tr")
                    after(pe, p + "_aT", i + (o + 1))
                    project(mats[f"L1_gnn_w{h - 3}"], lambda s: halves(3)[:, s, :], D, p + "_lin")

            pe.wait_ge(S("normed"), 4 * NB)
            T.matmul(bank(0)[:, 0:D], ones[0:TP, :], XN[:, 0, :], start=True, stop=False)
            with pe.Fori(1, NT - 1) as t:
                T.matmul(bank(0)[:, 0:D], ones[0:TP, :], XN[:, bass.ds(t, 1), :].rearrange("p a f -> p (a f)"), start=False, stop=False)
            T.matmul(bank(0)[:, 0:D], ones[0:TP, :], XN[:, NT - 1, :], start=False, stop=True).then_inc(S("mean_sum"), 1)
            pe.wait_ge(S("mean"), 1)
            for k in range(2):
                ins = T.transpose(bank(1)[:, k * P:(k + 1) * P], batch["b"][:, k * P:(k + 1) * P], ident[:, :])
            ins.then_inc(S("mean_tr"), 1)
            pe.wait_ge(S("mean_T"), 1)
            mT = aT[:, :, :, :].rearrange("p k s c -> p (k s c)")
            for k in range(2):
                ins = T.matmul(bank(2)[:, 0:E1], mT[:, k * P:(k + 1) * P], mats["L1_wr"][:, k, :], start=(k == 0), stop=(k == 1))
            ins.then_inc(S("route_logits"), 1)
            pe.wait_ge(S("L1_experts_in"), 64)
            with pe.Fori(0, NB) as i:
                after(pe, "ff_in", i + 1)
                after(pe, "ff_used", i * 2 + 1)
                transposes(a5, "ff_tr")
                after(pe, "ff_aT", i + 1)
                for j in range(2):
                    if j == 1:
                        after(pe, "ff_used", i * 2 + 2)
                    for f in range(4):
                        project_T(wexp[:, j, 0:2 * F].rearrange("p (k f) -> p k f", k=2), f, aT, 8 * f, "ff_hp")
                    after(pe, "ff_h", i * 8 + 4 * (j + 1))
                    second(lambda f: wexp[:, j, 2 * F + f * D:2 * F + (f + 1) * D], 4, "ff_y")

        @block.vector
        def _(dve):
            V = nc.vector
            ch = Chain(dve, S("dve_chain"), S("spare"))
            link = ch.link

            def ln(p, i, src, dst, done=None, affine=None):
                for s in range(BT):
                    ins = V.bn_stats(stats[:, s, :], src(s))
                link(ins)
                for s in range(BT):
                    ins = V.bn_aggr(mv[:, s, :], stats[:, s, :])
                ins.then_inc(S(p + "_var"), 1)
                after(dve, p + "_std", i + 1)
                link(V.reciprocal(rstd[:, :], std[:, :]))
                for s in range(BT):
                    ins = V.tensor_scalar(dst(s), src(s), mv[:, s, 0:1], rstd[:, s:s + 1], ALU.subtract, ALU.mult)
                if affine:
                    link(ins)
                    whole = affine[2]
                    link(V.tensor_tensor(whole, whole, rowbc(affine[0]), ALU.mult))
                    ins = V.tensor_tensor(whole, whole, rowbc(affine[1]), ALU.add)
                if done:
                    ins.then_inc(S(done), 1)
                else:
                    link(ins)

            def one(t, i, s):
                return t[:, bass.ds(i * BT + s, 1), :].rearrange("p a f -> p (a f)")

            def norm_pass(k):
                with dve.Fori(0, NB) as i:
                    ch.enter(i, 2)
                    ln("norm", i + k * NB, lambda s: one(X, i, s), lambda s: one(XN, i, s), done="normed")
                ch.leave(NB)

            def add_out(i, src, name):
                V.tensor_tensor(tiles(X, i), tiles(X, i), src, ALU.add).then_inc(S(name), 1)

            def mix(L):
                p, o = "m1", (NB if L == "L1" else 0)
                link(V.memset(kvacc[:, :], 0.0))
                link(V.memset(v5[:, :, :, P:P + 1], 1.0))
                if L == "L0":
                    dve.sem_inc(S(p + "_added"), 1)
                with dve.Fori(0, NB) as i:
                    ch.enter(i, 1)
                    after(dve, p + "_kv", i + (o + 1))
                    kv = bank(3, 5)[0:TP, :].rearrange("p (s f) -> p s f", s=BT)
                    vin = kv[:, :, D:2 * D].rearrange("p s (h f) -> p s h f", h=2)
                    if L == "L0":
                        bv = rows["L0_mix_bkv"][0:TP, D:2 * D].rearrange("p (h f) -> p h f", h=2)
                        V.tensor_tensor(v5[:, :, 0, 0:P], vin[:, :, 0, :], over(bv[:, 0, :], BT), ALU.add)
                        V.tensor_tensor(v5[:, :, 1, 0:P], vin[:, :, 1, :], over(bv[:, 1, :], BT), ALU.add)
                        link(V.tensor_tensor(k5, kv[:, :, 0:D], over(rows["L0_mix_bkv"][0:TP, 0:D], BT), ALU.add))
                    else:
                        V.tensor_copy(v5[:, :, :, 0:P], vin)
                        link(V.tensor_copy(k5, kv[:, :, 0:D]))
                    V.tensor_scalar(b5, k5, 0.0, None, ALU.min).then_inc(S(p + "_min"), 1)
                    after(dve, p + "_exp", i + (o + 1))
                    V.scalar_tensor_tensor(out=b5, in0=k5, scalar=0.0, in1=r5, op0=ALU.max, op1=ALU.add).then_inc(S(p + "_phi"), 1)
                    after(dve, p + "_kvp", i + (o + 1))
                    V.tensor_tensor(kvacc[:, :], kvacc[:, :], bank(0)[:, 0:2 * (P + 1)], ALU.add).then_inc(S(p + "_added"), 1)
                ch.leave(NB)
                dve.wait_ge(S(p + "_added"), o + NB + 1)
                p = "m2"
                link(V.memset(kvbd[:, :, :], 0.0))
                ka = kvacc[:, :].rearrange("p (k c) -> p k c", k=2)
                for j in range(4):
                    q = slice(32 * j, 32 * j + 32)
                    V.tensor_copy(kvbd[q, :, q], ka[q, :, q])
                    ins = V.tensor_copy(kvbd[q, :, P + j:P + j + 1], ka[q, :, P:P + 1])
                ins.then_inc(S(p + "_kvbd"), 1)
                if L == "L0":
                    dve.sem_inc(S(p + "_out"), 1)
                with dve.Fori(0, NB) as i:
                    ch.enter(i, 15)
                    after(dve, p + "_relu", i + (o + 1))
                    for k in range(2):
                        if L == "L0":
                            ins = V.tensor_scalar(bT[:, k, :, :], strips[:, k, :, :], cols[:, k:k + 1], 0.0, ALU.add, ALU.min)
                        else:
                            ins = V.tensor_scalar(bT[:, k, :, :], strips[:, k, :, :], 0.0, None, ALU.min)
                    ins.then_inc(S(p + "_min"), 1)
                    after(dve, p + "_exp", i + (o + 1))
                    V.tensor_tensor(pT[:, :, :, :], pT[:, :, :, :], bT, ALU.add).then_inc(S(p + "_phi"), 1)
                    after(dve, p + "_num", i + (o + 1))
                    nd = bank(3, 5)[0:TP, :].rearrange("p (s f) -> p s f", s=BT)[:, :, 0:2 * (P + 4)].rearrange("p s (k c) -> p s k c", k=2)
                    link(V.tensor_scalar(zt[:, :, :, :], nd[:, :, :, P:P + 4], 1e-6, None, ALU.add))
                    link(V.reciprocal(zt[:, :, :, :], zt[:, :, :, :]))
                    for k in range(2):
                        ins = V.tensor_tensor(r5[:, :, k * P:(k + 1) * P].rearrange("p s (h c) -> p s h c", h=4),
                                              nd[:, :, k, 0:P].rearrange("p s (h c) -> p s h c", h=4),
                                              zt[:, :, k, :].unsqueeze(3).broadcast_to([TP, BT, 4, 32]), ALU.mult)
                    if L == "L0":
                        ins.then_inc(S(p + "_t"), 1)
                        after(dve, p + "_o", i + (o + 1))
                        link(V.tensor_tensor(r5, halves(3), rowbc("L0_mix_bo"), ALU.add))
                    else:
                        link(ins)
                    link(V.tensor_tensor(r5, r5, a5, ALU.add))
                    ln(p + "a", i + o, lambda s: r5[:, s, :], lambda s: b5[:, s, :], done=p + "_x1",
                       affine=(L + "_mix_ln1_g", L + "_mix_ln1_b", b5))
                    after(dve, p + "_y", i + (o + 1))
                    link(V.tensor_tensor(r5, halves(0), rowbc(L + "_mix_b2"), ALU.add))
                    link(V.tensor_tensor(r5, r5, b5, ALU.add))
                    ln(p + "b", i + o, lambda s: r5[:, s, :], lambda s: a5[:, s, :],
                       affine=(L + "_mix_ln2_g", L + "_mix_ln2_b", a5))
                    add_out(i, a5, p + "_out")
                ch.leave(NB)

            def hop(h):
                first = h * ITEMS
                weighted = h < 3
                with dve.Fori(0, HI) as i:
                    n0 = (i + h * HI) * HU

                    def add(j):
                        t = dve.value_load(tile_i[0:1, bass.ds(i * HU + j, 1)], min_val=0, max_val=NT - 1)
                        after(dve, "item_sums", n0 + (HU + j + 1))
                        after(dve, "added", n0 + (HU + j))
                        w = D + 1 if h == 3 else D
                        dst = ACC[:, bass.ds(t, 1), 0:w].rearrange("p a f -> p (a f)")
                        V.tensor_tensor(dst, dst, bank(j)[0:TP, 0:w], ALU.add).then_inc(S("added"), 1)

                    for j in range(HU):
                        after(dve, "item_sums", n0 + (j + 1))
                        c = bass.ds(i * HU + j, 1)
                        if weighted:
                            ins = V.tensor_scalar(M8[:, j, :], iota_j[:, 0:TP], DLOC[:, c], WI[:, c], ALU.is_equal, ALU.mult)
                        else:
                            ins = V.tensor_scalar(M8[:, j, :], iota_j[:, 0:TP], DLOC[:, c], None, ALU.is_equal)
                        ins.then_inc(S("edge_maps"), 1)
                        if j >= 2:
                            add(j - 2)
                    add(HU - 2)
                    add(HU - 1)

            dve.wait_ge(S("constants"), NCONST)
            dve.wait_ge(S("edges_in"), 48)
            V.memset(one_row, 1.0)
            src_f, dst_f = record[:, :, 1], record[:, :, 0]
            V.tensor_copy(dst_f, edge_in[1].bitcast(I32))
            V.tensor_copy(record[:, :, 2], edge_in[2])
            V.memset(record[:, :, 3], 0.0)
            link(V.tensor_copy(src_f, edge_in[0].bitcast(I32)))
            link(V.tensor_scalar(tid, src_f, -(TP // 2) * 1.0, 1.0 / TP, ALU.add, ALU.mult))
            link(V.tensor_scalar(tid, tid, 12582912.0, None, ALU.add))
            link(V.tensor_scalar(tid, tid, 12582912.0, None, ALU.subtract))
            for t in range(NT):
                ins = V.tensor_scalar(in_tile[:, t, :], tid, float(t), 0.0, ALU.is_equal, ALU.add, accum_out=tiny[:, 0, t:t + 1])
            link(ins)
            dve.sem_inc(S("tile_counts"), 1)
            dve.wait_ge(S("tile_ranks"), 1)
            tI = tiny.bitcast(I32)
            row = lambda k: tiny[:, k, :]
            incl = small_keep[:, :]
            link(V.tensor_scalar(row(1), bank(1)[:, 0:NT], float(P - 1), None, ALU.add))
            link(V.tensor_copy(tI[:, 2, :], row(1)))
            link(V.tensor_scalar(tI[:, 3, :], tI[:, 2, :], 7, None, ALU.arith_shift_right))
            link(V.tensor_copy(row(4), tI[:, 3, :]))
            link(V.tensor_tensor_scan(incl, ones[:, 0:NT], row(4), 0.0, ALU.mult, ALU.add))
            link(V.tensor_tensor(row(5), incl, row(4), ALU.subtract))
            link(V.tensor_scalar(row(6), row(5), float(P), -1.0, ALU.mult, ALU.add))
            link(V.tensor_tensor(row(7), row(6), bank(0)[:, 0:NT], ALU.add))
            link(V.tensor_scalar(slot, tid, float(NT) - 0.5, float(2 * ITEMS * P), ALU.is_gt, ALU.mult))
            for t in range(NT):
                link(V.tensor_tensor_scan(slot_t, one_row, in_tile[:, t, :], tiny[:, 7, t:t + 1], ALU.mult, ALU.add))
                link(V.tensor_tensor(masked, slot_t, in_tile[:, t, :], ALU.mult))
                link(V.tensor_tensor(slot, slot, masked, ALU.add))
            link(V.tensor_copy(slot_i, slot))
            dve.sem_inc(S("slots_of_edges"), 1)
            dve.wait_ge(S("item_numbers"), 1)
            link(V.memset(tile_of, 0.0))
            for t in range(NT):
                link(V.scalar_tensor_tensor(out=tile_of, in0=item_i, scalar=incl[:, t:t + 1], in1=tile_of, op0=ALU.is_ge, op1=ALU.add))
            V.tensor_scalar(tile_i[:, :], tile_of, float(NT - 1), None, ALU.min)
            dve.wait_ge(S("item_edges"), 1)
            V.tensor_copy(SRCI[:, :], bank(1)[:, 0:ITEMS])
            V.scalar_tensor_tensor(out=DLOC[:, :], in0=tile_of, scalar=-float(TP), in1=bank(2)[:, 0:ITEMS], op0=ALU.mult, op1=ALU.add)
            link(V.tensor_copy(WI[:, :], bank(3)[:, 0:ITEMS]))
            dve.sem_inc(S("items_ready"), 1)

            dve.wait_ge(S("x_in"), 16)
            dve.wait_ge(S("L0_weights"), 16 * 9)
            norm_pass(0)
            mix("L0")
            dve.wait_ge(S("L0_support"), NB)
            dve.sem_inc(S("added"), HU)
            dve.wait_ge(S("m2_out"), NB + 1)
            for h in range(3):
                dve.wait_ge(S("rows_out"), 16 * (h + 1))
                link(V.tensor_copy(ACC[:, :, 0:D], H))
                hop(h)
            dve.wait_ge(S("added"), 3 * ITEMS + HU)
            link(V.tensor_tensor(X[:, :, :], X[:, :, :], ACC[:, :, 0:D], ALU.add))
            link(V.tensor_tensor(X[:, :, :], X[:, :, :], rowbc("L0_gnn_bias", NT), ALU.add))

            norm_pass(1)
            dve.sem_inc(S("gate_out"), 1)
            with dve.Fori(0, NB) as i:
                ch.enter(i, 3)
                after(dve, "gate_logits", i + 1)
                link(V.tensor_tensor(lg5[:, :, :], bank(3)[0:TP, 0:BT * E0].rearrange("p (s e) -> p s e", s=BT),
                                     rowbc("L0_ffn_gate_b"), ALU.add))
                for s in range(BT):
                    ins = V.max(mx5[0:TP, s, :], lg5[:, s, :])
                link(ins)
                for s in range(BT):
                    ins = V.max_index(mi5[0:TP, s, :], mx5[0:TP, s, :], lg5[:, s, :])
                link(ins)
                for j in range(2):
                    V.tensor_copy(top_v[:, j, bass.ds(i * BT, BT)], mx5[0:TP, :, j])
                    ins = V.tensor_copy(top_e[:, j, bass.ds(i * BT, BT)], mi5[0:TP, :, j])
                ins.then_inc(S("gate_out"), 1)
            ch.leave(NB)
            dve.wait_ge(S("gate_out"), NB + 1)
            V.tensor_tensor(gate[:, 0, :], top_v[:, 1, :], top_v[:, 0, :], ALU.subtract).then_inc(S("gate_diff"), 1)
            et = lambda k: cs[k].rearrange("p (e t) -> p e t", e=E0)
            expert = iota_j[0:TP, 0:E0].unsqueeze(2).broadcast_to([TP, E0, NT])
            for j in range(2):
                ins = V.tensor_tensor(et(j), expert, top_e[:, j, :].unsqueeze(1).broadcast_to([TP, E0, NT]), ALU.is_equal)
            link(ins)
            V.memset(cs[3], 1.0)
            link(V.tensor_tensor(cs[2], cs[0], cs[1], ALU.add))
            dve.sem_inc(S("choices"), 1)
            link(V.memset(et(3)[:, :, 0:1], 0.0))
            dve.wait_ge(S("gate_exp"), 1)
            link(V.tensor_scalar(rdeg[:, :], gate[:, 1, :], 1.0, None, ALU.add))
            link(V.reciprocal(gate[:, 0, :], rdeg[:, :]))
            link(V.tensor_tensor(gate[:, 1, :], gate[:, 1, :], gate[:, 0, :], ALU.mult))
            dve.wait_ge(S("ranks"), 1)
            link(V.tensor_copy(cs[4], bank(1)[0:TP, 0:400]))
            link(V.tensor_tensor_scan(cs[5], cs[3], cs[4], 0.0, ALU.mult, ALU.add))
            link(V.tensor_tensor(cs[6], cs[5], cs[4], ALU.subtract))
            sm = lambda k: small[0:TP, k, :]
            smi = small.bitcast(I32)
            link(V.tensor_scalar(sm(0), et(5)[:, :, NT - 1], 127.0, None, ALU.add))
            link(V.tensor_copy(smi[0:TP, 1, :], sm(0)))
            link(V.tensor_scalar(smi[0:TP, 2, :], smi[0:TP, 1, :], 7, None, ALU.arith_shift_right))
            link(V.tensor_copy(sm(3), smi[0:TP, 2, :]))
            link(V.tensor_tensor_scan(sm(4), ones[0:TP, 0:E0], sm(3), 0.0, ALU.mult, ALU.add))
            link(V.tensor_tensor(sm(5), sm(4), sm(3), ALU.subtract))
            link(V.tensor_scalar(sm(6), sm(5), float(P), None, ALU.mult))
            link(V.tensor_tensor(cs[7], cs[6], bank(0)[0:TP, 0:400], ALU.add))
            link(V.tensor_tensor(et(7), et(7), sm(6).unsqueeze(2).broadcast_to([TP, E0, NT]), ALU.add))
            for j in range(2):
                link(V.tensor_tensor(cs[8], cs[j], cs[7], ALU.mult))
                link(V.tensor_reduce(rdeg[:, :], et(8).rearrange("p e t -> p t e"), AX.X, ALU.add))
                link(V.tensor_copy(pos[:, j, :], rdeg[:, :]))
            blk = cs[8][:, 0:MB]
            link(V.memset(blk, 0.0))
            for e in range(E0 - 1):
                link(V.scalar_tensor_tensor(out=blk, in0=iota_j[0:TP, 0:MB], scalar=sm(4)[:, e:e + 1], in1=blk, op0=ALU.is_ge, op1=ALU.add))
            link(V.tensor_copy(block_e[0:TP, :], blk))
            dve.sem_inc(S("slot_tables"), 1)
            for s in range(BS):
                dve.sem_inc(S(f"block_y{s}"), 1)
            with dve.Fori(0, MB // BS) as i:
                for s in range(BS):
                    after(dve, "slots_yp", i * BS + (s + 1))
                    after(dve, f"block_stored{s}", i * 16 + 16)
                    V.tensor_tensor(yblk(s), bank(2 * s)[:, 2 * P:4 * P], b2b[:, s, :], ALU.add).then_inc(S(f"block_y{s}"), 1)
            dve.wait_ge(S("expert_rows"), 16 * 2 * NT)
            with dve.Fori(0, NB) as i:
                ch.enter(i, 8)

                def w5(j):
                    return gate[:, j, bass.ds(i * BT, BT)].unsqueeze(2).broadcast_to([TP, BT, D])

                V.tensor_tensor(r5, tiles(H, i), w5(0), ALU.mult)
                link(V.tensor_tensor(b5, tiles(ACC[:, :, 0:D], i), w5(1), ALU.mult))
                link(V.tensor_tensor(r5, r5, b5, ALU.add))
                link(V.tensor_tensor(r5, r5, tiles(XN, i), ALU.add))
                ln("norm", i + 2 * NB, lambda s: r5[:, s, :], lambda s: a5[:, s, :], affine=("L0_ffn_gamma", "L0_ffn_beta", a5))
                add_out(i, a5, "L0_ffn_out")
            ch.leave(NB)

            dve.wait_ge(S("L0_ffn_out"), NB)
            norm_pass(3)
            dve.wait_ge(S("L1_weights"), 16 * 10)
            mix("L1")
            for h in range(3, 5):
                p, o = "gnn", (h - 3) * NB
                dve.wait_ge(S("rows_out"), 16 * (h + 1))
                link(V.memset(g8[:, :, D:D + 1], 1.0))
                link(V.memset(ACC, 0.0))
                hop(h)
                dve.wait_ge(S("added"), (h + 1) * ITEMS + HU)
                if h == 3:
                    link(V.tensor_scalar(rdeg[:, :], ACC[:, :, D], 1.0, None, ALU.max))
                    link(V.reciprocal(rdeg[:, :], rdeg[:, :]))
                with dve.Fori(0, NB) as i:
                    ch.enter(i, 6)
                    link(V.tensor_tensor(r5, tiles(ACC[:, :, 0:D], i), rdeg[:, bass.ds(i * BT, BT)].unsqueeze(2).broadcast_to([TP, BT, D]), ALU.mult))
                    V.tensor_tensor(a5, r5, tiles(XN if h == 3 else H, i), ALU.add).then_inc(S(p + "_in"), 1)
                    after(dve, p + "_lin", i + (o + 1))
                    link(V.tensor_tensor(r5, halves(3), rowbc(f"L1_gnn_b{h - 3}"), ALU.add))
                    ln(p, i + o, lambda s: r5[:, s, :], lambda s: b5[:, s, :], done=p + "_pre",
                       affine=(f"L1_gnn_g{h - 3}", f"L1_gnn_beta{h - 3}", b5))
                    if h == 4:
                        after(dve, p + "_silu", i + 1)
                        add_out(i, r5, "L1_g1_out")
                        after(dve, "L1_g1_out", i + 1)
                ch.leave(NB)
            dve.wait_ge(S("L1_g1_out"), NB)

            norm_pass(4)
            dve.wait_ge(S("mean_sum"), 1)
            V.tensor_scalar(batch["b"][:, 0:D], bank(0)[:, 0:D], 1.0 / N, None, ALU.mult).then_inc(S("mean"), 1)
            R = lambda k: route[:, k, :]

            def softmax():
                link(V.max(mx5[:, 0, :], R(0)))
                V.tensor_scalar(route[:, 1, 0:1], mx5[:, 0, 0:1], -1.0, None, ALU.mult).then_inc(S("route_shift"), 1)

            dve.wait_ge(S("route_logits"), 1)
            link(V.tensor_tensor(R(0), bank(2)[:, 0:E1], rows["L1_ffn_br"], ALU.add))
            softmax()
            dve.wait_ge(S("route_exp"), 1)
            link(V.reciprocal(route[:, 5, 0:1], route[:, 3, 0:1]))
            link(V.tensor_scalar(R(4), R(2), route[:, 5, 0:1], None, ALU.mult))
            capacity = float(-(-N * 5 // (4 * E1)))
            link(V.tensor_scalar(R(6), R(4), float(N), None, ALU.mult))
            link(V.reciprocal(R(7), R(6)))
            link(V.tensor_scalar(R(8), R(7), capacity, 1.0, ALU.mult, ALU.min))
            link(V.tensor_tensor(R(0), R(4), R(8), ALU.mult))
            softmax()
            dve.wait_ge(S("route_exp"), 2)
            link(V.reciprocal(route[:, 5, 0:1], route[:, 3, 0:1]))
            link(V.tensor_scalar(R(4), R(2), route[:, 5, 0:1], None, ALU.mult))
            link(V.max(mx5[:, 0, :], R(4)))
            link(V.max_index(mi5[:, 0, :], mx5[:, 0, :], R(4)))
            dve.sem_inc(S("routed"), 1)
            V.tensor_tensor(route[:, 1, 0:1], mx5[:, 0, 1:2], mx5[:, 0, 0:1], ALU.subtract).then_inc(S("route_shift"), 1)
            dve.wait_ge(S("route_exp"), 3)
            link(V.tensor_scalar(route[:, 5, 0:1], route[:, 2, 0:1], 1.0, None, ALU.add))
            link(V.reciprocal(route[:, 9, 0:1], route[:, 5, 0:1]))
            link(V.tensor_tensor(route[:, 9, 1:2], route[:, 2, 0:1], route[:, 9, 0:1], ALU.mult))
            dve.wait_ge(S("L1_experts_in"), 64)
            link(V.tensor_scalar(b2x[:, 0, :], b2x[:, 0, :], route[:, 9, 0:1], None, ALU.mult))
            link(V.scalar_tensor_tensor(out=b2x[:, 0, :], in0=b2x[:, 1, :], scalar=route[:, 9, 1:2], in1=b2x[:, 0, :], op0=ALU.mult, op1=ALU.add))
            dve.sem_inc(S("ff_used"), 1)
            with dve.Fori(0, NB) as i:
                ch.enter(i, 6)
                after(dve, "ff_y", i * 2 + 1)
                V.scalar_tensor_tensor(out=r5, in0=halves(0), scalar=route[0:TP, 9, 0:1], in1=tiles(XN, i), op0=ALU.mult, op1=ALU.add).then_inc(S("ff_used"), 1)
                after(dve, "ff_y", i * 2 + 2)
                V.scalar_tensor_tensor(out=r5, in0=halves(0), scalar=route[0:TP, 9, 1:2], in1=r5, op0=ALU.mult, op1=ALU.add).then_inc(S("ff_used"), 1)
                after(dve, "ff_used", i * 2 + 3)
                link(V.tensor_tensor(r5, r5, over(b2x[0:TP, 0, :], BT), ALU.add))
                ln("ff", i, lambda s: r5[:, s, :], lambda s: b5[:, s, :], affine=("L1_ffn_gamma", "L1_ffn_beta", b5))
                add_out(i, b5, "L1_ffn_out")
            ch.leave(NB)


def kernel(**inputs):
    import numpy as np
    import concourse.bacc as bacc
    from concourse.bass_utils import run_bass_kernel_spmd as run

    v = {k: np.asarray(x) for k, x in inputs.items()}
    a = {"x": v["x"]}
    for name, fill in (("src", NOWHERE), ("dst", 0), ("edge_weight", 0)):
        pad = np.full(CH * P - EDGES, fill, v[name].dtype)
        a[name] = np.concatenate([v[name], pad]).reshape(P, CH)
    cat = np.concatenate
    a["L0_gnn_w"] = v["L0_gnn_weight"]
    a["L0_wq"], a["L0_wo"], a["L0_w1"], a["L0_w2"] = (v["L0_mix_" + n] for n in ("Wq", "Wo", "W1", "W2"))
    a["L0_wkv"] = cat([v["L0_mix_Wk"], v["L0_mix_Wv"]], axis=1)
    a["L0_gate"] = v["L0_ffn_gate_w"]
    a["L1_gnn_w0"], a["L1_gnn_w1"] = v["L1_gnn_W0"].T, v["L1_gnn_W1"].T
    qkv = v["L1_mix_Wqkv"].T
    a["L1_wq"], a["L1_wkv"] = qkv[:, 0:D], qkv[:, D:3 * D]
    a["L1_w1"], a["L1_w2"] = v["L1_mix_W1"].T, v["L1_mix_W2"].T
    a["L1_wr"] = v["L1_ffn_Wr"]
    v["L0_mix_bkv"] = cat([v["L0_mix_bk"], v["L0_mix_bv"]])
    for g, names in (("L0", ("L0_mix_bq", "L0_mix_b1")), ("L1", ("L1_mix_b1",))):
        c = [np.zeros((P, 2), np.float32)] * (g == "L1") + [v[n].reshape(-1, P).T for n in names]
        c = cat(c, axis=1)
        a[g + "_cols"] = cat([c, np.zeros((P, 16 - c.shape[1]), np.float32)], axis=1)
        a[g + "_rows"] = cat([v[r] for r in ROWS if r.startswith(g)])
    for g, w1, b1, w2, b2 in (("L0", "w1", "b1", "w2", "b2"), ("L1", "W1", "b1", "W2", "b2")):
        w1, b1, w2, b2 = (v[f"{g}_ffn_{n}"] for n in (w1, b1, w2, b2))
        e = w1.shape[0]
        a[g + "_experts"] = cat([w1.reshape(e, 2, P, F).transpose(0, 2, 1, 3).reshape(e, P, 2 * F),
                                 w2.reshape(e, 4, P, D).transpose(0, 2, 1, 3).reshape(e, P, 4 * D),
                                 b1.reshape(e, 4, P).transpose(0, 2, 1)], axis=2)
        a[g + "_b2"] = b2
    nc = bacc.Bacc("TRN2", target_bir_lowering=False, num_devices=1)
    arrays, aps = {}, {}
    for name, x in a.items():
        x = np.ascontiguousarray(x)
        arrays["in_" + name] = x
        aps[name] = nc.dram_tensor("in_" + name, x.shape, mybir.dt.from_np(x.dtype), kind="ExternalInput").ap()
    out = nc.dram_tensor("out_0", (N, D), F32, kind="ExternalOutput").ap()
    program(nc, aps, out)
    return run(nc, [arrays], core_ids=[0]).results[0]["out_0"]
```

```python
from contextlib import ExitStack

import concourse.bass as bass
from concourse import mybir

F32 = mybir.dt.float32
I32 = mybir.dt.int32
U32 = mybir.dt.uint32
ALU = mybir.AluOpType
ACT = mybir.ActivationFunctionType
AX = mybir.AxisListType

N = 3125
D = 256
TP = 125
NT = N // TP
BT = 5
NB = NT // BT
EDGES = 53125
P = 128
CH = 416
ITEMS = 450
GR, GC = 4, 114
RB = GR * GC
HU = 18
HG = 9
HM = 3
HB, HB0 = 3, 5
HI = ITEMS // HU
MAPS = ITEMS // HM + 1
E0, E1, F = 16, 8, 512
BS = 4
MB = 64
NOWHERE = 4000
EXP = 2 * F + 4 * D + 4
EPS = 1e-5


ROWS = ["L0_gnn_bias", "L0_mix_bkv", "L0_mix_bo", "L0_mix_b2", "L0_mix_ln1_g", "L0_mix_ln1_b", "L0_mix_ln2_g",
        "L0_mix_ln2_b", "L0_ffn_gate_b", "L0_ffn_gamma", "L0_ffn_beta", "L1_gnn_b0", "L1_gnn_g0", "L1_gnn_beta0",
        "L1_gnn_b1", "L1_gnn_g1", "L1_gnn_beta1", "L1_mix_ln1_g", "L1_mix_ln1_b", "L1_mix_b2", "L1_mix_ln2_g",
        "L1_mix_ln2_b", "L1_ffn_br", "L1_ffn_gamma", "L1_ffn_beta"]
ROW_LEN = {"L0_mix_bkv": 512, "L0_ffn_gate_b": E0, "L1_ffn_br": E1}
MATS = {"L0_gnn_w": D, "L0_wq": D, "L0_wkv": 2 * D, "L0_wo": D, "L0_w1": 1024, "L0_gate": E0,
        "L1_gnn_w0": D, "L1_gnn_w1": D, "L1_wq": D, "L1_wkv": 2 * D, "L1_w1": D, "L1_w2": D, "L1_wr": E1}


class Chain:

    def __init__(self, eng, sem, spare):
        self.eng, self.sem, self.spare, self.base, self.k, self.i, self.per = eng, sem, spare, 0, 0, None, 0

    def enter(self, i, per):
        self.i, self.per, self.k = i, per, 0

    def leave(self, times):
        assert self.k == self.per, (self.k, self.per)
        self.base, self.i, self.k = self.base + self.per * times, None, 0

    def link(self, ins):
        ins.then_inc(self.sem, 1)
        self.k += 1
        if self.i is None:
            self.base, self.k = self.base + 1, 0
            self.eng.wait_ge(self.sem, self.base)
        else:
            self.eng.wait_ge(self.sem, self.i * self.per + (self.base + self.k))
            self.eng.sem_inc(self.spare, 1)


def program(nc, a, out):
    with ExitStack() as ctx:
        def sb(name, shape, dt=F32):
            return ctx.enter_context(nc.sbuf_tensor(name, shape, dt))

        sems = {}

        def S(name):
            if name not in sems:
                sems[name] = ctx.enter_context(nc.semaphore(name))
            return sems[name]

        def dram(name, shape, dt=F32):
            return nc.dram_tensor(name, shape, dt, kind="Internal").ap()

        def after(eng, name, val):
            eng.wait_ge(S(name), val)
            if not isinstance(val, int):
                eng.sem_inc(S("spare"), 1)

        X = sb("X", [TP, NT, D])
        XN = sb("XN", [TP, NT, D])
        big = sb("big", [P, NT * D + NT * (D + 1)])
        H = big[0:TP, 0:NT * D].rearrange("p (t f) -> p t f", t=NT)
        ACC = big[0:TP, NT * D:].rearrange("p (t f) -> p t f", t=NT)
        wexp = big[:, 0:BS * EXP].rearrange("p (s f) -> p s f", s=BS)
        batch = {n: sb(n, [P, BT * D]) for n in ("a", "b", "r")}
        a5, b5, r5 = (batch[n][0:TP, :].rearrange("p (s f) -> p s f", s=BT) for n in ("a", "b", "r"))
        bT = batch["b"][:, 0:2 * BT * TP].rearrange("p (k s c) -> p k s c", k=2, s=BT)
        aT = sb("aT", [P, 2, BT, TP])
        pT = sb("pT", [P, 2, BT, TP])
        hid = sb("hid", [P, 8 * BT * TP])
        hT = hid[:, :].rearrange("p (f s c) -> p f s c", f=8, s=BT)
        k5 = hid[0:TP, 0:BT * D].rearrange("p (s f) -> p s f", s=BT)
        v5 = hid[0:TP, BT * D:BT * D + BT * 2 * (P + 1)].rearrange("p (s h f) -> p s h f", s=BT, h=2)
        xTb = hid[:, 0:BS * 2 * P].rearrange("p (s k c) -> p s k c", s=BS, k=2)
        hTb = hid[:, BS * 2 * P:BS * 6 * P].rearrange("p (s f c) -> p s f c", s=BS, f=4)
        stats = sb("stats", [TP, BT, 6])
        mv = sb("mv", [TP, BT, 2])
        std = sb("std", [TP, BT])
        rstd = sb("rstd", [TP, BT])
        zt = sb("zt", [TP, BT, 2, 4])
        kvacc = sb("kvacc", [P, 2 * (P + 1)])
        kvbd = sb("kvbd", [P, 2, P + 4])
        mats = {n: sb("w_" + n, [P, 2, c])[:, :, :] for n, c in MATS.items() if n.startswith("L0")}
        for mine, other, c0 in (("L1_gnn_w0", "L0_gnn_w", 0), ("L1_gnn_w1", "L0_wo", 0), ("L1_wq", "L0_wq", 0),
                                ("L1_wkv", "L0_wkv", 0), ("L1_wr", "L0_gate", 0), ("L1_w1", "L0_w1", 0),
                                ("L1_w2", "L0_w1", D)):
            mats[mine] = mats[other][:, :, c0:c0 + MATS[mine]]
        w2_0 = sb("w2_0", [P, 8, D])
        rows, at = {}, {"L0": 0, "L1": 0}
        total = {g: sum(ROW_LEN.get(r, D) for r in ROWS if r.startswith(g)) for g in at}
        row_store = sb("row_store", [P, total["L0"]])
        gnn1 = [r for r in ROWS if r.startswith("L1_gnn")]
        at["L1"] = -len(gnn1) * D
        for r in ROWS:
            g, n = r[:2], ROW_LEN.get(r, D)
            rows[r] = row_store[:, at[g]:at[g] + n] if at[g] >= 0 else \
                w2_0[:, :, :].rearrange("p a b -> p (a b)")[:, at[g] + len(gnn1) * D:][:, 0:n]
            at[g] += n
        cols = sb("cols", [P, 16])
        ident = sb("ident", [P, P])
        ones = sb("ones", [P, P])
        lower = sb("lower", [P, P])
        iota_j = sb("iota_j", [P, P])
        eps = sb("eps", [P, 1])
        ix = sb("ix", [P, HU // HG, HG], I32)
        ixs = sb("ixs", [P, 2, 4], I32)
        g8 = sb("g8", [P, HG, D + 1])
        M8 = sb("M8", [P, 2, HM, TP])
        SRCI = sb("SRCI", [P, ITEMS], I32)
        DLOC = sb("DLOC", [P, ITEMS + HM])
        WI = sb("WI", [P, ITEMS + HM])
        tile_i = sb("tile_i", [P, ITEMS], I32)
        rdeg = sb("rdeg", [TP, NT])
        lg5 = sb("lg5", [TP, BT, E0])
        mx5 = sb("mx5", [P, BT, 8])
        mi5 = sb("mi5", [P, BT, 8], U32)
        top_v = sb("top_v", [TP, 2, NT])
        top_e = sb("top_e", [TP, 2, NT])
        gate = sb("gate", [TP, 2, NT])
        pos = sb("pos", [TP, 2, NT], I32)
        block_e = sb("block_e", [P, MB], I32)
        route = sb("route", [P, 12, 8])
        b2x = M8[:, :, :, :].rearrange("p c a b -> p (c a b)")[:, 0:2 * D].rearrange("p (s f) -> p s f", s=2)
        b2b = batch["b"][:, 0:BS * D].rearrange("p (s f) -> p s f", s=BS)

        def scratch(k, n, width, rows_=P):
            return big[0:rows_, k:k + n * width]

        in_tile = scratch(0, NT, CH).rearrange("p (t c) -> p t c", t=NT)
        edge_in = batch["a"][:, 0:CH], batch["b"][:, 0:CH], batch["r"][:, 0:CH]
        tid, slot, slot_t = (batch[n][:, CH:2 * CH] for n in ("a", "b", "r"))
        masked = batch["a"][:, 2 * CH:3 * CH]
        at_acc = NT * D
        record = scratch(NT * CH, 4, CH).rearrange("p (c r) -> p c r", r=4)
        slot_i = scratch((NT + 4) * CH, 1, CH).bitcast(I32)
        tiny = scratch((NT + 5) * CH, 12, NT).rearrange("p (k t) -> p k t", k=12)
        tile_of, item_i = scratch(at_acc, 1, ITEMS), scratch(at_acc + 512, 1, ITEMS)
        records_n = scratch(at_acc + 1024, GR, 4 * P, GC).rearrange("q (g e r) -> q g e r", g=GR, r=4)
        record8 = sb("record8", [P, 2, 4, 4])
        small_keep = route[:, :, :].rearrange("p a b -> p (a b)")[:, 0:NT]
        one_row = pT[:, :, :, :].rearrange("p k s c -> p (k s c)")[:, 0:CH]
        unused = g8[:, HG - 1, 0:4 * 12]
        cs = [scratch(400 * k, 1, 400, TP) for k in range(10)]
        small = scratch(4096, 12, E0).rearrange("p (k e) -> p k e", k=12)

        PS = ctx.enter_context(nc.psum_tensor("PS", [P, 8 * 512], F32))
        ps = PS[:, :]

        def bank(b, n=1):
            return ps[:, b * 512:(b + n) * 512]

        strips = ps[:, 0:10 * P].rearrange("p (k s c) -> p k s c", k=2, s=BT)[:, :, :, 0:TP]

        def halves(b):
            return ps[0:TP, b * 512:b * 512 + BT * D].rearrange("p (s f) -> p s f", s=BT)

        def pair(j):
            return ps[:, j * 1024:j * 1024 + BT * P].rearrange("p (s c) -> p s c", s=BT)[:, :, 0:TP]

        upper = ps[0:TP, BT * D:2 * BT * D].rearrange("p (s f) -> p s f", s=BT)
        dens = ps[0:TP, 0:BT * 8].rearrange("p (s k c) -> p s k c", s=BT, k=2)

        def xblk(s):
            return g8[:, 2 * s, 0:D]

        def yblk(s):
            return g8[:, 2 * s + 1, 0:D]

        Sd = dram("gather_rows", [N, D])
        Rd = dram("edge_records", [RB * P, 4])
        Xs = dram("slot_rows", [MB * P, D])
        Ys = dram("slot_results", [MB * P, D])

        def over(r, n):
            return r.unsqueeze(1).broadcast_to([TP, n, r.shape[1]])

        def rowbc(name, n=BT):
            return over(rows[name][0:TP, :], n)

        def tiles(t, i):
            return t[:, bass.ds(i * BT, BT), :]

        FN = {"L0": 8, "L1": 2}
        NCONST = 9
        EARLY = 2
        SUB0, SUB1 = HI // (NB - EARLY), HI // NB

        def spread(sub, *lists):
            return [[q * sub * HU // 84 for q in at] for at in lists]

        AT = {
            "keys": spread(SUB1, [0, 8, 34], [4, 12, 42], [30, 36, 50]),
            "L0": spread(SUB0, [0, 3, 9, 13, 25, 37, 44] + [47 + 2 * f for f in range(8)] + [80],
                         [1, 5, 17, 24, 27, 43] + [46 + 2 * f for f in range(8)] + [63, 66, 69, 72, 75],
                         [10, 15, 21, 32, 38, 78, 81]),
            "L1": spread(SUB1, [0, 3, 11, 15, 31, 42] + [47, 51] + [70],
                         [1, 5, 19, 39, 45, 48, 54, 57, 60, 63, 66],
                         [12, 17, 24, 25, 34, 68, 73]),
        }
        block = ctx.enter_context(nc.Block())

        @block.sync
        def _(sp):
            for dst, src in zip(edge_in, ("src", "dst", "edge_weight")):
                sp.dma_start(dst if src == "edge_weight" else dst.bitcast(I32), a[src]).then_inc(S("edges_in"), 16)
            sp.dma_start(X[:, :, :], a["x"].rearrange("(t p) f -> p t f", p=TP)).then_inc(S("x_in"), 16)

            def load_layer(g):
                for m in MATS:
                    if m.startswith(g):
                        sp.dma_start(mats[m], a[m].rearrange("(k p) f -> p k f", p=P)).then_inc(S(g + "_weights"), 16)
                lo = len(gnn1) * D if g == "L1" else 0
                if lo:
                    sp.dma_start(w2_0[:, :, :].rearrange("p a b -> p (a b)")[:, 0:lo],
                                 a["L1_rows"][0:lo].partition_broadcast(P)).then_inc(S("L1_weights"), 16)
                else:
                    sp.dma_start(w2_0[:, :, :], a["L0_w2"].rearrange("(k p) f -> p k f", p=P)).then_inc(S("L0_weights"), 16)
                sp.dma_start(row_store[:, 0:total[g] - lo], a[g + "_rows"][lo:total[g]].partition_broadcast(P)).then_inc(S(g + "_weights"), 16)
                sp.dma_start(cols[:, :], a[g + "_cols"]).then_inc(S(g + "_weights"), 16)

            load_layer("L0")
            after(sp, "constants", NCONST)
            sp.dma_start(Rd.rearrange("(p k i) r -> p k (i r)", p=P, i=12),
                         unused[:, :].unsqueeze(1).broadcast_to([P, RB // 12, 48])).then_inc(S("records_clear"), 16)
            after(sp, "slots_of_edges", 1)

            def stage(i, half):
                c = bass.ds(i * 8 + 4 * half, 4)
                sp.dma_start(ixs[:, half, :], slot_i[:, c]).then_inc(S(f"records_staged{half}"), 16)
                sp.dma_start(record8[:, half, :, :].rearrange("p c r -> p (c r)"),
                             record[:, c, :].rearrange("p c r -> p (c r)")).then_inc(S(f"records_staged{half}"), 16)

            for half in range(2):
                stage(0, half)
            with sp.Fori(0, CH // 8 - 1) as i:
                for half in range(2):
                    after(sp, f"records_sent{half}", i * 64 + 64)
                    stage(i + 1, half)
            zero_rows = Xs.rearrange("(p k r) f -> p k (r f)", p=P, k=16)
            sp.dma_start(zero_rows, g8[:, :, :].rearrange("p a b -> p (a b)")[:, 0:1024].unsqueeze(1).broadcast_to([P, 16, 1024])).then_inc(S("slots_clear"), 16)

            def store_rows(rows_, wait, val):
                after(sp, wait, val)
                sp.dma_start(Sd.rearrange("(t p) f -> p t f", p=TP), rows_).then_inc(S("rows_out"), 16)

            store_rows(H, "L0_support", NB)
            for h in range(2):
                store_rows(ACC[:, :, 0:D], "added", ITEMS * (h + 1) + 2 * HB)

            after(sp, "slots_filled", 16 * 2 * NT)
            with sp.Fori(0, MB // BS) as i:
                for s in range(BS):
                    after(sp, f"block_y{s}", i + 1)
                    b = i * BS + s
                    e = sp.value_load(block_e[0:1, bass.ds(b, 1)], min_val=0, max_val=E0 - 1)
                    sp.dma_start(wexp[:, s, :], a["L0_experts"][bass.ds(e, 1), :, :].rearrange("a p f -> (a p) f")).then_inc(S(f"expert_in{s}"), 16)
                    sp.dma_start(b2b[:, s, :], a["L0_b2"][bass.ds(e, 1), :].rearrange("a f -> (a f)").partition_broadcast(P)).then_inc(S(f"expert_in{s}"), 16)
                    sp.dma_start(xblk(s), Xs[bass.ds(b * P, P), :]).then_inc(S(f"expert_in{s}"), 16)

            after(sp, "L0_ffn_out", NB)
            load_layer("L1")
            store_rows(XN[:, :, :], "normed", 3 * NB)
            store_rows(H, "L1_g0_out", NB)
            after(sp, "routed", 1)
            for j in range(2):
                e = sp.value_load(mi5[0:1, 0, j:j + 1].bitcast(I32), min_val=0, max_val=E1 - 1)
                sp.dma_start(wexp[:, j, :], a["L1_experts"][bass.ds(e, 1), :, :].rearrange("a p f -> (a p) f")).then_inc(S("L1_experts_in"), 16)
                sp.dma_start(b2x[:, j, :], a["L1_b2"][bass.ds(e, 1), :].rearrange("a f -> (a f)").partition_broadcast(P)).then_inc(S("L1_experts_in"), 16)
            after(sp, "L1_ffn_out", NB)
            sp.dma_start(out.rearrange("(t p) f -> p t f", p=TP), X[:, :, :]).then_inc(S("result_out"), 16)
            sp.wait_ge(S("result_out"), 16)

        @block.gpsimd
        def _(pool):
            g = nc.gpsimd
            g.memset(ident[:, :], 0.0).then_inc(S("constants"), 1)
            g.memset(ones[:, :], 1.0).then_inc(S("constants"), 1)
            g.memset(lower[:, :], 1.0).then_inc(S("constants"), 1)
            g.memset(eps[:, :], EPS).then_inc(S("constants"), 1)
            g.memset(g8[:, :, :], 0.0).then_inc(S("constants"), 1)
            g.iota(iota_j[:, :], [[1, P]], base=0, channel_multiplier=0, allow_small_or_imprecise_dtypes=True).then_inc(S("constants"), 1)
            pool.wait_ge(S("constants"), 6)
            g.affine_select(out=ident[:, :], in_=ident[:, :], compare_op=ALU.not_equal, fill=1.0, base=0,
                            pattern=[[-1, P]], channel_multiplier=1).then_inc(S("constants"), 1)
            g.affine_select(out=lower[:, :], in_=lower[:, :], compare_op=ALU.is_gt, fill=0.0, base=0,
                            pattern=[[1, P]], channel_multiplier=-1).then_inc(S("constants"), 1)
            g.memset(unused[:, :].rearrange("p (i r) -> p i r", r=4)[:, :, 1], float(NOWHERE)).then_inc(S("constants"), 1)

            pool.wait_ge(S("records_clear"), 16)
            with pool.Fori(0, CH // 8) as i:
                for half in range(2):
                    after(pool, f"records_staged{half}", i * 32 + 32)
                    for j in range(4):
                        g.indirect_dma_start(Rd, bass.IndirectOffsetOnAxis(ap=ixs[:, half, j:j + 1], axis=0), record8[:, half, j, :], None,
                                             bounds_check=ITEMS * P - 1, oob_is_err=False).then_inc(S(f"records_sent{half}"), 16)
            for half in range(2):
                pool.wait_ge(S(f"records_sent{half}"), 64 * (CH // 8))
            g.iota(item_i, [[1, ITEMS]], base=0, channel_multiplier=0, allow_small_or_imprecise_dtypes=True).then_inc(S("item_numbers"), 1)
            pool.dma_start(records_n.rearrange("q g e r -> q g (e r)"), Rd.rearrange("(g q e) r -> q g (e r)", g=GR, q=GC)).then_inc(S("records_in"), 16)

            def hop(h):
                pool.wait_ge(S("rows_out"), 16 * (h + 1))
                with pool.Fori(0, HI) as i:
                    for j in range(HU):
                        if j % HG == 0:
                            after(pool, "indices", (i + h * HI) * (HU // HG) + (j // HG + 1))
                        if j % HM == 0:
                            after(pool, "item_sums", (i + h * HI) * HU + (HU - HG + j + HM))
                        g.indirect_dma_start(g8[:, j % HG, 0:D], None, Sd, bass.IndirectOffsetOnAxis(
                            ap=ix[:, j // HG, j % HG:j % HG + 1], axis=0)).then_inc(S(f"gathered{j % HG}"), 16)

            pool.wait_ge(S("slots_clear"), 16)
            for h in range(3):
                hop(h)

            pool.wait_ge(S("slot_tables"), 1)
            for j in range(2):
                for t in range(NT):
                    g.indirect_dma_start(Xs, bass.IndirectOffsetOnAxis(ap=pos[:, j, t:t + 1], axis=0),
                                         XN[:, t, :], None).then_inc(S("slots_filled"), 16)
            for s in range(BS):
                pool.dma_start(Ys[s * P:(s + 1) * P, :], yblk(s)).then_inc(S(f"block_stored{s}"), 16)
            with pool.Fori(0, MB // BS) as i:
                for s in range(BS):
                    after(pool, f"block_y{s}", i + 2)
                    pool.dma_start(Ys[bass.ds((i * BS + s) * P, P), :], yblk(s)).then_inc(S(f"block_stored{s}"), 16)
            for s in range(BS):
                pool.wait_ge(S(f"block_stored{s}"), 16 * (MB // BS + 1))
            for j in range(2):
                for t in range(NT):
                    g.indirect_dma_start((H if j == 0 else ACC)[:, t, 0:D], None, Ys,
                                         bass.IndirectOffsetOnAxis(ap=pos[:, j, t:t + 1], axis=0)).then_inc(S("expert_rows"), 16)
            for h in range(3, 5):
                hop(h)

        @block.scalar
        def _(act):
            A = nc.scalar

            def ln_std(p, i):
                after(act, p + "_var", i + 1)
                A.activation(std[:, :], mv[:, :, 1], ACT.Sqrt, bias=eps[0:TP, :]).then_inc(S(p + "_std"), 1)

            def norm_pass(k):
                with act.Fori(0, NB) as i:
                    ln_std("norm", i + k * NB)

            def load_batch(i, name):
                A.activation(a5, tiles(XN, i), ACT.Copy).then_inc(S(name), 1)

            def transposed(p, i, frm, to):
                after(act, p + frm, i + 1)
                A.activation(aT[:, :, :, :], strips, ACT.Copy).then_inc(S(p + to), 1)

            def mix1(L, i):
                i1 = i + (1 if L == "L0" else NB + 1)
                load_batch(i, "m1_in")
                yield
                after(act, "m1_tr", i1)
                A.activation(aT[:, :, :, :], strips, ACT.Copy).then_inc(S("m1_aT"), 1)
                yield
                if L == "L0":
                    after(act, "m1_kv", i1)
                    A.activation(tiles(H, i), halves(5), ACT.Copy).then_inc(S("L0_support"), 1)
                after(act, "m1_min", i1)
                A.activation(r5, b5, ACT.Exp).then_inc(S("m1_exp"), 1)
                yield

            def mix2(L, i):
                i1 = i + (1 if L == "L0" else NB + 1)
                after(act, "m2_out", i1)
                load_batch(i, "m2_in")
                yield
                after(act, "m2_tr", i1)
                A.activation(aT[:, :, :, :], strips, ACT.Copy).then_inc(S("m2_aT"), 1)
                yield
                after(act, "m2_q", i1)
                for k in range(2):
                    if L == "L0":
                        ins = A.activation(pT[:, k, :, :], strips[:, k, :, :], ACT.Relu, bias=cols[:, k:k + 1])
                    else:
                        ins = A.activation(pT[:, k, :, :], strips[:, k, :, :], ACT.Relu)
                ins.then_inc(S("m2_relu"), 1)
                yield
                after(act, "m2_min", i1)
                A.activation(bT, bT, ACT.Exp).then_inc(S("m2_exp"), 1)
                yield
                if L == "L0":
                    after(act, "m2_ttr", i1)
                    A.activation(aT[:, :, :, :], strips, ACT.Copy).then_inc(S("m2_tT"), 1)
                    yield
                ln_std("m2a", i1 - 1)
                yield
                after(act, "m2_x1tr", i1)
                A.activation(aT[:, :, :, :], strips, ACT.Copy).then_inc(S("m2_x1T"), 1)
                yield
                fn, h0 = FN[L], (0 if L == "L0" else FN["L0"] * NB)
                for f in range(fn):
                    after(act, "m2_hp", i * fn + (h0 + f + 1))
                    A.activation(hT[:, f, :, :], pair(f % 2), ACT.Relu if L == "L0" else ACT.Gelu,
                                 bias=cols[:, 2 + f:3 + f]).then_inc(S("m2_h"), 1)
                    yield
                ln_std("m2b", i1 - 1)
                yield

            def alone(step, L, start, end):
                with act.Fori(start, end) as i:
                    for _ in step(L, i):
                        pass

            def hop(h, step=None, L=None, b0=NB, sub=1, at=()):
                def indices(i):
                    for k in range(HU // HG):
                        after(act, "item_sums", (i + h * HI) * HU + HG * (k + 1))
                        A.activation(ix[:, k, :], SRCI[:, bass.ds(i * HU + HG * k, HG)], ACT.Copy).then_inc(S("indices"), 1)
                        yield k

                if b0 < NB:
                    with act.Fori(b0, NB) as b:
                        steps = step(L, b)
                        for u in range(sub):
                            for k in indices((b - b0) * sub + u):
                                for q in range(u * HU + HG * k, u * HU + HG * (k + 1)):
                                    if q in at:
                                        next(steps)
                        assert next(steps, "end") == "end"
                if (NB - b0) * sub < HI:
                    with act.Fori((NB - b0) * sub, HI) as i:
                        for _ in indices(i):
                            pass

            act.wait_ge(S("constants"), NCONST)
            act.wait_ge(S("L0_weights"), 16 * 9)
            norm_pass(0)
            act.wait_ge(S("normed"), 1 * NB)
            alone(mix1, "L0", 0, NB)
            alone(mix2, "L0", 0, EARLY)
            act.wait_ge(S("items_ready"), 1)
            hop(0, mix2, "L0", EARLY, SUB0, AT["L0"][0])
            hop(1)
            hop(2)

            norm_pass(1)
            act.wait_ge(S("normed"), 2 * NB)
            with act.Fori(0, NB) as i:
                load_batch(i, "gate_in")
                transposed("gate", i, "_tr", "_aT")
            act.wait_ge(S("gate_diff"), 1)
            A.activation(gate[:, 1, :], gate[:, 0, :], ACT.Exp).then_inc(S("gate_exp"), 1)
            with act.Fori(0, MB // BS) as i:
                for s in range(BS):
                    after(act, "slots_tr", i * BS + (s + 1))
                    A.activation(xTb[:, s, :, :], bank(2 * s)[:, 0:2 * P].rearrange("p (k c) -> p k c", k=2), ACT.Copy).then_inc(S("slots_T"), 1)
                for s in range(BS):
                    after(act, "slots_hp", i * BS + (s + 1))
                    for f in range(4):
                        ins = A.activation(hTb[:, s, f, :], bank(2 * s + 1)[:, f * P:(f + 1) * P], ACT.Relu,
                                           bias=wexp[:, s, EXP - 4 + f:EXP - 3 + f])
                    ins.then_inc(S("slots_h"), 1)
            norm_pass(2)

            norm_pass(3)
            act.wait_ge(S("normed"), 3 * NB)
            act.wait_ge(S("L1_weights"), 16 * 10)
            for h in range(3, 5):
                if h == 3:
                    hop(h, mix1, "L1", 0, SUB1, AT["keys"][0])
                else:
                    hop(h, mix2, "L1", 0, SUB1, AT["L1"][0])
                p, o = "gnn", (h - 3) * NB
                with act.Fori(0, NB) as i:
                    transposed(p, i + o, "_tr", "_aT")
                    ln_std(p, i + o)
                    after(act, p + "_pre", i + (o + 1))
                    if h == 3:
                        A.activation(tiles(H, i), b5, ACT.Silu).then_inc(S("L1_g0_out"), 1)
                    else:
                        A.activation(r5, b5, ACT.Silu).then_inc(S(p + "_silu"), 1)

            norm_pass(4)
            act.wait_ge(S("mean_tr"), 1)
            A.activation(aT[:, :, :, :].rearrange("p k s c -> p (k s c)")[:, 0:2 * P], bank(1)[:, 0:2 * P], ACT.Copy).then_inc(S("mean_T"), 1)
            for k in range(3):
                act.wait_ge(S("route_shift"), k + 1)
                if k < 2:
                    A.activation(route[:, 2, :], route[:, 0, :], ACT.Exp, bias=route[:, 1, 0:1], accum_out=route[:, 3, 0:1]).then_inc(S("route_exp"), 1)
                else:
                    A.activation(route[:, 2, 0:1], route[:, 1, 0:1], ACT.Exp).then_inc(S("route_exp"), 1)
            act.wait_ge(S("L1_experts_in"), 64)
            with act.Fori(0, NB) as i:
                load_batch(i, "ff_in")
                transposed("ff", i, "_tr", "_aT")
                for j in range(2):
                    for f in range(4):
                        after(act, "ff_hp", i * 8 + (4 * j + f + 1))
                        A.activation(hT[:, f, :, :], bank(2 * f, 2)[:, 0:BT * P].rearrange("p (s c) -> p s c", s=BT)[:, :, 0:TP],
                                     ACT.Gelu, bias=wexp[:, j, EXP - 4 + f:EXP - 3 + f]).then_inc(S("ff_h"), 1)
                ln_std("ff", i)

        @block.tensor
        def _(pe):
            T = nc.tensor

            def transposes(src, name):
                for k in range(2):
                    for s in range(BT):
                        ins = T.transpose(strips[:, k, s, :], src[:, s, k * P:(k + 1) * P], ident[0:TP, 0:TP])
                ins.then_inc(S(name), 1)

            def project(w, out_, n, name):
                for s in range(BT):
                    for k in range(2):
                        ins = T.matmul(out_(s), aT[:, k, s, :], w[:, k, 0:n], start=(k == 0), stop=(k == 1))
                if name:
                    ins.then_inc(S(name), 1)

            def project_T(w, f, src, strip0, name):
                s = 0
                while s < BT:
                    c = strip0 + s
                    n = min(BT - s, 4 - c % 4)
                    dst = ps[:, c * P:(c + n) * P].rearrange("p (s c) -> p s c", s=n)[:, :, 0:TP]
                    for k in range(2):
                        ins = T.matmul(dst, w[:, k, f * P:(f + 1) * P], src[:, k, s:s + n, :], start=(k == 0), stop=(k == 1))
                    s += n
                if name:
                    ins.then_inc(S(name), 1)

            def second(w, fn, s, name):
                for f in range(fn):
                    ins = T.matmul(halves(0)[:, s, :], hT[:, f, s, :], w(f), start=(f == 0), stop=(f == fn - 1))
                if name:
                    ins.then_inc(S(name), 1)

            def mix1(L, i):
                i1 = i + (1 if L == "L0" else NB + 1)
                after(pe, "m1_in", i1)
                after(pe, "m1_added", i1)
                transposes(a5, "m1_tr")
                yield
                after(pe, "m1_aT", i1)
                if L == "L0":
                    project(mats["L0_gnn_w"], lambda s: halves(5)[:, s, :], D, None)
                project(mats[L + "_wkv"][:, :, 0:D], lambda s: halves(0)[:, s, :], D, None)
                project(mats[L + "_wkv"][:, :, D:2 * D], lambda s: upper[:, s, :], D, "m1_kv")
                yield
                after(pe, "m1_phi", i1)
                for k in range(2):
                    for s in range(BT):
                        ins = T.matmul(bank(0)[:, k * (P + 1):(k + 1) * (P + 1)], b5[:, s, k * P:(k + 1) * P], v5[:, s, k, :],
                                       start=(s == 0), stop=(s == BT - 1))
                ins.then_inc(S("m1_kvp"), 1)
                yield

            def mix2(L, i):
                i1 = i + (1 if L == "L0" else NB + 1)
                after(pe, "m2_in", i1)
                transposes(a5, "m2_tr")
                yield
                after(pe, "m2_aT", i1)
                project_T(mats[L + "_wq"], 0, aT, 0, None)
                project_T(mats[L + "_wq"], 1, aT, BT, "m2_q")
                yield
                after(pe, "m2_phi", i1)
                for s in range(BT):
                    for k in range(2):
                        T.matmul(upper[:, s, k * P:(k + 1) * P], pT[:, k, s, :], kvbd[:, k, 0:P], start=True, stop=True)
                        ins = T.matmul(dens[:, s, k, :], pT[:, k, s, :], kvbd[:, k, P:P + 4], start=True, stop=True)
                ins.then_inc(S("m2_num"), 1)
                yield
                if L == "L0":
                    after(pe, "m2_t", i1)
                    transposes(r5, "m2_ttr")
                    yield
                    after(pe, "m2_tT", i1)
                    project(mats["L0_wo"], lambda s: upper[:, s, :], D, "m2_o")
                    yield
                after(pe, "m2_x1", i1)
                transposes(b5, "m2_x1tr")
                yield
                after(pe, "m2_x1T", i1)
                fn, h0 = FN[L], (0 if L == "L0" else FN["L0"] * NB)
                for f in range(fn):
                    if f >= 2:
                        after(pe, "m2_h", i * fn + (h0 + f - 1))
                    project_T(mats[L + "_w1"], f, aT, 8 * (f % 2), "m2_hp")
                    yield
                after(pe, "m2_h", i * fn + (h0 + fn))
                for s in range(BT):
                    second((lambda f: w2_0[:, f, :]) if L == "L0" else (lambda f: mats["L1_w2"][:, f, :]), fn, s,
                           "m2_y" if s == BT - 1 else None)
                    yield

            def alone(step, L, start, end):
                with pe.Fori(start, end) as i:
                    for _ in step(L, i):
                        pass

            def hop(h, step=None, L=None, b0=NB, sub=1, at=()):
                n = D + 1 if h == 3 else D
                in_bank = 1 if h == 3 else 2

                def item(i, j):
                    n0 = (i + h * HI) * HU
                    after(pe, f"gathered{j % HG}", (i + h * HI) * (16 * HU // HG) + 16 * (j // HG + 1))
                    if j % HM == 0:
                        after(pe, "edge_maps", i * (HU // HM) + (h * MAPS + j // HM + 1))
                    if j % in_bank == 0:
                        after(pe, "added", n0 + (2 * HB - in_bank * HB + j + in_bank))
                    q = (j // in_bank) % HB * 512 + HB0 * 512 + j % in_bank * D
                    T.matmul(ps[0:TP, q:q + n], M8[:, j // HM % 2, j % HM, :], g8[:, j % HG, 0:n], start=True, stop=True).then_inc(S("item_sums"), 1)

                if b0 < NB:
                    with pe.Fori(b0, NB) as b:
                        steps = step(L, b)
                        for q in range(sub * HU):
                            item((b - b0) * sub + q // HU, q % HU)
                            for _ in range(at.count(q)):
                                next(steps)
                        assert next(steps, "end") == "end"
                if (NB - b0) * sub < HI:
                    with pe.Fori((NB - b0) * sub, HI) as i:
                        for j in range(HU):
                            item(i, j)

            pe.wait_ge(S("constants"), NCONST)
            pe.wait_ge(S("tile_counts"), 1)
            T.matmul(bank(0)[:, 0:NT], lower[:, :], tiny[:, 0, :], start=True, stop=True)
            T.matmul(bank(1)[:, 0:NT], ones[:, :], tiny[:, 0, :], start=True, stop=True).then_inc(S("tile_ranks"), 1)
            pe.wait_ge(S("L0_weights"), 16 * 9)
            alone(mix1, "L0", 0, NB)
            pe.sem_inc(S("item_sums"), HU)
            pe.wait_ge(S("m2_kvbd"), 1)
            alone(mix2, "L0", 0, EARLY)
            pe.wait_ge(S("m2_out"), EARLY + 1)
            pe.wait_ge(S("records_in"), 16)
            for r in range(3):
                for g in range(GR):
                    ins = T.transpose(bank(1 + r)[:, g * GC:(g + 1) * GC], records_n[:, g, :, r], ident[0:GC, 0:GC])
            ins.then_inc(S("item_edges"), 1)
            pe.wait_ge(S("items_ready"), 1)
            hop(0, mix2, "L0", EARLY, SUB0, AT["L0"][1])
            hop(1)
            hop(2)

            with pe.Fori(0, NB) as i:
                after(pe, "gate_in", i + 1)
                transposes(a5, "gate_tr")
                after(pe, "gate_aT", i + 1)
                after(pe, "gate_out", i + 1)
                project(mats["L0_gate"], lambda s: bank(3)[0:TP, s * E0:(s + 1) * E0], E0, "gate_logits")
            pe.wait_ge(S("choices"), 1)
            T.matmul(bank(0)[0:TP, 0:400], lower[0:TP, 0:TP], cs[2], start=True, stop=True)
            T.matmul(bank(1)[:, 0:400], ones[0:TP, :], cs[2], start=True, stop=True).then_inc(S("ranks"), 1)
            with pe.Fori(0, MB // BS) as i:
                for s in range(BS):
                    after(pe, f"expert_in{s}", i * 48 + 48)
                    for k in range(2):
                        ins = T.transpose(bank(2 * s)[:, k * P:(k + 1) * P], xblk(s)[:, k * P:(k + 1) * P], ident[:, :])
                    ins.then_inc(S("slots_tr"), 1)
                for s in range(BS):
                    after(pe, "slots_T", i * BS + (s + 1))
                    for f in range(4):
                        for k in range(2):
                            ins = T.matmul(bank(2 * s + 1)[:, f * P:(f + 1) * P], wexp[:, s, k * F + f * P:k * F + (f + 1) * P],
                                           xTb[:, s, k, :], start=(k == 0), stop=(k == 1))
                    ins.then_inc(S("slots_hp"), 1)
                for s in range(BS):
                    after(pe, "slots_h", i * BS + (s + 1))
                    for f in range(4):
                        ins = T.matmul(bank(2 * s)[:, 2 * P:4 * P], hTb[:, s, f, :], wexp[:, s, 2 * F + f * D:2 * F + (f + 1) * D],
                                       start=(f == 0), stop=(f == 3))
                    ins.then_inc(S("slots_yp"), 1)

            pe.wait_ge(S("L1_weights"), 16 * 10)
            pe.wait_ge(S("normed"), 3 * NB)
            for h in range(3, 5):
                if h == 3:
                    hop(h, mix1, "L1", 0, SUB1, AT["keys"][1])
                else:
                    pe.wait_ge(S("m2_kvbd"), 2)
                    hop(h, mix2, "L1", 0, SUB1, AT["L1"][1])
                p, o = "gnn", (h - 3) * NB
                with pe.Fori(0, NB) as i:
                    after(pe, p + "_in", i + (o + 1))
                    transposes(a5, p + "_tr")
                    after(pe, p + "_aT", i + (o + 1))
                    project(mats[f"L1_gnn_w{h - 3}"], lambda s: halves(3)[:, s, :], D, p + "_lin")

            pe.wait_ge(S("normed"), 4 * NB)
            T.matmul(bank(0)[:, 0:D], ones[0:TP, :], XN[:, 0, :], start=True, stop=False)
            with pe.Fori(1, NT - 1) as t:
                T.matmul(bank(0)[:, 0:D], ones[0:TP, :], XN[:, bass.ds(t, 1), :].rearrange("p a f -> p (a f)"), start=False, stop=False)
            T.matmul(bank(0)[:, 0:D], ones[0:TP, :], XN[:, NT - 1, :], start=False, stop=True).then_inc(S("mean_sum"), 1)
            pe.wait_ge(S("mean"), 1)
            for k in range(2):
                ins = T.transpose(bank(1)[:, k * P:(k + 1) * P], batch["b"][:, k * P:(k + 1) * P], ident[:, :])
            ins.then_inc(S("mean_tr"), 1)
            pe.wait_ge(S("mean_T"), 1)
            mT = aT[:, :, :, :].rearrange("p k s c -> p (k s c)")
            for k in range(2):
                ins = T.matmul(bank(2)[:, 0:E1], mT[:, k * P:(k + 1) * P], mats["L1_wr"][:, k, :], start=(k == 0), stop=(k == 1))
            ins.then_inc(S("route_logits"), 1)
            pe.wait_ge(S("L1_experts_in"), 64)
            with pe.Fori(0, NB) as i:
                after(pe, "ff_in", i + 1)
                after(pe, "ff_used", i * 2 + 1)
                transposes(a5, "ff_tr")
                after(pe, "ff_aT", i + 1)
                for j in range(2):
                    if j == 1:
                        after(pe, "ff_used", i * 2 + 2)
                    for f in range(4):
                        project_T(wexp[:, j, 0:2 * F].rearrange("p (k f) -> p k f", k=2), f, aT, 8 * f, "ff_hp")
                    after(pe, "ff_h", i * 8 + 4 * (j + 1))
                    for s in range(BT):
                        second(lambda f: wexp[:, j, 2 * F + f * D:2 * F + (f + 1) * D], 4, s, "ff_y" if s == BT - 1 else None)

        @block.vector
        def _(dve):
            V = nc.vector
            ch = Chain(dve, S("dve_chain"), S("spare"))
            link = ch.link

            def ln(*args, **kw):
                for _ in ln_steps(*args, **kw):
                    pass

            def ln_steps(p, i, src, dst, done=None, affine=None):
                for s in range(BT):
                    ins = V.bn_stats(stats[:, s, :], src(s))
                link(ins)
                for s in range(BT):
                    ins = V.bn_aggr(mv[:, s, :], stats[:, s, :])
                ins.then_inc(S(p + "_var"), 1)
                yield
                after(dve, p + "_std", i + 1)
                link(V.reciprocal(rstd[:, :], std[:, :]))
                for s in range(BT):
                    ins = V.tensor_scalar(dst(s), src(s), mv[:, s, 0:1], rstd[:, s:s + 1], ALU.subtract, ALU.mult)
                if affine:
                    link(ins)
                    whole = affine[2]
                    link(V.tensor_tensor(whole, whole, rowbc(affine[0]), ALU.mult))
                    ins = V.tensor_tensor(whole, whole, rowbc(affine[1]), ALU.add)
                if done:
                    ins.then_inc(S(done), 1)
                else:
                    link(ins)

            def one(t, i, s):
                return t[:, bass.ds(i * BT + s, 1), :].rearrange("p a f -> p (a f)")

            def norm_pass(k):
                with dve.Fori(0, NB) as i:
                    ch.enter(i, 2)
                    ln("norm", i + k * NB, lambda s: one(X, i, s), lambda s: one(XN, i, s), done="normed")
                ch.leave(NB)

            def add_out(i, src, name):
                V.tensor_tensor(tiles(X, i), tiles(X, i), src, ALU.add).then_inc(S(name), 1)

            def mix1(L, i):
                i1 = i + (1 if L == "L0" else NB + 1)
                after(dve, "m1_kv", i1)
                vin = upper.rearrange("p s (h f) -> p s h f", h=2)
                if L == "L0":
                    bkv = rows["L0_mix_bkv"][0:TP, :]
                    for k in range(2):
                        V.tensor_tensor(v5[:, :, k, 0:P], vin[:, :, k, :], over(bkv[:, D + k * P:D + (k + 1) * P], BT), ALU.add)
                    link(V.tensor_tensor(k5, halves(0), over(bkv[:, 0:D], BT), ALU.add))
                else:
                    V.tensor_copy(v5[:, :, :, 0:P], vin)
                    link(V.tensor_copy(k5, halves(0)))
                V.tensor_scalar(b5, k5, 0.0, None, ALU.min).then_inc(S("m1_min"), 1)
                yield
                after(dve, "m1_exp", i1)
                V.scalar_tensor_tensor(out=b5, in0=k5, scalar=0.0, in1=r5, op0=ALU.max, op1=ALU.add).then_inc(S("m1_phi"), 1)
                yield
                after(dve, "m1_kvp", i1)
                V.tensor_tensor(kvacc[:, :], kvacc[:, :], bank(0)[:, 0:2 * (P + 1)], ALU.add).then_inc(S("m1_added"), 1)
                yield

            def before_keys(L):
                link(V.memset(kvacc[:, :], 0.0))
                link(V.memset(v5[:, :, :, P:P + 1], 1.0))
                if L == "L0":
                    dve.sem_inc(S("m1_added"), 1)

            def after_keys(L):
                dve.wait_ge(S("m1_added"), (1 if L == "L0" else 2) * NB + 1)
                link(V.memset(kvbd[:, :, :], 0.0))
                ka = kvacc[:, :].rearrange("p (k c) -> p k c", k=2)
                for j in range(4):
                    q = slice(32 * j, 32 * j + 32)
                    V.tensor_copy(kvbd[q, :, q], ka[q, :, q])
                    ins = V.tensor_copy(kvbd[q, :, P + j:P + j + 1], ka[q, :, P:P + 1])
                ins.then_inc(S("m2_kvbd"), 1)
                if L == "L0":
                    dve.sem_inc(S("m2_out"), 1)

            def mix2(L, i):
                i1 = i + (1 if L == "L0" else NB + 1)
                after(dve, "m2_relu", i1)
                for k in range(2):
                    if L == "L0":
                        ins = V.tensor_scalar(bT[:, k, :, :], strips[:, k, :, :], cols[:, k:k + 1], 0.0, ALU.add, ALU.min)
                    else:
                        ins = V.tensor_scalar(bT[:, k, :, :], strips[:, k, :, :], 0.0, None, ALU.min)
                ins.then_inc(S("m2_min"), 1)
                yield
                after(dve, "m2_exp", i1)
                V.tensor_tensor(pT[:, :, :, :], pT[:, :, :, :], bT, ALU.add).then_inc(S("m2_phi"), 1)
                yield
                after(dve, "m2_num", i1)
                link(V.tensor_scalar(zt[:, :, :, :], dens, 1e-6, None, ALU.add))
                link(V.reciprocal(zt[:, :, :, :], zt[:, :, :, :]))
                for k in range(2):
                    ins = V.tensor_tensor(r5[:, :, k * P:(k + 1) * P].rearrange("p s (h c) -> p s h c", h=4),
                                          upper[:, :, k * P:(k + 1) * P].rearrange("p s (h c) -> p s h c", h=4),
                                          zt[:, :, k, :].unsqueeze(3).broadcast_to([TP, BT, 4, 32]), ALU.mult)
                if L == "L0":
                    ins.then_inc(S("m2_t"), 1)
                    yield
                    after(dve, "m2_o", i1)
                    link(V.tensor_tensor(r5, upper, rowbc("L0_mix_bo"), ALU.add))
                else:
                    link(ins)
                    yield
                link(V.tensor_tensor(r5, r5, a5, ALU.add))
                yield from ln_steps("m2a", i1 - 1, lambda s: r5[:, s, :], lambda s: b5[:, s, :], done="m2_x1",
                                    affine=(L + "_mix_ln1_g", L + "_mix_ln1_b", b5))
                yield
                after(dve, "m2_y", i1)
                link(V.tensor_tensor(r5, halves(0), rowbc(L + "_mix_b2"), ALU.add))
                link(V.tensor_tensor(r5, r5, b5, ALU.add))
                yield from ln_steps("m2b", i1 - 1, lambda s: r5[:, s, :], lambda s: a5[:, s, :],
                                    affine=(L + "_mix_ln2_g", L + "_mix_ln2_b", a5))
                add_out(i, a5, "m2_out")
                yield

            def alone(step, per, L, start, end):
                with dve.Fori(start, end) as i:
                    ch.enter(i - start, per)
                    for _ in step(L, i):
                        pass
                ch.leave(end - start)

            def hop(h, step=None, per=0, L=None, b0=NB, sub=1, at=()):
                w = D + 1 if h == 3 else D

                in_bank = 1 if h == 3 else 2

                def maps(c0, buf):
                    if h < 3:
                        for j in range(HM):
                            c = bass.ds(c0 + j, 1)
                            ins = V.tensor_scalar(M8[:, buf, j, :], iota_j[:, 0:TP], DLOC[:, c], WI[:, c], ALU.is_equal, ALU.mult)
                    else:
                        ins = V.tensor_tensor(M8[:, buf, :, :], iota_j[:, 0:TP].unsqueeze(1).broadcast_to([P, HM, TP]),
                                              DLOC[:, bass.ds(c0, HM)].unsqueeze(2).broadcast_to([P, HM, TP]), ALU.is_equal)
                    ins.then_inc(S("edge_maps"), 1)

                def add(i, j, t):
                    n0 = (i + h * HI) * HU
                    if j % in_bank == 0:
                        after(dve, "item_sums", n0 + (HU + j + in_bank))
                    after(dve, "added", n0 + (2 * HB + j))
                    dst = ACC[:, bass.ds(t, 1), 0:w].rearrange("p a f -> p (a f)")
                    q = (j // in_bank) % HB * 512 + HB0 * 512 + j % in_bank * D
                    V.tensor_tensor(dst, dst, ps[0:TP, q:q + w], ALU.add).then_inc(S("added"), 1)

                def items(i, q0, steps):
                    for m in range(HU // HM):
                        _, group = nc.values_load_multi_w_load_instructions(
                            tile_i[0:1, bass.ds(i * HU + m * HM, HM)], engines=[mybir.EngineType.DVE], min_val=0, max_val=NT - 1,
                            skip_runtime_bounds_check_because="tile_i is clamped to NT - 1 where it is made")
                        after(dve, "item_sums", (i + h * HI) * HU + (HU + m * HM))
                        maps(i * HU + (m + 1) * HM, (m + 1) % 2)
                        for j in range(m * HM, (m + 1) * HM):
                            add(i, j, group[j - m * HM])
                            for _ in range(at.count(q0 + j)):
                                next(steps)

                dve.wait_ge(S("item_sums"), h * ITEMS + HU)
                if h:
                    dve.wait_ge(S("edge_maps"), h * MAPS)
                maps(0, 0)
                if b0 < NB:
                    with dve.Fori(b0, NB) as b:
                        ch.enter(b - b0, per)
                        steps = step(L, b)
                        for u in range(sub):
                            items((b - b0) * sub + u, u * HU, steps)
                        assert next(steps, "end") == "end"
                    ch.leave(NB - b0)
                at = ()
                if (NB - b0) * sub < HI:
                    with dve.Fori((NB - b0) * sub, HI) as i:
                        items(i, 0, None)

            dve.wait_ge(S("constants"), NCONST)
            dve.wait_ge(S("edges_in"), 48)
            V.memset(one_row, 1.0)
            src_f, dst_f = record[:, :, 1], record[:, :, 0]
            V.tensor_copy(dst_f, edge_in[1].bitcast(I32))
            V.tensor_copy(record[:, :, 2], edge_in[2])
            V.memset(record[:, :, 3], 0.0)
            link(V.tensor_copy(src_f, edge_in[0].bitcast(I32)))
            link(V.tensor_scalar(tid, src_f, -(TP // 2) * 1.0, 1.0 / TP, ALU.add, ALU.mult))
            link(V.tensor_scalar(tid, tid, 12582912.0, None, ALU.add))
            link(V.tensor_scalar(tid, tid, 12582912.0, None, ALU.subtract))
            for t in range(NT):
                ins = V.tensor_scalar(in_tile[:, t, :], tid, float(t), 0.0, ALU.is_equal, ALU.add, accum_out=tiny[:, 0, t:t + 1])
            link(ins)
            dve.sem_inc(S("tile_counts"), 1)
            dve.wait_ge(S("tile_ranks"), 1)
            tI = tiny.bitcast(I32)
            row = lambda k: tiny[:, k, :]
            incl = small_keep[:, :]
            link(V.tensor_scalar(row(1), bank(1)[:, 0:NT], float(P - 1), None, ALU.add))
            link(V.tensor_copy(tI[:, 2, :], row(1)))
            link(V.tensor_scalar(tI[:, 3, :], tI[:, 2, :], 7, None, ALU.arith_shift_right))
            link(V.tensor_copy(row(4), tI[:, 3, :]))
            link(V.tensor_tensor_scan(incl, ones[:, 0:NT], row(4), 0.0, ALU.mult, ALU.add))
            link(V.tensor_tensor(row(5), incl, row(4), ALU.subtract))
            link(V.tensor_scalar(row(6), row(5), float(P), -1.0, ALU.mult, ALU.add))
            link(V.tensor_tensor(row(7), row(6), bank(0)[:, 0:NT], ALU.add))
            link(V.tensor_scalar(slot, tid, float(NT) - 0.5, float(2 * ITEMS * P), ALU.is_gt, ALU.mult))
            for t in range(NT):
                link(V.tensor_tensor_scan(slot_t, one_row, in_tile[:, t, :], tiny[:, 7, t:t + 1], ALU.mult, ALU.add))
                link(V.tensor_tensor(masked, slot_t, in_tile[:, t, :], ALU.mult))
                link(V.tensor_tensor(slot, slot, masked, ALU.add))
            link(V.tensor_copy(slot_i, slot))
            dve.sem_inc(S("slots_of_edges"), 1)
            dve.wait_ge(S("x_in"), 16)
            dve.wait_ge(S("L0_weights"), 16 * 9)
            norm_pass(0)
            before_keys("L0")
            alone(mix1, 1, "L0", 0, NB)
            after_keys("L0")
            alone(mix2, 15, "L0", 0, EARLY)
            dve.wait_ge(S("item_numbers"), 1)
            link(V.memset(tile_of, 0.0))
            for t in range(NT):
                link(V.scalar_tensor_tensor(out=tile_of, in0=item_i, scalar=incl[:, t:t + 1], in1=tile_of, op0=ALU.is_ge, op1=ALU.add))
            V.tensor_scalar(tile_i[:, :], tile_of, float(NT - 1), None, ALU.min)
            dve.wait_ge(S("item_edges"), 1)
            V.tensor_copy(SRCI[:, :], bank(1)[:, 0:ITEMS])
            V.memset(DLOC[:, ITEMS:ITEMS + HM], 0.0)
            V.memset(WI[:, ITEMS:ITEMS + HM], 0.0)
            V.scalar_tensor_tensor(out=DLOC[:, 0:ITEMS], in0=tile_of, scalar=-float(TP), in1=bank(2)[:, 0:ITEMS], op0=ALU.mult, op1=ALU.add)
            link(V.tensor_copy(WI[:, 0:ITEMS], bank(3)[:, 0:ITEMS]))
            dve.sem_inc(S("items_ready"), 1)

            dve.wait_ge(S("L0_support"), NB)
            dve.sem_inc(S("added"), 2 * HB)
            for h in range(3):
                dve.wait_ge(S("rows_out"), 16 * (h + 1))
                link(V.tensor_copy(ACC[:, :, 0:D], H))
                if h == 0:
                    hop(h, mix2, 15, "L0", EARLY, SUB0, AT["L0"][2])
                else:
                    hop(h)
            dve.wait_ge(S("m2_out"), NB + 1)
            dve.wait_ge(S("added"), 3 * ITEMS + 2 * HB)
            link(V.tensor_tensor(X[:, :, :], X[:, :, :], ACC[:, :, 0:D], ALU.add))
            link(V.tensor_tensor(X[:, :, :], X[:, :, :], rowbc("L0_gnn_bias", NT), ALU.add))

            norm_pass(1)
            dve.sem_inc(S("gate_out"), 1)
            with dve.Fori(0, NB) as i:
                ch.enter(i, 3)
                after(dve, "gate_logits", i + 1)
                link(V.tensor_tensor(lg5[:, :, :], bank(3)[0:TP, 0:BT * E0].rearrange("p (s e) -> p s e", s=BT),
                                     rowbc("L0_ffn_gate_b"), ALU.add))
                for s in range(BT):
                    ins = V.max(mx5[0:TP, s, :], lg5[:, s, :])
                link(ins)
                for s in range(BT):
                    ins = V.max_index(mi5[0:TP, s, :], mx5[0:TP, s, :], lg5[:, s, :])
                link(ins)
                for j in range(2):
                    V.tensor_copy(top_v[:, j, bass.ds(i * BT, BT)], mx5[0:TP, :, j])
                    ins = V.tensor_copy(top_e[:, j, bass.ds(i * BT, BT)], mi5[0:TP, :, j])
                ins.then_inc(S("gate_out"), 1)
            ch.leave(NB)
            dve.wait_ge(S("gate_out"), NB + 1)
            V.tensor_tensor(gate[:, 0, :], top_v[:, 1, :], top_v[:, 0, :], ALU.subtract).then_inc(S("gate_diff"), 1)
            et = lambda k: cs[k].rearrange("p (e t) -> p e t", e=E0)
            expert = iota_j[0:TP, 0:E0].unsqueeze(2).broadcast_to([TP, E0, NT])
            for j in range(2):
                ins = V.tensor_tensor(et(j), expert, top_e[:, j, :].unsqueeze(1).broadcast_to([TP, E0, NT]), ALU.is_equal)
            link(ins)
            V.memset(cs[3], 1.0)
            link(V.tensor_tensor(cs[2], cs[0], cs[1], ALU.add))
            dve.sem_inc(S("choices"), 1)
            link(V.memset(et(3)[:, :, 0:1], 0.0))
            dve.wait_ge(S("gate_exp"), 1)
            link(V.tensor_scalar(rdeg[:, :], gate[:, 1, :], 1.0, None, ALU.add))
            link(V.reciprocal(gate[:, 0, :], rdeg[:, :]))
            link(V.tensor_tensor(gate[:, 1, :], gate[:, 1, :], gate[:, 0, :], ALU.mult))
            dve.wait_ge(S("ranks"), 1)
            link(V.tensor_copy(cs[4], bank(1)[0:TP, 0:400]))
            link(V.tensor_tensor_scan(cs[5], cs[3], cs[4], 0.0, ALU.mult, ALU.add))
            link(V.tensor_tensor(cs[6], cs[5], cs[4], ALU.subtract))
            sm = lambda k: small[0:TP, k, :]
            smi = small.bitcast(I32)
            link(V.tensor_scalar(sm(0), et(5)[:, :, NT - 1], 127.0, None, ALU.add))
            link(V.tensor_copy(smi[0:TP, 1, :], sm(0)))
            link(V.tensor_scalar(smi[0:TP, 2, :], smi[0:TP, 1, :], 7, None, ALU.arith_shift_right))
            link(V.tensor_copy(sm(3), smi[0:TP, 2, :]))
            link(V.tensor_tensor_scan(sm(4), ones[0:TP, 0:E0], sm(3), 0.0, ALU.mult, ALU.add))
            link(V.tensor_tensor(sm(5), sm(4), sm(3), ALU.subtract))
            link(V.tensor_scalar(sm(6), sm(5), float(P), None, ALU.mult))
            link(V.tensor_tensor(cs[7], cs[6], bank(0)[0:TP, 0:400], ALU.add))
            link(V.tensor_tensor(et(7), et(7), sm(6).unsqueeze(2).broadcast_to([TP, E0, NT]), ALU.add))
            for j in range(2):
                link(V.tensor_tensor(cs[8], cs[j], cs[7], ALU.mult))
                link(V.tensor_reduce(rdeg[:, :], et(8).rearrange("p e t -> p t e"), AX.X, ALU.add))
                link(V.tensor_copy(pos[:, j, :], rdeg[:, :]))
            blk = cs[8][:, 0:MB]
            link(V.memset(blk, 0.0))
            for e in range(E0 - 1):
                link(V.scalar_tensor_tensor(out=blk, in0=iota_j[0:TP, 0:MB], scalar=sm(4)[:, e:e + 1], in1=blk, op0=ALU.is_ge, op1=ALU.add))
            link(V.tensor_copy(block_e[0:TP, :], blk))
            dve.sem_inc(S("slot_tables"), 1)
            for s in range(BS):
                dve.sem_inc(S(f"block_y{s}"), 1)
            with dve.Fori(0, MB // BS) as i:
                for s in range(BS):
                    after(dve, "slots_yp", i * BS + (s + 1))
                    after(dve, f"block_stored{s}", i * 16 + 16)
                    V.tensor_tensor(yblk(s), bank(2 * s)[:, 2 * P:4 * P], b2b[:, s, :], ALU.add).then_inc(S(f"block_y{s}"), 1)
            dve.wait_ge(S("expert_rows"), 16 * 2 * NT)
            with dve.Fori(0, NB) as i:
                ch.enter(i, 8)

                def w5(j):
                    return gate[:, j, bass.ds(i * BT, BT)].unsqueeze(2).broadcast_to([TP, BT, D])

                V.tensor_tensor(r5, tiles(H, i), w5(0), ALU.mult)
                link(V.tensor_tensor(b5, tiles(ACC[:, :, 0:D], i), w5(1), ALU.mult))
                link(V.tensor_tensor(r5, r5, b5, ALU.add))
                link(V.tensor_tensor(r5, r5, tiles(XN, i), ALU.add))
                ln("norm", i + 2 * NB, lambda s: r5[:, s, :], lambda s: a5[:, s, :], affine=("L0_ffn_gamma", "L0_ffn_beta", a5))
                add_out(i, a5, "L0_ffn_out")
            ch.leave(NB)

            dve.wait_ge(S("L0_ffn_out"), NB)
            norm_pass(3)
            dve.wait_ge(S("L1_weights"), 16 * 10)
            before_keys("L1")
            for h in range(3, 5):
                p, o = "gnn", (h - 3) * NB
                dve.wait_ge(S("rows_out"), 16 * (h + 1))
                link(V.memset(g8[:, :, D:D + 1], 1.0))
                link(V.memset(ACC, 0.0))
                if h == 3:
                    hop(h, mix1, 1, "L1", 0, SUB1, AT["keys"][2])
                    after_keys("L1")
                else:
                    hop(h, mix2, 15, "L1", 0, SUB1, AT["L1"][2])
                dve.wait_ge(S("added"), (h + 1) * ITEMS + 2 * HB)
                if h == 3:
                    link(V.tensor_scalar(rdeg[:, :], ACC[:, :, D], 1.0, None, ALU.max))
                    link(V.reciprocal(rdeg[:, :], rdeg[:, :]))
                with dve.Fori(0, NB) as i:
                    ch.enter(i, 6)
                    link(V.tensor_tensor(r5, tiles(ACC[:, :, 0:D], i), rdeg[:, bass.ds(i * BT, BT)].unsqueeze(2).broadcast_to([TP, BT, D]), ALU.mult))
                    V.tensor_tensor(a5, r5, tiles(XN if h == 3 else H, i), ALU.add).then_inc(S(p + "_in"), 1)
                    after(dve, p + "_lin", i + (o + 1))
                    link(V.tensor_tensor(r5, halves(3), rowbc(f"L1_gnn_b{h - 3}"), ALU.add))
                    ln(p, i + o, lambda s: r5[:, s, :], lambda s: b5[:, s, :], done=p + "_pre",
                       affine=(f"L1_gnn_g{h - 3}", f"L1_gnn_beta{h - 3}", b5))
                    if h == 4:
                        after(dve, p + "_silu", i + 1)
                        add_out(i, r5, "L1_g1_out")
                        after(dve, "L1_g1_out", i + 1)
                ch.leave(NB)
            dve.wait_ge(S("L1_g1_out"), NB)

            norm_pass(4)
            dve.wait_ge(S("mean_sum"), 1)
            V.tensor_scalar(batch["b"][:, 0:D], bank(0)[:, 0:D], 1.0 / N, None, ALU.mult).then_inc(S("mean"), 1)
            R = lambda k: route[:, k, :]

            def softmax():
                link(V.max(mx5[:, 0, :], R(0)))
                V.tensor_scalar(route[:, 1, 0:1], mx5[:, 0, 0:1], -1.0, None, ALU.mult).then_inc(S("route_shift"), 1)

            dve.wait_ge(S("route_logits"), 1)
            link(V.tensor_tensor(R(0), bank(2)[:, 0:E1], rows["L1_ffn_br"], ALU.add))
            softmax()
            dve.wait_ge(S("route_exp"), 1)
            link(V.reciprocal(route[:, 5, 0:1], route[:, 3, 0:1]))
            link(V.tensor_scalar(R(4), R(2), route[:, 5, 0:1], None, ALU.mult))
            capacity = float(-(-N * 5 // (4 * E1)))
            link(V.tensor_scalar(R(6), R(4), float(N), None, ALU.mult))
            link(V.reciprocal(R(7), R(6)))
            link(V.tensor_scalar(R(8), R(7), capacity, 1.0, ALU.mult, ALU.min))
            link(V.tensor_tensor(R(0), R(4), R(8), ALU.mult))
            softmax()
            dve.wait_ge(S("route_exp"), 2)
            link(V.reciprocal(route[:, 5, 0:1], route[:, 3, 0:1]))
            link(V.tensor_scalar(R(4), R(2), route[:, 5, 0:1], None, ALU.mult))
            link(V.max(mx5[:, 0, :], R(4)))
            link(V.max_index(mi5[:, 0, :], mx5[:, 0, :], R(4)))
            dve.sem_inc(S("routed"), 1)
            V.tensor_tensor(route[:, 1, 0:1], mx5[:, 0, 1:2], mx5[:, 0, 0:1], ALU.subtract).then_inc(S("route_shift"), 1)
            dve.wait_ge(S("route_exp"), 3)
            link(V.tensor_scalar(route[:, 5, 0:1], route[:, 2, 0:1], 1.0, None, ALU.add))
            link(V.reciprocal(route[:, 9, 0:1], route[:, 5, 0:1]))
            link(V.tensor_tensor(route[:, 9, 1:2], route[:, 2, 0:1], route[:, 9, 0:1], ALU.mult))
            dve.wait_ge(S("L1_experts_in"), 64)
            link(V.tensor_scalar(b2x[:, 0, :], b2x[:, 0, :], route[:, 9, 0:1], None, ALU.mult))
            link(V.scalar_tensor_tensor(out=b2x[:, 0, :], in0=b2x[:, 1, :], scalar=route[:, 9, 1:2], in1=b2x[:, 0, :], op0=ALU.mult, op1=ALU.add))
            dve.sem_inc(S("ff_used"), 1)
            with dve.Fori(0, NB) as i:
                ch.enter(i, 6)
                after(dve, "ff_y", i * 2 + 1)
                V.scalar_tensor_tensor(out=r5, in0=halves(0), scalar=route[0:TP, 9, 0:1], in1=tiles(XN, i), op0=ALU.mult, op1=ALU.add).then_inc(S("ff_used"), 1)
                after(dve, "ff_y", i * 2 + 2)
                V.scalar_tensor_tensor(out=r5, in0=halves(0), scalar=route[0:TP, 9, 1:2], in1=r5, op0=ALU.mult, op1=ALU.add).then_inc(S("ff_used"), 1)
                after(dve, "ff_used", i * 2 + 3)
                link(V.tensor_tensor(r5, r5, over(b2x[0:TP, 0, :], BT), ALU.add))
                ln("ff", i, lambda s: r5[:, s, :], lambda s: b5[:, s, :], affine=("L1_ffn_gamma", "L1_ffn_beta", b5))
                add_out(i, b5, "L1_ffn_out")
            ch.leave(NB)


def kernel(**inputs):
    import numpy as np
    import concourse.bacc as bacc
    from concourse.bass_utils import run_bass_kernel_spmd as run

    v = {k: np.asarray(x) for k, x in inputs.items()}
    a = {"x": v["x"]}
    for name, fill in (("src", NOWHERE), ("dst", 0), ("edge_weight", 0)):
        pad = np.full(CH * P - EDGES, fill, v[name].dtype)
        a[name] = np.concatenate([v[name], pad]).reshape(P, CH)
    cat = np.concatenate
    a["L0_gnn_w"] = v["L0_gnn_weight"]
    a["L0_wq"], a["L0_wo"], a["L0_w1"], a["L0_w2"] = (v["L0_mix_" + n] for n in ("Wq", "Wo", "W1", "W2"))
    a["L0_wkv"] = cat([v["L0_mix_Wk"], v["L0_mix_Wv"]], axis=1)
    a["L0_gate"] = v["L0_ffn_gate_w"]
    a["L1_gnn_w0"], a["L1_gnn_w1"] = v["L1_gnn_W0"].T, v["L1_gnn_W1"].T
    qkv = v["L1_mix_Wqkv"].T
    a["L1_wq"], a["L1_wkv"] = qkv[:, 0:D], qkv[:, D:3 * D]
    a["L1_w1"], a["L1_w2"] = v["L1_mix_W1"].T, v["L1_mix_W2"].T
    a["L1_wr"] = v["L1_ffn_Wr"]
    v["L0_mix_bkv"] = cat([v["L0_mix_bk"], v["L0_mix_bv"]])
    for g, names in (("L0", ("L0_mix_bq", "L0_mix_b1")), ("L1", ("L1_mix_b1",))):
        c = [np.zeros((P, 2), np.float32)] * (g == "L1") + [v[n].reshape(-1, P).T for n in names]
        c = cat(c, axis=1)
        a[g + "_cols"] = cat([c, np.zeros((P, 16 - c.shape[1]), np.float32)], axis=1)
        a[g + "_rows"] = cat([v[r] for r in ROWS if r.startswith(g)])
    for g, w1, b1, w2, b2 in (("L0", "w1", "b1", "w2", "b2"), ("L1", "W1", "b1", "W2", "b2")):
        w1, b1, w2, b2 = (v[f"{g}_ffn_{n}"] for n in (w1, b1, w2, b2))
        e = w1.shape[0]
        a[g + "_experts"] = cat([w1.reshape(e, 2, P, F).transpose(0, 2, 1, 3).reshape(e, P, 2 * F),
                                 w2.reshape(e, 4, P, D).transpose(0, 2, 1, 3).reshape(e, P, 4 * D),
                                 b1.reshape(e, 4, P).transpose(0, 2, 1)], axis=2)
        a[g + "_b2"] = b2
    nc = bacc.Bacc("TRN2", target_bir_lowering=False, num_devices=1)
    arrays, aps = {}, {}
    for name, x in a.items():
        x = np.ascontiguousarray(x)
        arrays["in_" + name] = x
        aps[name] = nc.dram_tensor("in_" + name, x.shape, mybir.dt.from_np(x.dtype), kind="ExternalInput").ap()
    out = nc.dram_tensor("out_0", (N, D), F32, kind="ExternalOutput").ap()
    program(nc, aps, out)
    return run(nc, [arrays], core_ids=[0]).results[0]["out_0"]
```

```python
from contextlib import ExitStack

import concourse.bass as bass
from concourse import mybir

F32 = mybir.dt.float32
I32 = mybir.dt.int32
U32 = mybir.dt.uint32
ALU = mybir.AluOpType
ACT = mybir.ActivationFunctionType
AX = mybir.AxisListType

N = 3125
D = 256
TP = 125
NT = N // TP
BT = 5
NB = NT // BT
EDGES = 53125
P = 128
FIRST = 64
CH = 416
ITEMS = 441
GR, GC = 4, 111
RB = GR * GC
HU = 18
HG = 9
HM = 3
SR = 8
HB, HB0 = 3, 5
HI = ITEMS // HU
TAIL = ITEMS - HI * HU
GROUPS = ITEMS // HG
MAPS = ITEMS // HM + 2
E0, E1, F = 16, 8, 512
BS = 4
MB = 64
NOWHERE = 4000
EXP = 2 * F + 4 * D + 4
EPS = 1e-5


ROWS = ["L0_gnn_bias", "L0_mix_bkv", "L0_mix_bo", "L0_mix_b2", "L0_mix_ln1_g", "L0_mix_ln1_b", "L0_mix_ln2_g",
        "L0_mix_ln2_b", "L0_ffn_gate_b", "L0_ffn_gamma", "L0_ffn_beta", "L1_gnn_b0", "L1_gnn_g0", "L1_gnn_beta0",
        "L1_gnn_b1", "L1_gnn_g1", "L1_gnn_beta1", "L1_mix_ln1_g", "L1_mix_ln1_b", "L1_mix_b2", "L1_mix_ln2_g",
        "L1_mix_ln2_b", "L1_ffn_br", "L1_ffn_gamma", "L1_ffn_beta"]
ROW_LEN = {"L0_mix_bkv": 512, "L0_ffn_gate_b": E0, "L1_ffn_br": E1}
MATS = {"L0_gnn_w": D, "L0_wq": D, "L0_wkv": 2 * D, "L0_wo": D, "L0_w1": 1024, "L0_gate": E0,
        "L1_gnn_w0": D, "L1_gnn_w1": D, "L1_wq": D, "L1_wkv": 2 * D, "L1_w1": D, "L1_w2": D, "L1_wr": E1}


def beside(steps, at):
    k, due = 0, None
    q = yield
    while True:
        if q >= due if due is not None else k < len(at) and q >= at[k]:
            k += due is None
            due = q + 1 if next(steps) == "more" else None
        q = yield


class Chain:

    def __init__(self, eng, sem, spare):
        self.eng, self.sem, self.spare, self.base, self.k, self.i, self.per = eng, sem, spare, 0, 0, None, 0

    def enter(self, i, per):
        self.i, self.per, self.k = i, per, 0

    def leave(self, times):
        assert self.k == self.per, (self.k, self.per)
        self.base, self.i, self.k = self.base + self.per * times, None, 0

    def link(self, ins):
        ins.then_inc(self.sem, 1)
        self.k += 1
        if self.i is None:
            self.base, self.k = self.base + 1, 0
            self.eng.wait_ge(self.sem, self.base)
        else:
            self.eng.wait_ge(self.sem, self.i * self.per + (self.base + self.k))
            self.eng.sem_inc(self.spare, 1)


def program(nc, a, out):
    with ExitStack() as ctx:
        def sb(name, shape, dt=F32):
            return ctx.enter_context(nc.sbuf_tensor(name, shape, dt))

        sems = {}

        def S(name):
            if name not in sems:
                sems[name] = ctx.enter_context(nc.semaphore(name))
            return sems[name]

        def dram(name, shape, dt=F32):
            return nc.dram_tensor(name, shape, dt, kind="Internal").ap()

        def after(eng, name, val):
            eng.wait_ge(S(name), val)
            if not isinstance(val, int):
                eng.sem_inc(S("spare"), 1)

        X = sb("X", [TP, NT, D])
        XN = sb("XN", [TP, NT, D])
        big = sb("big", [P, NT * D + NT * (D + 1)])
        H = big[0:TP, 0:NT * D].rearrange("p (t f) -> p t f", t=NT)
        ACC = big[0:TP, NT * D:].rearrange("p (t f) -> p t f", t=NT)
        wexp = big[:, 0:BS * EXP].rearrange("p (s f) -> p s f", s=BS)
        batch = {n: sb(n, [P, BT * D]) for n in ("a", "b", "r")}
        a5, b5, r5 = (batch[n][0:TP, :].rearrange("p (s f) -> p s f", s=BT) for n in ("a", "b", "r"))
        bT = batch["b"][:, 0:2 * BT * TP].rearrange("p (k s c) -> p k s c", k=2, s=BT)
        aT = sb("aT", [P, 2, BT, TP])
        pT = sb("pT", [P, 2, BT, TP])
        hid = sb("hid", [P, 8 * BT * TP])
        hT = hid[:, :].rearrange("p (f s c) -> p f s c", f=8, s=BT)
        k5 = hid[0:TP, 0:BT * D].rearrange("p (s f) -> p s f", s=BT)
        v5 = hid[0:TP, BT * D:BT * D + BT * 2 * (P + 1)].rearrange("p (s h f) -> p s h f", s=BT, h=2)
        xTb = hid[:, 0:BS * 2 * P].rearrange("p (s k c) -> p s k c", s=BS, k=2)
        hTb = hid[:, BS * 2 * P:BS * 6 * P].rearrange("p (s f c) -> p s f c", s=BS, f=4)
        stats = sb("stats", [TP, BT, 6])
        mv = sb("mv", [TP, BT, 2])
        std = sb("std", [TP, BT])
        rstd = sb("rstd", [TP, BT])
        zt = sb("zt", [TP, BT, 2, 4])
        kvacc = sb("kvacc", [P, 2 * (P + 1)])
        kvbd = sb("kvbd", [P, 2, P + 4])
        mats = {n: sb("w_" + n, [P, 2, c])[:, :, :] for n, c in MATS.items() if n.startswith("L0")}
        for mine, other, c0 in (("L1_gnn_w0", "L0_gnn_w", 0), ("L1_gnn_w1", "L0_wo", 0), ("L1_wq", "L0_wq", 0),
                                ("L1_wkv", "L0_wkv", 0), ("L1_wr", "L0_gate", 0), ("L1_w1", "L0_w1", 0),
                                ("L1_w2", "L0_w1", D)):
            mats[mine] = mats[other][:, :, c0:c0 + MATS[mine]]
        w2_0 = sb("w2_0", [P, 8, D])
        rows, at = {}, {"L0": 0, "L1": 0}
        total = {g: sum(ROW_LEN.get(r, D) for r in ROWS if r.startswith(g)) for g in at}
        row_store = sb("row_store", [P, total["L0"]])
        gnn1 = [r for r in ROWS if r.startswith("L1_gnn")]
        at["L1"] = -len(gnn1) * D
        for r in ROWS:
            g, n = r[:2], ROW_LEN.get(r, D)
            rows[r] = row_store[:, at[g]:at[g] + n] if at[g] >= 0 else \
                w2_0[:, :, :].rearrange("p a b -> p (a b)")[:, at[g] + len(gnn1) * D:][:, 0:n]
            at[g] += n
        cols = sb("cols", [P, 16])
        ident = sb("ident", [P, P])
        ones = sb("ones", [P, P])
        lower = sb("lower", [P, P])
        iota_j = sb("iota_j", [P, P])
        eps = sb("eps", [P, 1])
        ix = sb("ix", [P, HU // HG, HG], I32)
        ixs = sb("ixs", [P, 2, SR], I32)
        g8 = sb("g8", [P, HG, D + 1])
        M8 = sb("M8", [P, 2, HM, TP])
        SRCI = sb("SRCI", [P, ITEMS], I32)
        DLOC = sb("DLOC", [P, ITEMS + 2 * HM])
        WI = sb("WI", [P, ITEMS + 2 * HM])
        tile_i = sb("tile_i", [P, ITEMS], I32)
        rdeg = sb("rdeg", [TP, NT])
        lg5 = sb("lg5", [TP, BT, E0])
        mx5 = sb("mx5", [P, BT, 8])
        mi5 = sb("mi5", [P, BT, 8], U32)
        top_v = sb("top_v", [TP, 2, NT])
        top_e = sb("top_e", [TP, 2, NT])
        gate = sb("gate", [TP, 2, NT])
        pos = sb("pos", [TP, 2, NT], I32)
        block_e = sb("block_e", [P, MB], I32)
        route = sb("route", [P, 12, 8])
        b2x = M8[:, :, :, :].rearrange("p c a b -> p (c a b)")[:, 0:2 * D].rearrange("p (s f) -> p s f", s=2)
        b2b = batch["b"][:, 0:BS * D].rearrange("p (s f) -> p s f", s=BS)

        def maps_at(h, k):
            if k < 2:
                return M8[:, k, :, :]
            spare_w = mats["L0_gnn_w"].rearrange("p k f -> p (k f)") if h < 3 else \
                w2_0[:, :, :].rearrange("p a b -> p (a b)")[:, len(gnn1) * D:]
            return spare_w[:, 0:HM * TP].rearrange("p (j c) -> p j c", j=HM)

        def scratch(k, n, width, rows_=P):
            return big[0:rows_, k:k + n * width]

        in_tile = scratch(0, NT, CH).rearrange("p (t c) -> p t c", t=NT)
        edge_in = batch["a"][:, 0:CH], batch["b"][:, 0:CH], batch["r"][:, 0:CH]
        tid, slot, slot_t = (batch[n][:, CH:2 * CH] for n in ("a", "b", "r"))
        at_acc = NT * D
        record = scratch(NT * CH, 4, CH).rearrange("p (c r) -> p c r", r=4)
        slot_i = scratch((NT + 4) * CH, 1, CH).bitcast(I32)
        tiny = scratch((NT + 5) * CH, 12, NT).rearrange("p (k t) -> p k t", k=12)
        tile_of, item_i = WI[:, 0:ITEMS], DLOC[:, 0:ITEMS]
        records_n = scratch(at_acc + 1024, GR, 4 * P, GC).rearrange("q (g e r) -> q g e r", g=GR, r=4)
        record_stage = g8[:, HG // 2, 0:8 * SR].rearrange("p (h c r) -> p h c r", h=2, r=4)
        small_keep = route[:, :, :].rearrange("p a b -> p (a b)")[:, 0:NT]
        one_row = pT[:, :, :, :].rearrange("p k s c -> p (k s c)")[:, 0:CH]
        unused = g8[:, HG - 1, 0:4 * 12]
        cs = [scratch(400 * k, 1, 400, TP) for k in range(10)]
        small = scratch(4096, 12, E0).rearrange("p (k e) -> p k e", k=12)

        PS = ctx.enter_context(nc.psum_tensor("PS", [P, 8 * 512], F32))
        ps = PS[:, :]

        def bank(b, n=1):
            return ps[:, b * 512:(b + n) * 512]

        strips = ps[:, 0:10 * P].rearrange("p (k s c) -> p k s c", k=2, s=BT)[:, :, :, 0:TP]

        def halves(b):
            return ps[0:TP, b * 512:b * 512 + BT * D].rearrange("p (s f) -> p s f", s=BT)

        def pair(j):
            return ps[:, j * 1024:j * 1024 + BT * P].rearrange("p (s c) -> p s c", s=BT)[:, :, 0:TP]

        def pair_at(strip):
            return ps[:, strip * P:(strip + BT) * P].rearrange("p (s c) -> p s c", s=BT)[:, :, 0:TP]

        upper = ps[0:TP, BT * D:2 * BT * D].rearrange("p (s f) -> p s f", s=BT)
        dens = ps[0:TP, 0:BT * 8].rearrange("p (s k c) -> p s k c", s=BT, k=2)

        def xblk(s):
            return g8[:, 2 * s, 0:D]

        def yblk(s):
            return g8[:, 2 * s + 1, 0:D]

        Sd = dram("gather_rows", [N, D])
        Rd = dram("edge_records", [RB * P, 4])
        Xs = dram("slot_rows", [MB * P, D])
        Ys = dram("slot_results", [MB * P, D])

        def over(r, n):
            return r.unsqueeze(1).broadcast_to([TP, n, r.shape[1]])

        def rowbc(name, n=BT):
            return over(rows[name][0:TP, :], n)

        def tiles(t, i):
            return t[:, bass.ds(i * BT, BT), :]

        def rows_stored(h):
            return 16 * (h + 1 if h < 3 else 3 + NB * (h - 2))

        FN = {"L0": 8, "L1": 2}
        NCONST = 10
        EARLY = 2
        SUB0, SUB1 = HI // (NB - EARLY), HI // NB

        AT = {
            "keys": ([0, 12, 31], [1, 6, 31], [18, 24, 36]),
            "L0": ([9, 10, 18, 19, 45, 63, 72, 81, 82, 83, 90, 91, 92, 99, 100, 135],
                   [2, 6, 20, 34, 39, 62] + [68 + 7 * f // 2 for f in range(8)] + [96, 102, 108, 114, 120],
                   [9, 13, 26, 46, 52, 126, 134]),
            "L1": ([9, 10, 18, 19, 36, 45, 46, 54, 63],
                   [2, 6, 19, 35, 38, 41, 45, 47, 49, 51, 53],
                   [9, 13, 24, 26, 28, 53, 58]),
        }
        block = ctx.enter_context(nc.Block())

        @block.sync
        def _(sp):
            for dst, src in zip(edge_in, ("src", "dst", "edge_weight")):
                sp.dma_start(dst if src == "edge_weight" else dst.bitcast(I32), a[src]).then_inc(S("edges_in"), 16)
            sp.dma_start(X[:, :, :], a["x"].rearrange("(t p) f -> p t f", p=TP)).then_inc(S("x_in"), 16)

            def load_layer(g):
                for m in MATS:
                    if m.startswith(g):
                        sp.dma_start(mats[m], a[m].rearrange("(k p) f -> p k f", p=P)).then_inc(S(g + "_weights"), 16)
                lo = len(gnn1) * D if g == "L1" else 0
                if lo:
                    sp.dma_start(w2_0[:, :, :].rearrange("p a b -> p (a b)")[:, 0:lo],
                                 a["L1_rows"][0:lo].partition_broadcast(P)).then_inc(S("L1_weights"), 16)
                else:
                    sp.dma_start(w2_0[:, :, :], a["L0_w2"].rearrange("(k p) f -> p k f", p=P)).then_inc(S("L0_weights"), 16)
                sp.dma_start(row_store[:, 0:total[g] - lo], a[g + "_rows"][lo:total[g]].partition_broadcast(P)).then_inc(S(g + "_weights"), 16)
                sp.dma_start(cols[:, :], a[g + "_cols"]).then_inc(S(g + "_weights"), 16)

            load_layer("L0")
            after(sp, "constants", NCONST)
            sp.dma_start(Rd.rearrange("(p k i) r -> p k (i r)", p=P, i=12),
                         unused[:, :].unsqueeze(1).broadcast_to([P, RB // 12, 48])).then_inc(S("records_clear"), 16)
            after(sp, "slots_of_edges", 1)

            def stage(i, half):
                c = bass.ds((2 * i + half) * SR, SR)
                sp.dma_start(ixs[:, half, :], slot_i[:, c]).then_inc(S(f"records_staged{half}"), 16)
                sp.dma_start(record_stage[:, half, :, :].rearrange("p c r -> p (c r)"),
                             record[:, c, :].rearrange("p c r -> p (c r)")).then_inc(S(f"records_staged{half}"), 16)

            for half in range(2):
                stage(0, half)
            first = FIRST // (2 * SR)
            for k, (lo, hi) in enumerate(((1, first), (first, CH // (2 * SR)))):
                after(sp, "slots_of_edges", k + 1)
                with sp.Fori(lo, hi) as i:
                    for half in range(2):
                        after(sp, f"records_sent{half}", i * (16 * SR))
                        stage(i, half)
            zero_rows = Xs.rearrange("(p k r) f -> p k (r f)", p=P, k=16)
            sp.dma_start(zero_rows, g8[:, :, :].rearrange("p a b -> p (a b)")[:, 0:1024].unsqueeze(1).broadcast_to([P, 16, 1024])).then_inc(S("slots_clear"), 16)

            def store_rows(rows_, wait, val):
                after(sp, wait, val)
                sp.dma_start(Sd.rearrange("(t p) f -> p t f", p=TP), rows_).then_inc(S("rows_out"), 16)

            def store_batches(rows_, wait, val):
                for b in range(NB):
                    after(sp, wait, val + b)
                    sp.dma_start(Sd.rearrange("(t p) f -> p t f", p=TP)[:, b * BT:(b + 1) * BT, :],
                                 rows_[:, b * BT:(b + 1) * BT, :]).then_inc(S("rows_out"), 16)

            store_rows(H, "L0_support", NB)
            for h in range(2):
                store_rows(ACC[:, :, 0:D], "added", ITEMS * (h + 1) + 2 * HB)

            after(sp, "slots_filled", 16 * 2 * NT)
            with sp.Fori(0, MB // BS) as i:
                for s in range(BS):
                    after(sp, f"block_y{s}", i + 1)
                    b = i * BS + s
                    sp.dma_start(xblk(s), Xs[bass.ds(b * P, P), :]).then_inc(S(f"block_in{s}"), 16)
                    e = sp.value_load(block_e[0:1, bass.ds(b, 1)], min_val=0, max_val=E0 - 1)
                    sp.dma_start(wexp[:, s, :], a["L0_experts"][bass.ds(e, 1), :, :].rearrange("a p f -> (a p) f")).then_inc(S(f"expert_in{s}"), 16)
                    sp.dma_start(b2b[:, s, :], a["L0_b2"][bass.ds(e, 1), :].rearrange("a f -> (a f)").partition_broadcast(P)).then_inc(S(f"expert_in{s}"), 16)

            after(sp, "L0_ffn_out", NB)
            store_batches(XN[:, :, :], "normed", 2 * NB + 1)
            load_layer("L1")
            store_batches(H, "L1_g0_out", 2)
            after(sp, "routed", 1)
            for j in range(2):
                e = sp.value_load(mi5[0:1, 0, j:j + 1].bitcast(I32), min_val=0, max_val=E1 - 1)
                sp.dma_start(wexp[:, j, :], a["L1_experts"][bass.ds(e, 1), :, :].rearrange("a p f -> (a p) f")).then_inc(S("L1_experts_in"), 16)
                sp.dma_start(b2x[:, j, :], a["L1_b2"][bass.ds(e, 1), :].rearrange("a f -> (a f)").partition_broadcast(P)).then_inc(S("L1_experts_in"), 16)
            after(sp, "L1_ffn_out", NB)
            sp.dma_start(out.rearrange("(t p) f -> p t f", p=TP), X[:, :, :]).then_inc(S("result_out"), 16)
            sp.wait_ge(S("result_out"), 16)

        @block.gpsimd
        def _(pool):
            g = nc.gpsimd
            g.memset(ident[:, :], 0.0).then_inc(S("constants"), 1)
            g.memset(ones[:, :], 1.0).then_inc(S("constants"), 1)
            g.memset(lower[:, :], 1.0).then_inc(S("constants"), 1)
            g.memset(eps[:, :], EPS).then_inc(S("constants"), 1)
            g.memset(g8[:, :, :], 0.0).then_inc(S("constants"), 1)
            g.iota(item_i, [[1, ITEMS]], base=0, channel_multiplier=0, allow_small_or_imprecise_dtypes=True).then_inc(S("constants"), 1)
            g.iota(iota_j[:, :], [[1, P]], base=0, channel_multiplier=0, allow_small_or_imprecise_dtypes=True).then_inc(S("constants"), 1)
            pool.wait_ge(S("constants"), 7)
            g.affine_select(out=ident[:, :], in_=ident[:, :], compare_op=ALU.not_equal, fill=1.0, base=0,
                            pattern=[[-1, P]], channel_multiplier=1).then_inc(S("constants"), 1)
            g.affine_select(out=lower[:, :], in_=lower[:, :], compare_op=ALU.is_gt, fill=0.0, base=0,
                            pattern=[[1, P]], channel_multiplier=-1).then_inc(S("constants"), 1)
            g.memset(unused[:, :].rearrange("p (i r) -> p i r", r=4)[:, :, 1], float(NOWHERE)).then_inc(S("constants"), 1)

            pool.wait_ge(S("records_clear"), 16)
            with pool.Fori(0, CH // (2 * SR)) as i:
                for half in range(2):
                    after(pool, f"records_staged{half}", i * 32 + 32)
                    for j in range(SR):
                        g.indirect_dma_start(Rd, bass.IndirectOffsetOnAxis(ap=ixs[:, half, j:j + 1], axis=0), record_stage[:, half, j, :], None,
                                             bounds_check=ITEMS * P - 1, oob_is_err=False).then_inc(S(f"records_sent{half}"), 16)
            for half in range(2):
                pool.wait_ge(S(f"records_sent{half}"), 16 * (CH // 2))
            pool.dma_start(records_n.rearrange("q g e r -> q g (e r)"), Rd.rearrange("(g q e) r -> q g (e r)", g=GR, q=GC)).then_inc(S("records_in"), 16)

            def hop(h):
                pool.wait_ge(S("rows_out"), rows_stored(h))

                def gathers(i, n):
                    for j in range(n):
                        if j % HG == 0:
                            after(pool, "indices", i * (HU // HG) + (h * GROUPS + j // HG + 1))
                        if j % HM == 0:
                            after(pool, "item_sums", i * HU + (h * ITEMS + HU - HG + j + HM))
                        g.indirect_dma_start(g8[:, j % HG, 0:D], None, Sd, bass.IndirectOffsetOnAxis(
                            ap=ix[:, j // HG, j % HG:j % HG + 1], axis=0)).then_inc(S(f"gathered{j % HG}"), 16)

                with pool.Fori(0, HI) as i:
                    gathers(i, HU)
                gathers(HI, TAIL)

            pool.wait_ge(S("slots_clear"), 16)
            for k in range(HU // HG):
                pool.dma_start(g8[:, HG - 1, 0:D], a["x"][0:P, :]).then_inc(S(f"gathered{HG - 1}"), 16)
                pool.wait_ge(S(f"gathered{HG - 1}"), 16 * (k + 1))
            for h in range(3):
                hop(h)

            pool.wait_ge(S("slot_tables"), 1)
            for j in range(2):
                for t in range(NT):
                    g.indirect_dma_start(Xs, bass.IndirectOffsetOnAxis(ap=pos[:, j, t:t + 1], axis=0),
                                         XN[:, t, :], None).then_inc(S("slots_filled"), 16)
            for s in range(BS):
                pool.dma_start(Ys[s * P:(s + 1) * P, :], yblk(s)).then_inc(S(f"block_stored{s}"), 16)
            with pool.Fori(0, MB // BS) as i:
                for s in range(BS):
                    after(pool, f"block_y{s}", i + 2)
                    pool.dma_start(Ys[bass.ds((i * BS + s) * P, P), :], yblk(s)).then_inc(S(f"block_stored{s}"), 16)
            for s in range(BS):
                pool.wait_ge(S(f"block_stored{s}"), 16 * (MB // BS + 1))
            for t in range(NT):
                for j in range(2):
                    g.indirect_dma_start((H if j == 0 else ACC)[:, t, 0:D], None, Ys,
                                         bass.IndirectOffsetOnAxis(ap=pos[:, j, t:t + 1], axis=0)).then_inc(S(f"expert_rows{t // BT}"), 16)
            for h in range(3, 5):
                hop(h)

        @block.scalar
        def _(act):
            A = nc.scalar

            def ln_std(p, i):
                after(act, p + "_var", i + 1)
                A.activation(std[:, :], mv[:, :, 1], ACT.Sqrt, bias=eps[0:TP, :]).then_inc(S(p + "_std"), 1)

            def norm_pass(k):
                with act.Fori(0, NB) as i:
                    ln_std("norm", i + k * NB)

            def load_batch(i, name):
                A.activation(a5, tiles(XN, i), ACT.Copy).then_inc(S(name), 1)

            def transposed(p, i, frm, to):
                after(act, p + frm, i + 1)
                A.activation(aT[:, :, :, :], strips, ACT.Copy).then_inc(S(p + to), 1)

            def mix1(L, i):
                i1 = i + (1 if L == "L0" else NB + 1)
                load_batch(i, "m1_in")
                yield
                after(act, "m1_tr", i1)
                A.activation(aT[:, :, :, :], strips, ACT.Copy).then_inc(S("m1_aT"), 1)
                yield
                if L == "L0":
                    after(act, "m1_kv", i1)
                    A.activation(tiles(H, i), halves(5), ACT.Copy).then_inc(S("L0_support"), 1)
                after(act, "m1_min", i1)
                A.activation(r5, b5, ACT.Exp).then_inc(S("m1_exp"), 1)
                yield

            def mix2(L, i):
                i1 = i + (1 if L == "L0" else NB + 1)
                after(act, "m2_out", i1)
                load_batch(i, "m2_in")
                yield
                after(act, "m2_tr", i1)
                A.activation(aT[:, :, :, :], strips, ACT.Copy).then_inc(S("m2_aT"), 1)
                yield
                after(act, "m2_q", i1)
                for k in range(2):
                    if L == "L0":
                        ins = A.activation(pT[:, k, :, :], strips[:, k, :, :], ACT.Relu, bias=cols[:, k:k + 1])
                    else:
                        ins = A.activation(pT[:, k, :, :], strips[:, k, :, :], ACT.Relu)
                ins.then_inc(S("m2_relu"), 1)
                yield
                after(act, "m2_min", i1)
                A.activation(bT, bT, ACT.Exp).then_inc(S("m2_exp"), 1)
                yield
                if L == "L0":
                    after(act, "m2_ttr", i1)
                    A.activation(aT[:, :, :, :], strips, ACT.Copy).then_inc(S("m2_tT"), 1)
                    yield
                ln_std("m2a", i1 - 1)
                yield
                after(act, "m2_x1tr", i1)
                A.activation(aT[:, :, :, :], strips, ACT.Copy).then_inc(S("m2_x1T"), 1)
                yield
                fn, h0 = FN[L], (0 if L == "L0" else FN["L0"] * NB)
                for f in range(fn):
                    after(act, "m2_hp", i * fn + (h0 + f + 1))
                    A.activation(hT[:, f, :, :], pair(f % 2), ACT.Relu if L == "L0" else ACT.Gelu,
                                 bias=cols[:, 2 + f:3 + f]).then_inc(S("m2_h"), 1)
                    yield
                ln_std("m2b", i1 - 1)
                yield

            def alone(step, L, start, end):
                with act.Fori(start, end) as i:
                    for _ in step(L, i):
                        pass

            def hop(h, step=None, L=None, b0=NB, sub=1, at=()):
                def indices(i, n=HU):
                    for k in range(n // HG):
                        after(act, f"gathered{HG - 1}", i * (16 * HU // HG) + 16 * (h * GROUPS + k + 1))
                        A.activation(ix[:, k, :], SRCI[:, bass.ds(i * HU + HG * k, HG)], ACT.Copy).then_inc(S("indices"), 1)
                        yield k

                if h:
                    act.wait_ge(S(f"gathered{HG - 1}"), 16 * (h * GROUPS + HU // HG))
                if b0 < NB:
                    with act.Fori(b0, NB) as b:
                        steps = step(L, b)
                        turn = beside(steps, at)
                        next(turn)
                        for u in range(sub):
                            for k in indices((b - b0) * sub + u):
                                for q in range(u * HU + HG * k, u * HU + HG * (k + 1)):
                                    turn.send(q)
                        for _ in steps:
                            pass
                if (NB - b0) * sub < HI:
                    with act.Fori((NB - b0) * sub, HI) as i:
                        for _ in indices(i):
                            pass
                for _ in indices(HI, TAIL):
                    pass

            act.wait_ge(S("constants"), NCONST)
            act.wait_ge(S("L0_weights"), 16 * 9)
            norm_pass(0)
            act.wait_ge(S("normed"), 1 * NB)
            alone(mix1, "L0", 0, NB)
            alone(mix2, "L0", 0, EARLY)
            act.wait_ge(S("items_ready"), 1)
            hop(0, mix2, "L0", EARLY, SUB0, AT["L0"][0])
            hop(1)
            hop(2)

            ln_std("norm", NB)
            after(act, "normed", NB + 1)
            load_batch(0, "gate_in")
            with act.Fori(0, NB - 1) as i:
                ln_std("norm", i + (NB + 1))
                transposed("gate", i, "_tr", "_aT")
                after(act, "normed", i + (NB + 2))
                load_batch(i + 1, "gate_in")
            transposed("gate", NB - 1, "_tr", "_aT")
            act.wait_ge(S("gate_diff"), 1)
            A.activation(gate[:, 1, :], gate[:, 0, :], ACT.Exp).then_inc(S("gate_exp"), 1)

            def block_xT(i, s):
                after(act, "slots_tr", i * BS + (s + 1))
                A.activation(xTb[:, s, :, :], bank(2 * s)[:, 0:2 * P].rearrange("p (k c) -> p k c", k=2), ACT.Copy).then_inc(S("slots_T"), 1)

            def block_h(i, s):
                after(act, "slots_hp", i * BS + (s + 1))
                s %= BS
                for f in range(4):
                    ins = A.activation(hTb[:, s, f, :], bank(2 * s + 1)[:, f * P:(f + 1) * P], ACT.Relu,
                                       bias=wexp[:, s, EXP - 4 + f:EXP - 3 + f])
                ins.then_inc(S("slots_h"), 1)

            for s in range(BS):
                block_xT(0, s)
                if s >= 1:
                    block_h(0, s - 1)
            with act.Fori(1, MB // BS) as i:
                for s in range(BS):
                    block_xT(i, s)
                    block_h(i, s - 1)
            block_h(MB // BS, -1)
            norm_pass(2)

            norm_pass(3)
            act.wait_ge(S("normed"), 3 * NB)
            act.wait_ge(S("L1_weights"), 16 * 10)
            for h in range(3, 5):
                if h == 3:
                    hop(h, mix1, "L1", 0, SUB1, AT["keys"][0])
                else:
                    hop(h, mix2, "L1", 0, SUB1, AT["L1"][0])
                p, o = "gnn", (h - 3) * NB

                def gnn_silu(i, more):
                    if more:
                        transposed(p, i + (o + 1), "_tr", "_aT")
                    ln_std(p, i + o)
                    after(act, p + "_pre", i + (o + 1))
                    if h == 3:
                        A.activation(tiles(H, i), b5, ACT.Silu).then_inc(S("L1_g0_out"), 1)
                    else:
                        A.activation(r5, b5, ACT.Silu).then_inc(S(p + "_silu"), 1)
                        ln_std("norm", i + 4 * NB)

                transposed(p, o, "_tr", "_aT")
                with act.Fori(0, NB - 1) as i:
                    gnn_silu(i, True)
                gnn_silu(NB - 1, False)

            act.wait_ge(S("mean_tr"), 1)
            A.activation(aT[:, :, :, :].rearrange("p k s c -> p (k s c)")[:, 0:2 * P], bank(1)[:, 0:2 * P], ACT.Copy).then_inc(S("mean_T"), 1)
            for k in range(3):
                act.wait_ge(S("route_shift"), k + 1)
                if k < 2:
                    A.activation(route[:, 2, :], route[:, 0, :], ACT.Exp, bias=route[:, 1, 0:1], accum_out=route[:, 3, 0:1]).then_inc(S("route_exp"), 1)
                else:
                    A.activation(route[:, 2, 0:1], route[:, 1, 0:1], ACT.Exp).then_inc(S("route_exp"), 1)
            act.wait_ge(S("L1_experts_in"), 64)

            def ff_transposed(i):
                after(act, "ff_tr", i + 1)
                for k in range(2):
                    ins = A.activation(aT[:, k, :, :], pair_at(12 + 8 * k), ACT.Copy)
                ins.then_inc(S("ff_aT"), 1)

            def ff_hidden(i, first, last):
                if not last:
                    load_batch(i + 1, "ff_in")
                for c in range(8):
                    after(act, "ff_hp", i * 8 + (c + 1))
                    A.activation(hT[:, c, :, :], pair_at(12 + 8 * (c % 2)), ACT.Gelu,
                                 bias=wexp[:, c // 4, EXP - 4 + c % 4:EXP - 3 + c % 4]).then_inc(S("ff_h"), 1)
                    if c == 3 and not first:
                        ln_std("ff", i - 1)
                if not last:
                    ff_transposed(i + 1)

            load_batch(0, "ff_in")
            ff_transposed(0)
            ff_hidden(0, True, False)
            with act.Fori(1, NB - 1) as i:
                ff_hidden(i, False, False)
            ff_hidden(NB - 1, False, True)
            ln_std("ff", NB - 1)

        @block.tensor
        def _(pe):
            T = nc.tensor

            def transposes(src, name):
                for k in range(2):
                    for s in range(BT):
                        ins = T.transpose(strips[:, k, s, :], src[:, s, k * P:(k + 1) * P], ident[0:TP, 0:TP])
                ins.then_inc(S(name), 1)

            def project(*args):
                for _ in project_steps(*args):
                    pass

            def project_steps(w, out_, n, name):
                for s in range(BT):
                    for k in range(2):
                        ins = T.matmul(out_(s), aT[:, k, s, :], w[:, k, 0:n], start=(k == 0), stop=(k == 1))
                    if s < BT - 1:
                        yield "more"
                if name:
                    ins.then_inc(S(name), 1)

            def project_T(w, f, src, strip0, name):
                s = 0
                while s < BT:
                    c = strip0 + s
                    n = min(BT - s, 4 - c % 4)
                    dst = ps[:, c * P:(c + n) * P].rearrange("p (s c) -> p s c", s=n)[:, :, 0:TP]
                    for k in range(2):
                        ins = T.matmul(dst, w[:, k, f * P:(f + 1) * P], src[:, k, s:s + n, :], start=(k == 0), stop=(k == 1))
                    s += n
                if name:
                    ins.then_inc(S(name), 1)

            def second(w, fn, s, name):
                for f in range(fn):
                    ins = T.matmul(halves(0)[:, s, :], hT[:, f, s, :], w(f), start=(f == 0), stop=(f == fn - 1))
                if name:
                    ins.then_inc(S(name), 1)

            def mix1(L, i):
                i1 = i + (1 if L == "L0" else NB + 1)
                after(pe, "m1_in", i1)
                after(pe, "m1_added", i1)
                transposes(a5, "m1_tr")
                yield
                after(pe, "m1_aT", i1)
                if L == "L0":
                    yield from project_steps(mats["L0_gnn_w"], lambda s: halves(5)[:, s, :], D, None)
                yield from project_steps(mats[L + "_wkv"][:, :, 0:D], lambda s: halves(0)[:, s, :], D, None)
                yield "more"
                yield from project_steps(mats[L + "_wkv"][:, :, D:2 * D], lambda s: upper[:, s, :], D, "m1_kv")
                yield
                after(pe, "m1_phi", i1)
                for k in range(2):
                    for s in range(BT):
                        ins = T.matmul(bank(0)[:, k * (P + 1):(k + 1) * (P + 1)], b5[:, s, k * P:(k + 1) * P], v5[:, s, k, :],
                                       start=(s == 0), stop=(s == BT - 1))
                ins.then_inc(S("m1_kvp"), 1)
                yield

            def mix2(L, i):
                i1 = i + (1 if L == "L0" else NB + 1)
                after(pe, "m2_in", i1)
                transposes(a5, "m2_tr")
                yield
                after(pe, "m2_aT", i1)
                project_T(mats[L + "_wq"], 0, aT, 0, None)
                yield "more"
                project_T(mats[L + "_wq"], 1, aT, BT, "m2_q")
                yield
                after(pe, "m2_phi", i1)
                for s in range(BT):
                    for k in range(2):
                        T.matmul(upper[:, s, k * P:(k + 1) * P], pT[:, k, s, :], kvbd[:, k, 0:P], start=True, stop=True)
                        ins = T.matmul(dens[:, s, k, :], pT[:, k, s, :], kvbd[:, k, P:P + 4], start=True, stop=True)
                    if s < BT - 1:
                        yield "more"
                ins.then_inc(S("m2_num"), 1)
                yield
                if L == "L0":
                    after(pe, "m2_t", i1)
                    transposes(r5, "m2_ttr")
                    yield
                    after(pe, "m2_tT", i1)
                    yield from project_steps(mats["L0_wo"], lambda s: upper[:, s, :], D, "m2_o")
                    yield
                after(pe, "m2_x1", i1)
                transposes(b5, "m2_x1tr")
                yield
                after(pe, "m2_x1T", i1)
                fn, h0 = FN[L], (0 if L == "L0" else FN["L0"] * NB)
                for f in range(fn):
                    if f >= 2:
                        after(pe, "m2_h", i * fn + (h0 + f - 1))
                    project_T(mats[L + "_w1"], f, aT, 8 * (f % 2), "m2_hp")
                    yield
                after(pe, "m2_h", i * fn + (h0 + fn))
                for s in range(BT):
                    second((lambda f: w2_0[:, f, :]) if L == "L0" else (lambda f: mats["L1_w2"][:, f, :]), fn, s,
                           "m2_y" if s == BT - 1 else None)
                    yield

            def alone(step, L, start, end):
                with pe.Fori(start, end) as i:
                    for _ in step(L, i):
                        pass

            def hop(h, step=None, L=None, b0=NB, sub=1, at=()):
                n = D + 1 if h == 3 else D
                in_bank = 1 if h == 3 else 2

                def item(i, j):
                    n0 = i * HU + h * ITEMS
                    first = 16 * HU // HG if j % HG == HG - 1 else 0
                    after(pe, f"gathered{j % HG}", i * (16 * HU // HG) + (16 * (h * GROUPS + j // HG + 1) + first))
                    if j % HM == 0:
                        after(pe, "edge_maps", i * (HU // HM) + (h * MAPS + j // HM + 1))
                    if j % in_bank == 0:
                        after(pe, "added", n0 + (2 * HB - in_bank * HB + j + in_bank))
                    q = (j // in_bank) % HB * 512 + HB0 * 512 + j % in_bank * D
                    T.matmul(ps[0:TP, q:q + n], maps_at(h, j // HM % 3)[:, j % HM, :], g8[:, j % HG, 0:n], start=True, stop=True).then_inc(S("item_sums"), 1)

                if b0 < NB:
                    with pe.Fori(b0, NB) as b:
                        steps = step(L, b)
                        turn = beside(steps, at)
                        next(turn)
                        for q in range(sub * HU):
                            item((b - b0) * sub + q // HU, q % HU)
                            turn.send(q)
                        for _ in steps:
                            pass
                if (NB - b0) * sub < HI:
                    with pe.Fori((NB - b0) * sub, HI) as i:
                        for j in range(HU):
                            item(i, j)
                for j in range(TAIL):
                    item(HI, j)

            pe.wait_ge(S("constants"), NCONST)
            pe.wait_ge(S("tile_counts"), 1)
            T.matmul(bank(0)[:, 0:NT], lower[:, :], tiny[:, 0, :], start=True, stop=True)
            T.matmul(bank(1)[:, 0:NT], ones[:, :], tiny[:, 0, :], start=True, stop=True).then_inc(S("tile_ranks"), 1)
            pe.wait_ge(S("L0_weights"), 16 * 9)
            alone(mix1, "L0", 0, NB)
            pe.sem_inc(S("item_sums"), HU)
            pe.wait_ge(S("m2_kvbd"), 1)
            alone(mix2, "L0", 0, EARLY)
            pe.wait_ge(S("m2_out"), EARLY + 1)
            pe.wait_ge(S("records_in"), 16)
            for r in range(3):
                for g in range(GR):
                    ins = T.transpose(bank(1 + r)[:, g * GC:(g + 1) * GC], records_n[:, g, :, r], ident[0:GC, 0:GC])
            ins.then_inc(S("item_edges"), 1)
            pe.wait_ge(S("items_ready"), 1)
            hop(0, mix2, "L0", EARLY, SUB0, AT["L0"][1])
            hop(1)
            hop(2)

            with pe.Fori(0, NB) as i:
                after(pe, "gate_in", i + 1)
                transposes(a5, "gate_tr")
                after(pe, "gate_aT", i + 1)
                after(pe, "gate_out", i + 1)
                project(mats["L0_gate"], lambda s: bank(3)[0:TP, s * E0:(s + 1) * E0], E0, "gate_logits")
            pe.wait_ge(S("choices"), 1)
            T.matmul(bank(0)[0:TP, 0:400], lower[0:TP, 0:TP], cs[2], start=True, stop=True)
            T.matmul(bank(1)[:, 0:400], ones[0:TP, :], cs[2], start=True, stop=True).then_inc(S("ranks"), 1)
            def block_x(i, s):
                after(pe, f"block_in{s}", i * 16 + 16)
                for k in range(2):
                    ins = T.transpose(bank(2 * s)[:, k * P:(k + 1) * P], xblk(s)[:, k * P:(k + 1) * P], ident[:, :])
                ins.then_inc(S("slots_tr"), 1)

            def block_hidden(i, s):
                after(pe, "slots_T", i * BS + (s + 1))
                after(pe, f"expert_in{s % BS}", i * 32 + (32 if s >= 0 else 0))
                s %= BS
                for f in range(4):
                    for k in range(2):
                        ins = T.matmul(bank(2 * s + 1)[:, f * P:(f + 1) * P], wexp[:, s, k * F + f * P:k * F + (f + 1) * P],
                                       xTb[:, s, k, :], start=(k == 0), stop=(k == 1))
                ins.then_inc(S("slots_hp"), 1)

            def block_out(i, s):
                after(pe, "slots_h", i * BS + (s + 1))
                s %= BS
                for f in range(4):
                    ins = T.matmul(bank(2 * s)[:, 2 * P:4 * P], hTb[:, s, f, :], wexp[:, s, 2 * F + f * D:2 * F + (f + 1) * D],
                                   start=(f == 0), stop=(f == 3))
                ins.then_inc(S("slots_yp"), 1)

            for s in range(BS):
                block_x(0, s)
                if s >= 1:
                    block_hidden(0, s - 1)
                if s >= 2:
                    block_out(0, s - 2)
            with pe.Fori(1, MB // BS) as i:
                for s in range(BS):
                    block_x(i, s)
                    block_hidden(i, s - 1)
                    block_out(i, s - 2)
            block_hidden(MB // BS, -1)
            block_out(MB // BS, -2)
            block_out(MB // BS, -1)

            pe.wait_ge(S("L1_weights"), 16 * 10)
            pe.wait_ge(S("normed"), 3 * NB)
            for h in range(3, 5):
                if h == 3:
                    hop(h, mix1, "L1", 0, SUB1, AT["keys"][1])
                else:
                    pe.wait_ge(S("m2_kvbd"), 2)
                    hop(h, mix2, "L1", 0, SUB1, AT["L1"][1])
                p, o = "gnn", (h - 3) * NB
                with pe.Fori(0, NB) as i:
                    after(pe, p + "_in", i + (o + 1))
                    transposes(a5, p + "_tr")
                    after(pe, p + "_aT", i + (o + 1))
                    after(pe, "gnn_read", i + (o + 1))
                    project(mats[f"L1_gnn_w{h - 3}"], lambda s: halves(3)[:, s, :], D, p + "_lin")

            pe.wait_ge(S("normed"), 4 * NB)
            T.matmul(bank(0)[:, 0:D], ones[0:TP, :], XN[:, 0, :], start=True, stop=False)
            with pe.Fori(1, NT - 1) as t:
                T.matmul(bank(0)[:, 0:D], ones[0:TP, :], XN[:, bass.ds(t, 1), :].rearrange("p a f -> p (a f)"), start=False, stop=False)
            T.matmul(bank(0)[:, 0:D], ones[0:TP, :], XN[:, NT - 1, :], start=False, stop=True).then_inc(S("mean_sum"), 1)
            pe.wait_ge(S("mean"), 1)
            for k in range(2):
                ins = T.transpose(bank(1)[:, k * P:(k + 1) * P], batch["b"][:, k * P:(k + 1) * P], ident[:, :])
            ins.then_inc(S("mean_tr"), 1)
            pe.wait_ge(S("mean_T"), 1)
            mT = aT[:, :, :, :].rearrange("p k s c -> p (k s c)")
            for k in range(2):
                ins = T.matmul(bank(2)[:, 0:E1], mT[:, k * P:(k + 1) * P], mats["L1_wr"][:, k, :], start=(k == 0), stop=(k == 1))
            ins.then_inc(S("route_logits"), 1)
            pe.wait_ge(S("L1_experts_in"), 64)

            def ff_transposes(i):
                after(pe, "ff_in", i + 1)
                for k in range(2):
                    for s in range(BT):
                        ins = T.transpose(pair_at(12 + 8 * k)[:, s, :], a5[:, s, k * P:(k + 1) * P], ident[0:TP, 0:TP])
                ins.then_inc(S("ff_tr"), 1)

            def ff_hidden(i, c):
                if c >= 2:
                    after(pe, "ff_h", i * 8 + (c - 1))
                project_T(wexp[:, c // 4, 0:2 * F].rearrange("p (k f) -> p k f", k=2), c % 4, aT, 12 + 8 * (c % 2), "ff_hp")

            def ff_second(i, j):
                after(pe, "ff_h", i * 8 + 4 * (j + 1))
                after(pe, "ff_used", i * 2 + (j + 1))
                for s in range(BT):
                    for f in range(4):
                        ins = T.matmul(halves(0)[:, s, :], hT[:, 4 * j + f, s, :], wexp[:, j, 2 * F + f * D:2 * F + (f + 1) * D],
                                       start=(f == 0), stop=(f == 3))
                ins.then_inc(S("ff_y"), 1)

            def ff_batch(i, last):
                after(pe, "ff_aT", i + 1)
                for c in range(6):
                    ff_hidden(i, c)
                ff_second(i, 0)
                ff_hidden(i, 6)
                ff_hidden(i, 7)
                if not last:
                    after(pe, "ff_h", i * 8 + 8)
                    ff_transposes(i + 1)
                ff_second(i, 1)

            ff_transposes(0)
            with pe.Fori(0, NB - 1) as i:
                ff_batch(i, False)
            ff_batch(NB - 1, True)

        @block.vector
        def _(dve):
            V = nc.vector
            ch = Chain(dve, S("dve_chain"), S("spare"))
            link = ch.link

            def ln(*args, **kw):
                for _ in ln_steps(*args, **kw):
                    pass

            def ln_steps(p, i, src, dst, done=None, affine=None):
                for s in range(BT):
                    ins = V.bn_stats(stats[:, s, :], src(s))
                link(ins)
                for s in range(BT):
                    ins = V.bn_aggr(mv[:, s, :], stats[:, s, :])
                ins.then_inc(S(p + "_var"), 1)
                yield
                if affine:
                    gain, offset = (rows[affine[k]][0:TP, :] for k in range(2))
                    after(dve, p + "_var", i + 1)
                    for s in range(BT):
                        ins = V.scalar_tensor_tensor(out=dst(s), in0=src(s), scalar=mv[:, s, 0:1], in1=gain, op0=ALU.subtract, op1=ALU.mult)
                    link(ins)
                    yield "more"
                after(dve, p + "_std", i + 1)
                link(V.reciprocal(rstd[:, :], std[:, :]))
                for s in range(BT):
                    if affine:
                        ins = V.scalar_tensor_tensor(out=dst(s), in0=dst(s), scalar=rstd[:, s:s + 1], in1=offset, op0=ALU.mult, op1=ALU.add)
                    else:
                        ins = V.tensor_scalar(dst(s), src(s), mv[:, s, 0:1], rstd[:, s:s + 1], ALU.subtract, ALU.mult)
                if done:
                    ins.then_inc(S(done), 1)
                else:
                    link(ins)

            def one(t, i, s):
                return t[:, bass.ds(i * BT + s, 1), :].rearrange("p a f -> p (a f)")

            def norm_pass(k):
                with dve.Fori(0, NB) as i:
                    ch.enter(i, 2)
                    ln("norm", i + k * NB, lambda s: one(X, i, s), lambda s: one(XN, i, s), done="normed")
                ch.leave(NB)

            def add_out(i, src, name):
                V.tensor_tensor(tiles(X, i), tiles(X, i), src, ALU.add).then_inc(S(name), 1)

            def mix1(L, i):
                i1 = i + (1 if L == "L0" else NB + 1)
                after(dve, "m1_kv", i1)
                vin = upper.rearrange("p s (h f) -> p s h f", h=2)
                if L == "L0":
                    bkv = rows["L0_mix_bkv"][0:TP, :]
                    for k in range(2):
                        V.tensor_tensor(v5[:, :, k, 0:P], vin[:, :, k, :], over(bkv[:, D + k * P:D + (k + 1) * P], BT), ALU.add)
                    link(V.tensor_tensor(k5, halves(0), over(bkv[:, 0:D], BT), ALU.add))
                else:
                    V.tensor_copy(v5[:, :, :, 0:P], vin)
                    link(V.tensor_copy(k5, halves(0)))
                V.tensor_scalar(b5, k5, 0.0, None, ALU.min).then_inc(S("m1_min"), 1)
                yield
                after(dve, "m1_exp", i1)
                V.scalar_tensor_tensor(out=b5, in0=k5, scalar=0.0, in1=r5, op0=ALU.max, op1=ALU.add).then_inc(S("m1_phi"), 1)
                yield
                after(dve, "m1_kvp", i1)
                V.tensor_tensor(kvacc[:, :], kvacc[:, :], bank(0)[:, 0:2 * (P + 1)], ALU.add).then_inc(S("m1_added"), 1)
                yield

            def before_keys(L):
                link(V.memset(kvacc[:, :], 0.0))
                link(V.memset(v5[:, :, :, P:P + 1], 1.0))
                if L == "L0":
                    dve.sem_inc(S("m1_added"), 1)

            def after_keys(L):
                dve.wait_ge(S("m1_added"), (1 if L == "L0" else 2) * NB + 1)
                link(V.memset(kvbd[:, :, :], 0.0))
                ka = kvacc[:, :].rearrange("p (k c) -> p k c", k=2)
                for j in range(4):
                    q = slice(32 * j, 32 * j + 32)
                    V.tensor_copy(kvbd[q, :, q], ka[q, :, q])
                    ins = V.tensor_copy(kvbd[q, :, P + j:P + j + 1], ka[q, :, P:P + 1])
                ins.then_inc(S("m2_kvbd"), 1)
                if L == "L0":
                    dve.sem_inc(S("m2_out"), 1)

            def mix2(L, i):
                i1 = i + (1 if L == "L0" else NB + 1)
                after(dve, "m2_relu", i1)
                for k in range(2):
                    if L == "L0":
                        ins = V.tensor_scalar(bT[:, k, :, :], strips[:, k, :, :], cols[:, k:k + 1], 0.0, ALU.add, ALU.min)
                    else:
                        ins = V.tensor_scalar(bT[:, k, :, :], strips[:, k, :, :], 0.0, None, ALU.min)
                ins.then_inc(S("m2_min"), 1)
                yield
                after(dve, "m2_exp", i1)
                V.tensor_tensor(pT[:, :, :, :], pT[:, :, :, :], bT, ALU.add).then_inc(S("m2_phi"), 1)
                yield
                after(dve, "m2_num", i1)
                link(V.tensor_scalar(zt[:, :, :, :], dens, 1e-6, None, ALU.add))
                link(V.reciprocal(zt[:, :, :, :], zt[:, :, :, :]))
                for k in range(2):
                    ins = V.tensor_tensor(r5[:, :, k * P:(k + 1) * P].rearrange("p s (h c) -> p s h c", h=4),
                                          upper[:, :, k * P:(k + 1) * P].rearrange("p s (h c) -> p s h c", h=4),
                                          zt[:, :, k, :].unsqueeze(3).broadcast_to([TP, BT, 4, 32]), ALU.mult)
                if L == "L0":
                    ins.then_inc(S("m2_t"), 1)
                    yield
                    after(dve, "m2_o", i1)
                    link(V.tensor_tensor(r5, upper, rowbc("L0_mix_bo"), ALU.add))
                    yield "more"
                else:
                    link(ins)
                    yield
                link(V.tensor_tensor(r5, r5, a5, ALU.add))
                yield "more"
                yield from ln_steps("m2a", i1 - 1, lambda s: r5[:, s, :], lambda s: b5[:, s, :], done="m2_x1",
                                    affine=(L + "_mix_ln1_g", L + "_mix_ln1_b"))
                yield
                after(dve, "m2_y", i1)
                link(V.tensor_tensor(r5, halves(0), rowbc(L + "_mix_b2"), ALU.add))
                yield "more"
                link(V.tensor_tensor(r5, r5, b5, ALU.add))
                yield "more"
                yield from ln_steps("m2b", i1 - 1, lambda s: r5[:, s, :], lambda s: a5[:, s, :],
                                    affine=(L + "_mix_ln2_g", L + "_mix_ln2_b"))
                yield "more"
                add_out(i, a5, "m2_out")
                yield

            def alone(step, per, L, start, end):
                with dve.Fori(start, end) as i:
                    ch.enter(i - start, per)
                    for _ in step(L, i):
                        pass
                ch.leave(end - start)

            def hop(h, step=None, per=0, L=None, b0=NB, sub=1, at=()):
                w = D + 1 if h == 3 else D

                in_bank = 1 if h == 3 else 2

                def map_part(c0, buf, j):
                    m8 = maps_at(h, buf)
                    if h < 3:
                        c = bass.ds(c0 + j, 1)
                        ins = V.tensor_scalar(m8[:, j, :], iota_j[:, 0:TP], DLOC[:, c], WI[:, c], ALU.is_equal, ALU.mult)
                    elif j == HM - 1:
                        ins = V.tensor_tensor(m8, iota_j[:, 0:TP].unsqueeze(1).broadcast_to([P, HM, TP]),
                                              DLOC[:, bass.ds(c0, HM)].unsqueeze(2).broadcast_to([P, HM, TP]), ALU.is_equal)
                    if j == HM - 1:
                        ins.then_inc(S("edge_maps"), 1)

                def add(i, j, t, n):
                    n0 = i * HU + h * ITEMS
                    if j % in_bank == 0:
                        after(dve, "item_sums", n0 + (HU + min(j + in_bank, n)))
                    after(dve, "added", n0 + (2 * HB + j))
                    dst = ACC[:, bass.ds(t, 1), 0:w].rearrange("p a f -> p (a f)")
                    q = (j // in_bank) % HB * 512 + HB0 * 512 + j % in_bank * D
                    V.tensor_tensor(dst, dst, ps[0:TP, q:q + w], ALU.add).then_inc(S("added"), 1)

                def items(i, q0=0, turn=None, n=HU):
                    for m in range(n // HM):
                        if m * HM % HG == 0:
                            _, tile_of_item = nc.values_load_multi_w_load_instructions(
                                tile_i[0:1, bass.ds(i * HU + m * HM, HG)], engines=[mybir.EngineType.DVE], min_val=0, max_val=NT - 1,
                                skip_runtime_bounds_check_because="tile_i is clamped to NT - 1 where it is made")
                        for j in range(m * HM, (m + 1) * HM):
                            add(i, j, tile_of_item[j % HG], n)
                            if j % HM == 0:
                                after(dve, "item_sums", i * HU + (h * ITEMS + HU + m * HM))
                            map_part(i * HU + (m + 2) * HM, (m + 2) % 3, j % HM)
                            if turn:
                                turn.send(q0 + j)

                dve.wait_ge(S("item_sums"), h * ITEMS + HU)
                if h:
                    dve.wait_ge(S("edge_maps"), h * MAPS)
                for k in range(2):
                    for j in range(HM):
                        map_part(k * HM, k, j)
                if b0 < NB:
                    with dve.Fori(b0, NB) as b:
                        ch.enter(b - b0, per)
                        steps = step(L, b)
                        turn = beside(steps, at)
                        next(turn)
                        for u in range(sub):
                            items((b - b0) * sub + u, u * HU, turn)
                        for _ in steps:
                            pass
                    ch.leave(NB - b0)
                if (NB - b0) * sub < HI:
                    with dve.Fori((NB - b0) * sub, HI) as i:
                        items(i)
                items(HI, n=TAIL)

            dve.wait_ge(S("constants"), NCONST)
            dve.wait_ge(S("edges_in"), 48)
            V.memset(one_row, 1.0)
            src_f, dst_f = record[:, :, 1], record[:, :, 0]
            V.tensor_copy(dst_f, edge_in[1].bitcast(I32))
            V.tensor_copy(record[:, :, 2], edge_in[2])
            V.memset(record[:, :, 3], 0.0)
            link(V.tensor_copy(src_f, edge_in[0].bitcast(I32)))
            link(V.tensor_scalar(tid, src_f, -(TP // 2) * 1.0, 1.0 / TP, ALU.add, ALU.mult))
            link(V.tensor_scalar(tid, tid, 12582912.0, None, ALU.add))
            link(V.tensor_scalar(tid, tid, 12582912.0, None, ALU.subtract))
            parts = (0, FIRST), (FIRST, CH)
            for k, (c0, c1) in enumerate(parts):
                for t in range(NT):
                    ins = V.tensor_scalar(in_tile[:, t, c0:c1], tid[:, c0:c1], float(t), 0.0, ALU.is_equal, ALU.add,
                                          accum_out=tiny[:, 9 + k, t:t + 1])
            link(ins)
            link(V.tensor_tensor(tiny[:, 0, :], tiny[:, 9, :], tiny[:, 10, :], ALU.add))
            dve.sem_inc(S("tile_counts"), 1)
            dve.wait_ge(S("tile_ranks"), 1)
            tI = tiny.bitcast(I32)
            row = lambda k: tiny[:, k, :]
            incl = small_keep[:, :]
            link(V.tensor_scalar(row(1), bank(1)[:, 0:NT], float(P - 1), None, ALU.add))
            link(V.tensor_copy(tI[:, 2, :], row(1)))
            link(V.tensor_scalar(tI[:, 3, :], tI[:, 2, :], 7, None, ALU.arith_shift_right))
            link(V.tensor_copy(row(4), tI[:, 3, :]))
            link(V.tensor_tensor_scan(incl, ones[:, 0:NT], row(4), 0.0, ALU.mult, ALU.add))
            link(V.tensor_tensor(row(5), incl, row(4), ALU.subtract))
            link(V.tensor_scalar(row(6), row(5), float(P), -1.0, ALU.mult, ALU.add))
            link(V.tensor_tensor(row(7), row(6), bank(0)[:, 0:NT], ALU.add))
            link(V.tensor_scalar(slot, tid, float(NT) - 0.5, float(2 * ITEMS * P), ALU.is_gt, ALU.mult))
            link(V.tensor_tensor(row(8), row(7), row(9), ALU.add))
            for k, (c0, c1) in enumerate(parts):
                for t in range(NT):
                    inside = in_tile[:, t, c0:c1]
                    link(V.tensor_tensor_scan(slot_t[:, c0:c1], one_row[:, c0:c1], inside, tiny[:, 7 + k, t:t + 1], ALU.mult, ALU.add))
                    link(V.copy_predicated(slot[:, c0:c1], inside.bitcast(U32), slot_t[:, c0:c1]))
                link(V.tensor_copy(slot_i[:, c0:c1], slot[:, c0:c1]))
                dve.sem_inc(S("slots_of_edges"), 1)
            link(V.memset(tile_of, 0.0))
            for t in range(NT):
                link(V.scalar_tensor_tensor(out=tile_of, in0=item_i, scalar=incl[:, t:t + 1], in1=tile_of, op0=ALU.is_ge, op1=ALU.add))
            link(V.tensor_scalar(tile_i[:, :], tile_of, float(NT - 1), None, ALU.min))

            dve.wait_ge(S("x_in"), 16)
            dve.wait_ge(S("L0_weights"), 16 * 9)
            norm_pass(0)
            before_keys("L0")
            alone(mix1, 1, "L0", 0, NB)
            after_keys("L0")
            link(V.tensor_tensor(X[:, :, :], X[:, :, :], rowbc("L0_gnn_bias", NT), ALU.add))
            alone(mix2, 13, "L0", 0, EARLY)
            dve.wait_ge(S("item_edges"), 1)
            V.tensor_copy(SRCI[:, :], bank(1)[:, 0:ITEMS])
            V.memset(DLOC[:, ITEMS:ITEMS + 2 * HM], 0.0)
            V.memset(WI[:, ITEMS:ITEMS + 2 * HM], 0.0)
            link(V.scalar_tensor_tensor(out=DLOC[:, 0:ITEMS], in0=tile_of, scalar=-float(TP), in1=bank(2)[:, 0:ITEMS], op0=ALU.mult, op1=ALU.add))
            link(V.tensor_copy(WI[:, 0:ITEMS], bank(3)[:, 0:ITEMS]))
            dve.sem_inc(S("items_ready"), 1)

            dve.wait_ge(S("L0_support"), NB)
            dve.sem_inc(S("added"), 2 * HB)
            for h in range(3):
                if h:
                    dve.wait_ge(S("rows_out"), rows_stored(h))
                link(V.tensor_copy(ACC[:, :, 0:D], H))
                if h == 0:
                    hop(h, mix2, 13, "L0", EARLY, SUB0, AT["L0"][2])
                else:
                    hop(h)
            dve.wait_ge(S("m2_out"), NB + 1)
            dve.wait_ge(S("added"), 3 * ITEMS + 2 * HB)

            def sum_and_norm(i):
                link(V.tensor_tensor(tiles(X, i), tiles(X, i), tiles(ACC[:, :, 0:D], i), ALU.add))
                ln("norm", i + NB, lambda s: one(X, i, s), lambda s: one(XN, i, s), done="normed")

            def choose(i):
                after(dve, "gate_logits", i + 1)
                link(V.tensor_tensor(lg5[:, :, :], bank(3)[0:TP, 0:BT * E0].rearrange("p (s e) -> p s e", s=BT),
                                     rowbc("L0_ffn_gate_b"), ALU.add))
                for s in range(BT):
                    ins = V.max(mx5[0:TP, s, :], lg5[:, s, :])
                link(ins)
                for s in range(BT):
                    ins = V.max_index(mi5[0:TP, s, :], mx5[0:TP, s, :], lg5[:, s, :])
                link(ins)
                for j in range(2):
                    V.tensor_copy(top_v[:, j, bass.ds(i * BT, BT)], mx5[0:TP, :, j])
                    ins = V.tensor_copy(top_e[:, j, bass.ds(i * BT, BT)], mi5[0:TP, :, j])
                ins.then_inc(S("gate_out"), 1)

            dve.sem_inc(S("gate_out"), 1)
            sum_and_norm(0)
            with dve.Fori(0, NB - 1) as i:
                ch.enter(i, 6)
                sum_and_norm(i + 1)
                choose(i)
            ch.leave(NB - 1)
            choose(NB - 1)
            dve.wait_ge(S("gate_out"), NB + 1)
            V.tensor_tensor(gate[:, 0, :], top_v[:, 1, :], top_v[:, 0, :], ALU.subtract).then_inc(S("gate_diff"), 1)
            et = lambda k: cs[k].rearrange("p (e t) -> p e t", e=E0)
            expert = iota_j[0:TP, 0:E0].unsqueeze(2).broadcast_to([TP, E0, NT])
            for j in range(2):
                ins = V.tensor_tensor(et(j), expert, top_e[:, j, :].unsqueeze(1).broadcast_to([TP, E0, NT]), ALU.is_equal)
            link(ins)
            V.memset(cs[3], 1.0)
            link(V.tensor_tensor(cs[2], cs[0], cs[1], ALU.add))
            dve.sem_inc(S("choices"), 1)
            link(V.memset(et(3)[:, :, 0:1], 0.0))
            dve.wait_ge(S("gate_exp"), 1)
            link(V.tensor_scalar(rdeg[:, :], gate[:, 1, :], 1.0, None, ALU.add))
            link(V.reciprocal(gate[:, 0, :], rdeg[:, :]))
            link(V.tensor_tensor(gate[:, 1, :], gate[:, 1, :], gate[:, 0, :], ALU.mult))
            dve.wait_ge(S("ranks"), 1)
            link(V.tensor_copy(cs[4], bank(1)[0:TP, 0:400]))
            link(V.tensor_tensor_scan(cs[5], cs[3], cs[4], 0.0, ALU.mult, ALU.add))
            link(V.tensor_tensor(cs[6], cs[5], cs[4], ALU.subtract))
            sm = lambda k: small[0:TP, k, :]
            smi = small.bitcast(I32)
            link(V.tensor_scalar(sm(0), et(5)[:, :, NT - 1], 127.0, None, ALU.add))
            link(V.tensor_copy(smi[0:TP, 1, :], sm(0)))
            link(V.tensor_scalar(smi[0:TP, 2, :], smi[0:TP, 1, :], 7, None, ALU.arith_shift_right))
            link(V.tensor_copy(sm(3), smi[0:TP, 2, :]))
            link(V.tensor_tensor_scan(sm(4), ones[0:TP, 0:E0], sm(3), 0.0, ALU.mult, ALU.add))
            link(V.tensor_tensor(sm(5), sm(4), sm(3), ALU.subtract))
            link(V.tensor_scalar(sm(6), sm(5), float(P), None, ALU.mult))
            link(V.tensor_tensor(cs[7], cs[6], bank(0)[0:TP, 0:400], ALU.add))
            link(V.tensor_tensor(et(7), et(7), sm(6).unsqueeze(2).broadcast_to([TP, E0, NT]), ALU.add))
            for j in range(2):
                link(V.tensor_tensor(cs[8], cs[j], cs[7], ALU.mult))
                link(V.tensor_reduce(rdeg[:, :], et(8).rearrange("p e t -> p t e"), AX.X, ALU.add))
                link(V.tensor_copy(pos[:, j, :], rdeg[:, :]))
            blk = cs[8][:, 0:MB]
            link(V.memset(blk, 0.0))
            for e in range(E0 - 1):
                link(V.scalar_tensor_tensor(out=blk, in0=iota_j[0:TP, 0:MB], scalar=sm(4)[:, e:e + 1], in1=blk, op0=ALU.is_ge, op1=ALU.add))
            link(V.tensor_copy(block_e[0:TP, :], blk))
            dve.sem_inc(S("slot_tables"), 1)
            for s in range(BS):
                dve.sem_inc(S(f"block_y{s}"), 1)
            with dve.Fori(0, MB // BS) as i:
                for s in range(BS):
                    after(dve, "slots_yp", i * BS + (s + 1))
                    after(dve, f"block_stored{s}", i * 16 + 16)
                    V.tensor_tensor(yblk(s), bank(2 * s)[:, 2 * P:4 * P], b2b[:, s, :], ALU.add).then_inc(S(f"block_y{s}"), 1)
            for i in range(NB):
                dve.wait_ge(S(f"expert_rows{i}"), 16 * 2 * BT)
                for j, (res, rest) in enumerate(((H, XN), (ACC, None))):
                    for s in range(BT):
                        t = i * BT + s
                        ins = V.scalar_tensor_tensor(out=r5[:, s, :], in0=res[:, t, 0:D], scalar=gate[:, j, t:t + 1],
                                                     in1=r5[:, s, :] if rest is None else rest[:, t, :], op0=ALU.mult, op1=ALU.add)
                    link(ins)
                ln("norm", 2 * NB + 2 * i, lambda s: r5[:, s, :], lambda s: a5[:, s, :], affine=("L0_ffn_gamma", "L0_ffn_beta"))
                add_out(i, a5, "L0_ffn_out")
                dve.wait_ge(S("L0_ffn_out"), i + 1)
                ln("norm", 2 * NB + 2 * i + 1, lambda s: X[:, i * BT + s, :], lambda s: XN[:, i * BT + s, :], done="normed")

            dve.wait_ge(S("L1_weights"), 16 * 10)
            before_keys("L1")
            for h in range(3, 5):
                p, o = "gnn", (h - 3) * NB
                link(V.memset(g8[:, :, D:D + 1], 1.0))
                link(V.memset(ACC, 0.0))
                if h == 3:
                    hop(h, mix1, 1, "L1", 0, SUB1, AT["keys"][2])
                    after_keys("L1")
                else:
                    hop(h, mix2, 13, "L1", 0, SUB1, AT["L1"][2])
                dve.wait_ge(S("added"), (h + 1) * ITEMS + 2 * HB)
                if h == 3:
                    link(V.tensor_scalar(rdeg[:, :], ACC[:, :, D], 1.0, None, ALU.max))
                    link(V.reciprocal(rdeg[:, :], rdeg[:, :]))
                x_h = XN if h == 3 else H

                def gnn_in(i):
                    link(V.tensor_tensor(a5, tiles(ACC[:, :, 0:D], i), rdeg[:, bass.ds(i * BT, BT)].unsqueeze(2).broadcast_to([TP, BT, D]), ALU.mult))
                    V.tensor_tensor(a5, a5, tiles(x_h, i), ALU.add).then_inc(S(p + "_in"), 1)

                def gnn_norm(i, more):
                    if more:
                        after(dve, p + "_tr", i + (o + 1))
                        gnn_in(i + 1)
                    after(dve, p + "_lin", i + (o + 1))
                    V.tensor_tensor(r5, halves(3), rowbc(f"L1_gnn_b{h - 3}"), ALU.add).then_inc(S("gnn_read"), 1)
                    after(dve, "gnn_read", i + (o + 2))
                    if h == 3:
                        after(dve, "L1_g0_out", i + 1)
                    ln(p, i + o, lambda s: r5[:, s, :], lambda s: b5[:, s, :], done=p + "_pre",
                       affine=(f"L1_gnn_g{h - 3}", f"L1_gnn_beta{h - 3}"))
                    if h == 4:
                        after(dve, p + "_silu", i + 1)
                        add_out(i, r5, "L1_g1_out")
                        after(dve, "L1_g1_out", i + 1)
                        ln("norm", i + 4 * NB, lambda s: one(X, i, s), lambda s: one(XN, i, s), done="normed")

                if h == 3:
                    dve.sem_inc(S("L1_g0_out"), 1)
                    dve.sem_inc(S("gnn_read"), 1)
                gnn_in(0)
                with dve.Fori(0, NB - 1) as i:
                    ch.enter(i, 4 if h == 3 else 6)
                    gnn_norm(i, True)
                ch.leave(NB - 1)
                gnn_norm(NB - 1, False)

            dve.wait_ge(S("mean_sum"), 1)
            V.tensor_scalar(batch["b"][:, 0:D], bank(0)[:, 0:D], 1.0 / N, None, ALU.mult).then_inc(S("mean"), 1)
            R = lambda k: route[:, k, :]

            def softmax():
                link(V.max(mx5[:, 0, :], R(0)))
                V.tensor_scalar(route[:, 1, 0:1], mx5[:, 0, 0:1], -1.0, None, ALU.mult).then_inc(S("route_shift"), 1)

            dve.wait_ge(S("route_logits"), 1)
            link(V.tensor_tensor(R(0), bank(2)[:, 0:E1], rows["L1_ffn_br"], ALU.add))
            softmax()
            dve.wait_ge(S("route_exp"), 1)
            link(V.reciprocal(route[:, 5, 0:1], route[:, 3, 0:1]))
            link(V.tensor_scalar(R(4), R(2), route[:, 5, 0:1], None, ALU.mult))
            capacity = float(-(-N * 5 // (4 * E1)))
            link(V.tensor_scalar(R(6), R(4), float(N), None, ALU.mult))
            link(V.reciprocal(R(7), R(6)))
            link(V.tensor_scalar(R(8), R(7), capacity, 1.0, ALU.mult, ALU.min))
            link(V.tensor_tensor(R(0), R(4), R(8), ALU.mult))
            softmax()
            dve.wait_ge(S("route_exp"), 2)
            link(V.reciprocal(route[:, 5, 0:1], route[:, 3, 0:1]))
            link(V.tensor_scalar(R(4), R(2), route[:, 5, 0:1], None, ALU.mult))
            link(V.max(mx5[:, 0, :], R(4)))
            link(V.max_index(mi5[:, 0, :], mx5[:, 0, :], R(4)))
            dve.sem_inc(S("routed"), 1)
            V.tensor_tensor(route[:, 1, 0:1], mx5[:, 0, 1:2], mx5[:, 0, 0:1], ALU.subtract).then_inc(S("route_shift"), 1)
            dve.wait_ge(S("route_exp"), 3)
            link(V.tensor_scalar(route[:, 5, 0:1], route[:, 2, 0:1], 1.0, None, ALU.add))
            link(V.reciprocal(route[:, 9, 0:1], route[:, 5, 0:1]))
            link(V.tensor_tensor(route[:, 9, 1:2], route[:, 2, 0:1], route[:, 9, 0:1], ALU.mult))
            dve.wait_ge(S("L1_experts_in"), 64)
            link(V.tensor_scalar(b2x[:, 0, :], b2x[:, 0, :], route[:, 9, 0:1], None, ALU.mult))
            link(V.scalar_tensor_tensor(out=b2x[:, 0, :], in0=b2x[:, 1, :], scalar=route[:, 9, 1:2], in1=b2x[:, 0, :], op0=ALU.mult, op1=ALU.add))
            dve.sem_inc(S("ff_used"), 1)
            with dve.Fori(0, NB) as i:
                ch.enter(i, 5)
                after(dve, "ff_y", i * 2 + 1)
                V.scalar_tensor_tensor(out=r5, in0=halves(0), scalar=route[0:TP, 9, 0:1], in1=tiles(XN, i), op0=ALU.mult, op1=ALU.add).then_inc(S("ff_used"), 1)
                after(dve, "ff_y", i * 2 + 2)
                V.scalar_tensor_tensor(out=r5, in0=halves(0), scalar=route[0:TP, 9, 1:2], in1=r5, op0=ALU.mult, op1=ALU.add).then_inc(S("ff_used"), 1)
                after(dve, "ff_used", i * 2 + 3)
                link(V.tensor_tensor(r5, r5, over(b2x[0:TP, 0, :], BT), ALU.add))
                ln("ff", i, lambda s: r5[:, s, :], lambda s: b5[:, s, :], affine=("L1_ffn_gamma", "L1_ffn_beta"))
                add_out(i, b5, "L1_ffn_out")
            ch.leave(NB)


def kernel(**inputs):
    import numpy as np
    import concourse.bacc as bacc
    from concourse.bass_utils import run_bass_kernel_spmd as run

    v = {k: np.asarray(x) for k, x in inputs.items()}
    a = {"x": v["x"]}
    for name, fill in (("src", NOWHERE), ("dst", 0), ("edge_weight", 0)):
        pad = np.full(CH * P - EDGES, fill, v[name].dtype)
        a[name] = np.concatenate([v[name], pad]).reshape(P, CH)
    cat = np.concatenate
    a["L0_gnn_w"] = v["L0_gnn_weight"]
    a["L0_wq"], a["L0_wo"], a["L0_w1"], a["L0_w2"] = (v["L0_mix_" + n] for n in ("Wq", "Wo", "W1", "W2"))
    a["L0_wkv"] = cat([v["L0_mix_Wk"], v["L0_mix_Wv"]], axis=1)
    a["L0_gate"] = v["L0_ffn_gate_w"]
    a["L1_gnn_w0"], a["L1_gnn_w1"] = v["L1_gnn_W0"].T, v["L1_gnn_W1"].T
    qkv = v["L1_mix_Wqkv"].T
    a["L1_wq"], a["L1_wkv"] = qkv[:, 0:D], qkv[:, D:3 * D]
    a["L1_w1"], a["L1_w2"] = v["L1_mix_W1"].T, v["L1_mix_W2"].T
    a["L1_wr"] = v["L1_ffn_Wr"]
    v["L0_mix_bkv"] = cat([v["L0_mix_bk"], v["L0_mix_bv"]])
    for g, names in (("L0", ("L0_mix_bq", "L0_mix_b1")), ("L1", ("L1_mix_b1",))):
        c = [np.zeros((P, 2), np.float32)] * (g == "L1") + [v[n].reshape(-1, P).T for n in names]
        c = cat(c, axis=1)
        a[g + "_cols"] = cat([c, np.zeros((P, 16 - c.shape[1]), np.float32)], axis=1)
        a[g + "_rows"] = cat([v[r] for r in ROWS if r.startswith(g)])
    for g, w1, b1, w2, b2 in (("L0", "w1", "b1", "w2", "b2"), ("L1", "W1", "b1", "W2", "b2")):
        w1, b1, w2, b2 = (v[f"{g}_ffn_{n}"] for n in (w1, b1, w2, b2))
        e = w1.shape[0]
        a[g + "_experts"] = cat([w1.reshape(e, 2, P, F).transpose(0, 2, 1, 3).reshape(e, P, 2 * F),
                                 w2.reshape(e, 4, P, D).transpose(0, 2, 1, 3).reshape(e, P, 4 * D),
                                 b1.reshape(e, 4, P).transpose(0, 2, 1)], axis=2)
        a[g + "_b2"] = b2
    nc = bacc.Bacc("TRN2", target_bir_lowering=False, num_devices=1)
    arrays, aps = {}, {}
    for name, x in a.items():
        x = np.ascontiguousarray(x)
        arrays["in_" + name] = x
        aps[name] = nc.dram_tensor("in_" + name, x.shape, mybir.dt.from_np(x.dtype), kind="ExternalInput").ap()
    out = nc.dram_tensor("out_0", (N, D), F32, kind="ExternalOutput").ap()
    program(nc, aps, out)
    return run(nc, [arrays], core_ids=[0]).results[0]["out_0"]
```
